# Optimizing a Trainium2 kernel written in Bass

```python
import numpy as np
import jax
import jax.numpy as jnp

def _softmax(x, axis=-1):
    return jax.nn.softmax(x, axis=axis)

def _gelu(x):
    return jax.nn.gelu(x, approximate=True)

def _silu(x):
    return jax.nn.silu(x)

def _sigmoid(x):
    return jax.nn.sigmoid(x)

def _layernorm(x, axis=-1, eps=1e-05):
    m = jnp.mean(x, axis=axis, keepdims=True)
    v = jnp.var(x, axis=axis, keepdims=True)
    return (x - m) / jnp.sqrt(v + eps)

def _scatter_add(tgt, idx, src, axis=0):
    return tgt.at[idx].add(src)

def _segment_sum(src, seg, n):
    return jax.ops.segment_sum(src, seg, n)
kernel_name = 'mk_hybrid_d1_jaxref_r4_3046f2'

def setup_inputs(seed: int=0):
    np.random.seed(seed)
    _w = jnp.asarray

    def _L0_attn_a_setup():
        import jax, jax.numpy as jnp
        import numpy as np
        from jax import lax
        CHUNK = 64
        ROPE_BASE = 10000.0

        def _forward(x, norm_scale, conv_w, conv_b, in_proj_w, dt_bias, head_mix, out_proj_w):
            B, N, D = x.shape
            H = head_mix.shape[0]
            Dh = D // H
            K = conv_w.shape[-1]
            residual = x
            xf = x.astype(jnp.float32)
            rms = lax.rsqrt(jnp.mean(xf * xf, -1, keepdims=True) + 1e-06)
            xn = jnp.clip(norm_scale * xf * rms, -60000.0, 60000.0).astype(x.dtype)
            xc = lax.conv_general_dilated(xn.transpose(0, 2, 1), conv_w, (1,), [(K - 1, 0)], dimension_numbers=('NCH', 'OIH', 'NCH'), feature_group_count=D)
            xc = xc + conv_b[None, :, None]
            xc = jax.nn.silu(xc.transpose(0, 2, 1))
            fused = xc @ in_proj_w.T
            dt_raw, v, gate = jnp.split(fused, 3, axis=-1)
            dt = jnp.clip(jax.nn.softplus(dt_raw.astype(jnp.float32) + dt_bias), 0.001, 2.0)
            gate = jax.nn.sigmoid(gate)
            log_alpha = -dt
            inv_freq = 1.0 / ROPE_BASE ** (jnp.arange(0, Dh, 2, dtype=jnp.float32) / Dh)
            t = jnp.arange(N, dtype=jnp.float32)
            freqs = t[:, None] * inv_freq[None, :]
            cos = jnp.cos(freqs)[None, :, None, :]
            sin = jnp.sin(freqs)[None, :, None, :]
            v4 = v.reshape(B, N, H, Dh)
            v1, v2 = (v4[..., :Dh // 2], v4[..., Dh // 2:])
            v_rot = jnp.concatenate([v1 * cos - v2 * sin, v1 * sin + v2 * cos], -1).reshape(B, N, D)
            v_in = v_rot * dt
            pad = -N % CHUNK
            if pad:
                v_in = jnp.pad(v_in, ((0, 0), (0, pad), (0, 0)))
                log_alpha = jnp.pad(log_alpha, ((0, 0), (0, pad), (0, 0)))
            NC = v_in.shape[1] // CHUNK
            vc = v_in.reshape(B, NC, CHUNK, D)
            la = log_alpha.reshape(B, NC, CHUNK, D)
            L = jnp.clip(jnp.cumsum(la, axis=2), -20.0, 0.0)
            Lmax = jnp.max(L, axis=2, keepdims=True)
            Ls = L - Lmax
            cum = jnp.cumsum(jnp.exp(-Ls) * vc, axis=2)
            chunk_out = jnp.exp(Ls) * cum
            if NC > 1:
                bd = L[:, :, -1, :]
                bo = chunk_out[:, :, -1, :]
                cd = jnp.clip(jnp.cumsum(bd, axis=1), -80.0, 0.0)
                stab = jnp.max(cd, axis=1, keepdims=True)
                ncd = jnp.clip(cd - stab, -20.0, 0.0)
                seeds = bo * jnp.exp(-ncd)
                shifted = jnp.pad(seeds[:, :-1], ((0, 0), (1, 0), (0, 0)))
                carries = jnp.cumsum(shifted, axis=1) * jnp.exp(ncd)
                final = chunk_out + carries[:, :, None, :] * jnp.exp(L)
            else:
                final = chunk_out
            final = final.astype(x.dtype).reshape(B, -1, D)[:, :N, :]
            vm = jnp.einsum('bnhd,hm->bnmd', final.reshape(B, N, H, Dh), head_mix).reshape(B, N, D)
            out = vm * gate @ out_proj_w.T
            return residual + out
        D, H, K = (512, 16, 4)
        Dh = D // H
        key = jax.random.key(seed)
        ks = jax.random.split(key, 8)
        x = jax.random.normal(ks[0], (2, 1024, D), dtype=jnp.float32)
        norm_scale = jnp.ones((D,), jnp.float32)
        conv_w = jax.random.normal(ks[1], (D, 1, K), jnp.float32) * 0.1
        conv_b = jnp.zeros((D,), jnp.float32)
        in_proj_w = jax.random.normal(ks[2], (3 * D, D), jnp.float32) * 0.02
        out_proj_w = jax.random.normal(ks[3], (D, D), jnp.float32) * 0.02
        u = jax.random.uniform(ks[4], (H, Dh), jnp.float32)
        dt = jnp.clip(jnp.exp(u * (np.log(0.1) - np.log(10.0)) + np.log(10.0)), 0.001, None)
        dt_bias = (dt + jnp.log(-jnp.expm1(-dt))).reshape(-1)
        head_mix = jnp.eye(H, dtype=jnp.float32)
        return {'x': x, 'norm_scale': norm_scale, 'conv_w': conv_w, 'conv_b': conv_b, 'in_proj_w': in_proj_w, 'dt_bias': dt_bias, 'head_mix': head_mix, 'out_proj_w': out_proj_w}
    _L0_attn_a_in = _L0_attn_a_setup()

    def _L0_attn_b_setup():
        import jax, jax.numpy as jnp
        import numpy as np
        HIDDEN = 512
        NUM_V = 16
        NUM_K = 8
        HK = 128
        HV = 128
        KCONV = 4
        KEY_DIM = NUM_K * HK
        VALUE_DIM = NUM_V * HV
        CONV_DIM = 2 * KEY_DIM + VALUE_DIM
        R = NUM_V // NUM_K
        L2_EPS = 1e-06
        NORM_EPS = 1e-06
        key = jax.random.key(seed)
        ks = jax.random.split(key, 8)
        s = 0.02
        return {'hidden_states': jax.random.normal(ks[0], (1, 256, HIDDEN), jnp.float32), 'w_qkvz': jax.random.normal(ks[1], (2 * KEY_DIM + 2 * VALUE_DIM, HIDDEN), jnp.float32) * s, 'w_ba': jax.random.normal(ks[2], (2 * NUM_V, HIDDEN), jnp.float32) * s, 'conv_w': jax.random.normal(ks[3], (CONV_DIM, KCONV), jnp.float32) * s, 'dt_bias': jnp.ones((NUM_V,), jnp.float32), 'A_log': jnp.log(jax.random.uniform(ks[4], (NUM_V,), jnp.float32, 0.001, 16.0)), 'norm_weight': jnp.ones((HV,), jnp.float32), 'w_out': jax.random.normal(ks[5], (HIDDEN, VALUE_DIM), jnp.float32) * s}
    _L0_attn_b_in = _L0_attn_b_setup()

    def _L0_ffn_setup():
        import jax, jax.numpy as jnp
        import numpy as np

        def _sparsify_2to4(h):
            B, S, I = h.shape
            g = h.reshape(B, S, I // 4, 4)
            a = jnp.abs(g)
            _, idx = jax.lax.top_k(a, 2)
            pos = jnp.arange(4)
            mask = (pos == idx[..., 0:1]) | (pos == idx[..., 1:2])
            return (g * mask.astype(g.dtype)).reshape(B, S, I)
        key = jax.random.key(seed)
        k1, k2, k3, k4 = jax.random.split(key, 4)
        B, S, H, I = (4, 512, 512, 2048)
        x = jax.random.normal(k1, (B, S, H), dtype=jnp.float32)
        w_gate = jax.random.normal(k2, (H, I), dtype=jnp.float32) / np.sqrt(H)
        w_up = jax.random.normal(k3, (H, I), dtype=jnp.float32) / np.sqrt(H)
        w_down = jax.random.normal(k4, (I, H), dtype=jnp.float32) / np.sqrt(I)
        return {'x': x, 'w_gate': w_gate, 'w_up': w_up, 'w_down': w_down}
    _L0_ffn_in = _L0_ffn_setup()
    _d = {'L0_attn_a_x': _L0_attn_a_in['x'], 'L0_attn_a_norm_scale': _L0_attn_a_in['norm_scale'], 'L0_attn_a_conv_w': _L0_attn_a_in['conv_w'], 'L0_attn_a_conv_b': _L0_attn_a_in['conv_b'], 'L0_attn_a_in_proj_w': _L0_attn_a_in['in_proj_w'], 'L0_attn_a_dt_bias': _L0_attn_a_in['dt_bias'], 'L0_attn_a_head_mix': _L0_attn_a_in['head_mix'], 'L0_attn_a_out_proj_w': _L0_attn_a_in['out_proj_w'], 'L0_attn_b_w_qkvz': _L0_attn_b_in['w_qkvz'], 'L0_attn_b_w_ba': _L0_attn_b_in['w_ba'], 'L0_attn_b_conv_w': _L0_attn_b_in['conv_w'], 'L0_attn_b_dt_bias': _L0_attn_b_in['dt_bias'], 'L0_attn_b_A_log': _L0_attn_b_in['A_log'], 'L0_attn_b_norm_weight': _L0_attn_b_in['norm_weight'], 'L0_attn_b_w_out': _L0_attn_b_in['w_out'], 'L0_ffn_w_gate': _L0_ffn_in['w_gate'], 'L0_ffn_w_up': _L0_ffn_in['w_up'], 'L0_ffn_w_down': _L0_ffn_in['w_down']}
    _x0 = _d['L0_attn_a_x']
    _d['L0_attn_a_x'] = jax.random.normal(jax.random.fold_in(jax.random.key(seed), 1), (2, 1024, 512), dtype=_x0.dtype)
    del _x0
    return _d

def reference(L0_attn_a_x, L0_attn_a_norm_scale, L0_attn_a_conv_w, L0_attn_a_conv_b, L0_attn_a_in_proj_w, L0_attn_a_dt_bias, L0_attn_a_head_mix, L0_attn_a_out_proj_w, L0_attn_b_w_qkvz, L0_attn_b_w_ba, L0_attn_b_conv_w, L0_attn_b_dt_bias, L0_attn_b_A_log, L0_attn_b_norm_weight, L0_attn_b_w_out, L0_ffn_w_gate, L0_ffn_w_up, L0_ffn_w_down):

    def _L0_attn_a_ref(x, norm_scale, conv_w, conv_b, in_proj_w, dt_bias, head_mix, out_proj_w):
        import jax, jax.numpy as jnp
        import numpy as np
        from jax import lax
        CHUNK = 64
        ROPE_BASE = 10000.0

        def _forward(x, norm_scale, conv_w, conv_b, in_proj_w, dt_bias, head_mix, out_proj_w):
            B, N, D = x.shape
            H = head_mix.shape[0]
            Dh = D // H
            K = conv_w.shape[-1]
            residual = x
            xf = x.astype(jnp.float32)
            rms = lax.rsqrt(jnp.mean(xf * xf, -1, keepdims=True) + 1e-06)
            xn = jnp.clip(norm_scale * xf * rms, -60000.0, 60000.0).astype(x.dtype)
            xc = lax.conv_general_dilated(xn.transpose(0, 2, 1), conv_w, (1,), [(K - 1, 0)], dimension_numbers=('NCH', 'OIH', 'NCH'), feature_group_count=D)
            xc = xc + conv_b[None, :, None]
            xc = jax.nn.silu(xc.transpose(0, 2, 1))
            fused = xc @ in_proj_w.T
            dt_raw, v, gate = jnp.split(fused, 3, axis=-1)
            dt = jnp.clip(jax.nn.softplus(dt_raw.astype(jnp.float32) + dt_bias), 0.001, 2.0)
            gate = jax.nn.sigmoid(gate)
            log_alpha = -dt
            inv_freq = 1.0 / ROPE_BASE ** (jnp.arange(0, Dh, 2, dtype=jnp.float32) / Dh)
            t = jnp.arange(N, dtype=jnp.float32)
            freqs = t[:, None] * inv_freq[None, :]
            cos = jnp.cos(freqs)[None, :, None, :]
            sin = jnp.sin(freqs)[None, :, None, :]
            v4 = v.reshape(B, N, H, Dh)
            v1, v2 = (v4[..., :Dh // 2], v4[..., Dh // 2:])
            v_rot = jnp.concatenate([v1 * cos - v2 * sin, v1 * sin + v2 * cos], -1).reshape(B, N, D)
            v_in = v_rot * dt
            pad = -N % CHUNK
            if pad:
                v_in = jnp.pad(v_in, ((0, 0), (0, pad), (0, 0)))
                log_alpha = jnp.pad(log_alpha, ((0, 0), (0, pad), (0, 0)))
            NC = v_in.shape[1] // CHUNK
            vc = v_in.reshape(B, NC, CHUNK, D)
            la = log_alpha.reshape(B, NC, CHUNK, D)
            L = jnp.clip(jnp.cumsum(la, axis=2), -20.0, 0.0)
            Lmax = jnp.max(L, axis=2, keepdims=True)
            Ls = L - Lmax
            cum = jnp.cumsum(jnp.exp(-Ls) * vc, axis=2)
            chunk_out = jnp.exp(Ls) * cum
            if NC > 1:
                bd = L[:, :, -1, :]
                bo = chunk_out[:, :, -1, :]
                cd = jnp.clip(jnp.cumsum(bd, axis=1), -80.0, 0.0)
                stab = jnp.max(cd, axis=1, keepdims=True)
                ncd = jnp.clip(cd - stab, -20.0, 0.0)
                seeds = bo * jnp.exp(-ncd)
                shifted = jnp.pad(seeds[:, :-1], ((0, 0), (1, 0), (0, 0)))
                carries = jnp.cumsum(shifted, axis=1) * jnp.exp(ncd)
                final = chunk_out + carries[:, :, None, :] * jnp.exp(L)
            else:
                final = chunk_out
            final = final.astype(x.dtype).reshape(B, -1, D)[:, :N, :]
            vm = jnp.einsum('bnhd,hm->bnmd', final.reshape(B, N, H, Dh), head_mix).reshape(B, N, D)
            out = vm * gate @ out_proj_w.T
            return residual + out
        return _forward(x, norm_scale, conv_w, conv_b, in_proj_w, dt_bias, head_mix, out_proj_w)

    def _L0_attn_b_ref(hidden_states, w_qkvz, w_ba, conv_w, dt_bias, A_log, norm_weight, w_out):
        import jax, jax.numpy as jnp
        import numpy as np
        HIDDEN = 512
        NUM_V = 16
        NUM_K = 8
        HK = 128
        HV = 128
        KCONV = 4
        KEY_DIM = NUM_K * HK
        VALUE_DIM = NUM_V * HV
        CONV_DIM = 2 * KEY_DIM + VALUE_DIM
        R = NUM_V // NUM_K
        L2_EPS = 1e-06
        NORM_EPS = 1e-06
        B, T, _ = hidden_states.shape
        qkvz = hidden_states @ w_qkvz.T
        ba = hidden_states @ w_ba.T
        qkvz = qkvz.reshape(B, T, NUM_K, 2 * HK + 2 * R * HV)
        q, k, v, z = jnp.split(qkvz, [HK, 2 * HK, 2 * HK + R * HV], axis=3)
        v = v.reshape(B, T, NUM_V, HV)
        z = z.reshape(B, T, NUM_V, HV)
        ba = ba.reshape(B, T, NUM_K, 2 * R)
        b = ba[..., :R].reshape(B, T, NUM_V)
        a = ba[..., R:].reshape(B, T, NUM_V)
        mixed = jnp.concatenate([q.reshape(B, T, KEY_DIM), k.reshape(B, T, KEY_DIM), v.reshape(B, T, VALUE_DIM)], axis=-1)
        xc = mixed.transpose(0, 2, 1)
        yc = jax.lax.conv_general_dilated(xc, conv_w[:, None, :], (1,), [(KCONV - 1, 0)], feature_group_count=CONV_DIM, dimension_numbers=('NCH', 'OIH', 'NCH'))
        yc = jax.nn.silu(yc).transpose(0, 2, 1)
        q, k, v = jnp.split(yc, [KEY_DIM, 2 * KEY_DIM], axis=-1)
        q = q.reshape(B, T, NUM_K, HK)
        k = k.reshape(B, T, NUM_K, HK)
        v = v.reshape(B, T, NUM_V, HV)
        beta = jax.nn.sigmoid(b)
        g = -jnp.exp(A_log) * jax.nn.softplus(a + dt_bias)
        q = jnp.repeat(q, R, axis=2)
        k = jnp.repeat(k, R, axis=2)
        q = q * jax.lax.rsqrt(jnp.sum(q * q, -1, keepdims=True) + L2_EPS)
        k = k * jax.lax.rsqrt(jnp.sum(k * k, -1, keepdims=True) + L2_EPS)
        scale = HK ** (-0.5)

        def step(S, xs):
            qt, kt, vt, gt, bt = xs
            S = S * jnp.exp(gt)[..., None, None]
            kv = jnp.einsum('bhk,bhkv->bhv', kt, S)
            delta = (vt - kv) * bt[..., None]
            S = S + jnp.einsum('bhk,bhv->bhkv', kt, delta)
            o = jnp.einsum('bhk,bhkv->bhv', qt * scale, S)
            return (S, o)
        S0 = jnp.zeros((B, NUM_V, HK, HV), hidden_states.dtype)
        xs = (q.transpose(1, 0, 2, 3), k.transpose(1, 0, 2, 3), v.transpose(1, 0, 2, 3), g.transpose(1, 0, 2), beta.transpose(1, 0, 2))
        _, o = jax.lax.scan(step, S0, xs)
        o = o.transpose(1, 0, 2, 3)
        xf = o.astype(jnp.float32) * jax.nn.silu(z.astype(jnp.float32))
        var = jnp.mean(xf * xf, -1, keepdims=True)
        xn = xf * jax.lax.rsqrt(var + NORM_EPS) * norm_weight
        return xn.reshape(B, T, VALUE_DIM) @ w_out.T

    def _L0_ffn_ref(x, w_gate, w_up, w_down):
        import jax, jax.numpy as jnp
        import numpy as np

        def _sparsify_2to4(h):
            B, S, I = h.shape
            g = h.reshape(B, S, I // 4, 4)
            a = jnp.abs(g)
            _, idx = jax.lax.top_k(a, 2)
            pos = jnp.arange(4)
            mask = (pos == idx[..., 0:1]) | (pos == idx[..., 1:2])
            return (g * mask.astype(g.dtype)).reshape(B, S, I)
        h = jax.nn.silu(jnp.einsum('bsh,hi->bsi', x, w_gate)) * jnp.einsum('bsh,hi->bsi', x, w_up)
        h_sparse = _sparsify_2to4(h)
        return jnp.einsum('bsi,ih->bsh', h_sparse, w_down)
    x = L0_attn_a_x
    x = x + _L0_attn_a_ref(_layernorm(x, axis=-1), L0_attn_a_norm_scale, L0_attn_a_conv_w, L0_attn_a_conv_b, L0_attn_a_in_proj_w, L0_attn_a_dt_bias, L0_attn_a_head_mix, L0_attn_a_out_proj_w)
    x = x + _L0_ffn_ref(_layernorm(x, axis=-1), L0_ffn_w_gate, L0_ffn_w_up, L0_ffn_w_down)
    x = x + _L0_attn_b_ref(_layernorm(x, axis=-1), L0_attn_b_w_qkvz, L0_attn_b_w_ba, L0_attn_b_conv_w, L0_attn_b_dt_bias, L0_attn_b_A_log, L0_attn_b_norm_weight, L0_attn_b_w_out)
    x = x + _L0_ffn_ref(_layernorm(x, axis=-1), L0_ffn_w_gate, L0_ffn_w_up, L0_ffn_w_down)
    return x

_drawn_inputs = setup_inputs


def setup_inputs(seed=0):
    import zlib

    import numpy as np

    out = dict(_drawn_inputs(seed))
    spreads = {'L0_attn_a_norm_scale': (1.0, 0.6),
     'L0_attn_a_conv_b': (0.0, 0.1),
     'L0_attn_b_dt_bias': (1.0, 0.6),
     'L0_attn_b_norm_weight': (1.0, 0.6)}
    factors = {'L0_attn_b_w_qkvz': 8.0,
     'L0_attn_b_w_ba': 8.0,
     'L0_attn_b_conv_w': 8.0,
     'L0_attn_b_A_log': 8.0,
     'L0_attn_b_w_out': 8.0}
    for name, (base, spread) in spreads.items():
        noise = np.random.default_rng([zlib.crc32(name.encode()), seed]).standard_normal(out[name].shape)
        drawn = base * np.exp(spread * noise) if base else spread * noise
        out[name] = jnp.asarray(drawn.astype(out[name].dtype))
    for name, factor in factors.items():
        out[name] = (out[name] * factor).astype(out[name].dtype)
    return out
```

```python
from contextlib import ExitStack, contextmanager

import concourse.bass as bass
from concourse import mybir

P = 128
LN_EPS = 1e-5
F32 = mybir.dt.float32
F32R = mybir.dt.float32r
BF16 = mybir.dt.bfloat16
ALU = mybir.AluOpType
ACT = mybir.ActivationFunctionType
AX = mybir.AxisListType


@contextmanager
def cleared_semaphores(nc, prefix):
    taken = []

    def sem(name):
        taken.append(nc.alloc_semaphore(f"{prefix}_{name}"))
        return taken[-1]

    yield sem
    nc.clear_and_free_semaphores(taken)
    nc.all_engine_barrier()


def layer_a_tables():
    import numpy as np
    tokens, head = 1024, 32
    inv = (1.0 / 10000.0 ** (np.arange(0, head, 2, dtype=np.float32) / np.float32(head))).astype(np.float32)
    angle = np.arange(tokens, dtype=np.float32)[None, :] * inv[:, None]
    row = np.arange(P) % (head // 2)
    rot = np.zeros((P, P), np.float32)
    for m in range(P):
        h, e = divmod(m, head)
        if e < head // 2:
            rot[h * head + e + head // 2, m] = -1.0
        else:
            rot[h * head + e - head // 2, m] = 1.0
    within = np.ones((P, tokens), np.float32)
    within[:, ::64] = 0.0
    eye = (np.arange(P)[:, None] % head == np.arange(head)[None, :]).astype(np.float32)
    return {"ident": np.eye(P, dtype=np.float32), "rot": rot, "cos": np.cos(angle)[row], "sin": np.sin(angle)[row],
            "within": within, "eye_head": eye}


def layer_b_tables():
    import numpy as np
    r, c = np.arange(P)[:, None], np.arange(P)[None, :]
    joins = [-((r // (2 * n) == c // (2 * n)) & ((c // n) % 2 == 1) & ((r // n) % 2 == 0)).astype(np.float32)
             for n in (1, 2, 4, 8, 16, 32, 64)]
    return {"ident": np.eye(P, dtype=np.float32), "upto": (r <= c).astype(np.float32),
            "after": (r > c).astype(np.float32), "below": (r < c).astype(np.float32),
            "joins": np.ascontiguousarray(np.stack(joins, 1))}


def decay_mixer(nc, psum, consts, x_in, x_out, w):
    BATCH, N, D = x_in.shape
    KD = D // P
    SUB = N // P
    HALF = N // 2
    TAPS = 4
    CH = 64
    NCH = N // CH
    with ExitStack() as ctx:
        def sb(n, shape, dt=F32):
            return ctx.enter_context(nc.sbuf_tensor(f"a_{n}", shape, dt))

        sem = ctx.enter_context(cleared_semaphores(nc, "a"))

        ident = sb("ident", [P, P])
        rot = sb("rot", [P, P])
        cos, sin = sb("cos", [P, N]), sb("sin", [P, N])
        within = sb("within", [P, N])
        ones = sb("ones", [P, NCH])
        mhalf = sb("mhalf", [P, SUB])
        w_in = sb("w_in", [P, KD, 3 * D])
        w_out = sb("w_out", [P, KD, D])
        mix = sb("mix", [P, KD, D])
        mix_rows = sb("mix_rows", [P, KD, D // 32])
        eye_head = sb("eye_head", [P, 32])
        cols = sb("cols", [P, 3 + TAPS, KD])
        x = sb("x", [P, SUB, D])
        y = sb("y", [P, SUB, D])
        stats = sb("stats", [P, SUB, 6])
        mean2, mean, gap, gap2, var, var_eps, rstd, msq, msq_eps, rrms = (
            sb(n, [P, SUB]) for n in ("mean2", "mean", "gap", "gap2", "var", "var_eps", "rstd", "msq", "msq_eps",
                                      "rrms"))
        xnT = sb("xnT", [P, KD, TAPS - 1 + N])
        xc = sb("xc", [P, KD, N])
        gate = sb("gate", [P, KD, N])
        final = sb("final", [P, KD, N])
        arg, ex, dt, dec, decs, grow, fade, fade0, v, va, vb = (
            sb(n, [P, N]) for n in ("arg", "ex", "dt", "dec", "decs", "grow", "fade", "fade0", "v", "va", "vb"))
        cd, cdc, ncd, up, down, seeds, csum, carry = (
            sb(n, [P, NCH]) for n in ("cd", "cdc", "ncd", "up", "down", "seeds", "csum", "carry"))
        ps_dt, ps_v, ps_g, ps_p = banks = psum

        s_tab = sem("s_tab")
        s_w = sem("s_w")
        s_set = sem("s_set")
        s_mix = sem("s_mix")
        s_x = sem("s_x")
        s_ln = sem("s_ln")
        s_var = sem("s_var")
        s_rstd = sem("s_rstd")
        s_y = sem("s_y")
        s_sq = sem("s_sq")
        s_msq = sem("s_msq")
        s_rrms = sem("s_rrms")
        s_xy = sem("s_xy")
        s_yn = sem("s_yn")
        s_tr = sem("s_tr")
        s_sc = sem("s_sc")
        s_conv = sem("s_conv")
        s_tap = sem("s_tap")
        s_xc = sem("s_xc")
        s_pdt, s_pv, s_pg, s_pp = sem("s_pdt"), sem("s_pv"), sem("s_pg"), sem("s_pp")
        s_arg = sem("s_arg")
        s_ex = sem("s_ex")
        s_dt = sem("s_dt")
        s_dec = sem("s_dec")
        s_exps = sem("s_exps")
        s_v = sem("s_v")
        s_gate = sem("s_gate")
        s_va = sem("s_va")
        s_vb = sem("s_vb")
        s_cum = sem("s_cum")
        s_cd = sem("s_cd")
        s_cexp = sem("s_cexp")
        s_car = sem("s_car")
        s_fin = sem("s_fin")
        s_sig = sem("s_sig")
        s_pm = sem("s_pm")
        s_gm = sem("s_gm")
        s_po = sem("s_po")
        s_res = sem("s_res")
        s_store = sem("s_store")
        LN = SUB + 6
        CONV = TAPS

        block = ctx.enter_context(nc.Block())

        @block.sync
        def _(sp):
            xr = x_in.rearrange("b (s p) d -> b p s d", p=P)
            outr = x_out.rearrange("(b s p) d -> b p s d", p=P, b=BATCH)
            for s in range(2):
                part = slice(s * SUB // 2, (s + 1) * SUB // 2)
                sp.dma_start(x[:, part, :], xr[0, :, part, :]).then_inc(s_x, 16)
            for tile, src in ((ident, "ident"), (cols, "cols"), (within, "within"), (rot, "rot"),
                              (cos, "cos"), (sin, "sin"), (mix_rows, "mix_rows"), (eye_head, "eye_head")):
                full = tile[:, :] if len(tile.shape) == 2 else tile[:, :, :]
                sp.dma_start(full, w[src] if src in w else consts[src]).then_inc(s_tab, 16)
            sp.dma_start(w_in[:, :, :], w["a_in"].rearrange("(k p) n -> p k n", p=P)).then_inc(s_w, 16)
            sp.dma_start(w_out[:, :, :], w["a_out"].rearrange("(k p) n -> p k n", p=P)).then_inc(s_w, 16)
            for b in range(BATCH):
                for s in range(2):
                    part = slice(s * SUB // 2, (s + 1) * SUB // 2)
                    sp.wait_ge(s_res, SUB * b + (s + 1) * SUB // 2)
                    sp.dma_start(outr[b][:, part, :], x[:, part, :]).then_inc(s_store, 16)
                if b < BATCH - 1:
                    sp.wait_ge(s_store, 32 * (b + 1))
                    for s in range(2):
                        part = slice(s * SUB // 2, (s + 1) * SUB // 2)
                        sp.dma_start(x[:, part, :], xr[b + 1, :, part, :]).then_inc(s_x, 16)
            sp.wait_ge(s_store, 32 * BATCH)

        @block.gpsimd
        def _(pool):
            pool.memset(mhalf[:, :], -0.5).then_inc(s_set, 1)
            pool.memset(ones[:, :], 1.0).then_inc(s_set, 1)
            pool.memset(carry[:, 0:1], 0.0).then_inc(s_set, 1)
            pool.memset(xnT[:, :, 0:TAPS - 1], 0.0).then_inc(s_set, 1)
            pool.wait_ge(s_set, 4)
            pool.wait_ge(s_tab, 16 * 8)
            with pool.Fori(0, BATCH) as b:
                pool.wait_ge(s_var, b + 1)
                pool.tensor_tensor(rstd[:, :], var[:, :], mhalf[:, :], ALU.pow).then_inc(s_rstd, 1)
                pool.wait_ge(s_msq, b + 1)
                pool.tensor_tensor(rrms[:, :], msq_eps[:, :], mhalf[:, :], ALU.pow).then_inc(s_rrms, 1)
                for j in range(KD):
                    n = b * KD + j
                    pool.wait_ge(s_v, n + 1)
                    pool.wait_ge(s_cum, 3 * n)
                    pool.tensor_tensor(va[:, :], v[:, :], cos[:, :], ALU.mult).then_inc(s_va, 1)
                    pool.wait_ge(s_dt, n + 1)
                    pool.wait_ge(s_vb, 2 * n + 2)
                    pool.tensor_tensor(va[:, :], vb[:, :], dt[:, :], ALU.mult).then_inc(s_va, 1)

        @block.scalar
        def _(act):
            act.wait_ge(s_tab, 16 * 8)
            with act.Fori(0, BATCH) as b:
                for i in range(SUB):
                    act.wait_ge(s_y, SUB * b + i + 1)
                    act.wait_ge(s_sq, SUB * b + i)
                    act.activation(final[:, 0, 0:D], y[:, i, :], ACT.Square,
                                   accum_out=msq[:, i:i + 1]).then_inc(s_sq, 1)
                for k in range(KD):
                    act.wait_ge(s_tr, KD * b + k + 1)
                    act.activation(xnT[:, k, TAPS - 1:], banks[k][:, :], ACT.Copy,
                                   scale=cols[:, 0, k:k + 1]).then_inc(s_sc, 1)
                for k in range(KD):
                    n = b * KD + k
                    act.wait_ge(s_conv, CONV * n + 1)
                    act.activation(xc[:, k, :], xnT[:, k, 0:N], ACT.Copy, scale=cols[:, 3, k:k + 1]).then_inc(s_tap, 1)
                for k in range(KD):
                    n = b * KD + k
                    act.wait_ge(s_conv, CONV * (n + 1))
                    act.activation(xc[:, k, :], xc[:, k, :], ACT.Silu, bias=cols[:, 1, k:k + 1]).then_inc(s_xc, 1)
                for j in range(KD):
                    n = b * KD + j
                    act.wait_ge(s_arg, n + 1)
                    act.activation(ex[:, :], arg[:, :], ACT.Exp).then_inc(s_ex, 1)
                    act.wait_ge(s_ex, 2 * n + 1)
                    act.activation(ex[:, :], ex[:, :], ACT.Ln, bias=1.0).then_inc(s_ex, 1)
                    act.wait_ge(s_pv, n + 1)
                    act.wait_ge(s_va, 2 * n)
                    act.wait_ge(s_pp, n)
                    act.copy(v[:, :], ps_v[:, :]).then_inc(s_v, 1)
                    act.wait_ge(s_dec, 3 * n + 3)
                    act.activation(grow[:, :], decs[:, :], ACT.Exp, scale=-1.0).then_inc(s_exps, 1)
                    act.activation(fade0[:, :], decs[:, :], ACT.Exp).then_inc(s_exps, 1)
                    act.activation(fade[:, :], dec[:, :], ACT.Exp).then_inc(s_exps, 1)
                    act.wait_ge(s_cd, 3 * n + 3)
                    act.activation(up[:, :], ncd[:, :], ACT.Exp, scale=-1.0).then_inc(s_cexp, 1)
                    act.activation(down[:, :], ncd[:, :], ACT.Exp).then_inc(s_cexp, 1)
                    act.wait_ge(s_pg, n + 1)
                    act.wait_ge(s_po, SUB * b)
                    act.copy(gate[:, j, :], ps_g[:, :]).then_inc(s_gate, 1)
                act.wait_ge(s_gate, KD * (b + 1))
                for j in range(KD):
                    act.activation(gate[:, j, :], gate[:, j, :], ACT.Sigmoid).then_inc(s_sig, 1)

        @block.vector
        def _(dve):
            dve.wait_ge(s_tab, 16 * 8)
            dve.wait_ge(s_set, 4)
            for k in range(KD):
                dve.tensor_tensor(mix[:, k, :].rearrange("p (m e) -> p m e", e=32),
                                  mix_rows[:, k, :].rearrange("p (m e) -> p m e", e=1).to_broadcast([P, D // 32, 32]),
                                  eye_head[:, :].rearrange("p (m e) -> p m e", m=1).to_broadcast([P, D // 32, 32]),
                                  ALU.mult).then_inc(s_mix, 1)
            with dve.Fori(0, BATCH) as b:
                dve.wait_ge(s_x, 32 * (b + 1))
                for i in range(SUB):
                    dve.bn_stats(stats[:, i, :], x[:, i, :]).then_inc(s_ln, 1)
                c = LN * b + SUB
                dve.wait_ge(s_ln, c)
                dve.tensor_tensor(mean2[:, :], stats[:, :, 1], stats[:, :, 4], ALU.add).then_inc(s_ln, 1)
                dve.tensor_tensor(gap[:, :], stats[:, :, 1], stats[:, :, 4], ALU.subtract).then_inc(s_ln, 1)
                dve.tensor_tensor(var[:, :], stats[:, :, 2], stats[:, :, 5], ALU.add).then_inc(s_ln, 1)
                dve.wait_ge(s_ln, c + 3)
                dve.tensor_scalar(mean[:, :], mean2[:, :], 0.5, None, ALU.mult).then_inc(s_ln, 1)
                dve.scalar_tensor_tensor(gap2[:, :], gap[:, :], 0.25, gap[:, :], ALU.mult, ALU.mult).then_inc(s_ln, 1)
                dve.tensor_scalar(var_eps[:, :], var[:, :], 1.0 / D, LN_EPS, ALU.mult, ALU.add).then_inc(s_ln, 1)
                dve.wait_ge(s_ln, c + 6)
                dve.tensor_tensor(var[:, :], var_eps[:, :], gap2[:, :], ALU.add).then_inc(s_var, 1)
                dve.wait_ge(s_tr, KD * b)
                dve.wait_ge(s_rstd, b + 1)
                for i in range(SUB):
                    dve.tensor_scalar(y[:, i, :], x[:, i, :], mean[:, i:i + 1], rstd[:, i:i + 1],
                                      ALU.subtract, ALU.mult).then_inc(s_y, 1)
                dve.wait_ge(s_y, SUB * (b + 1))
                for i in range(SUB):
                    dve.tensor_tensor(x[:, i, :], x[:, i, :], y[:, i, :], ALU.add).then_inc(s_xy, 1)
                dve.wait_ge(s_sq, SUB * (b + 1))
                dve.tensor_scalar(msq_eps[:, :], msq[:, :], 1.0 / D, 1e-6, ALU.mult, ALU.add).then_inc(s_msq, 1)
                dve.wait_ge(s_xy, SUB * (b + 1))
                dve.wait_ge(s_rrms, b + 1)
                for i in range(SUB):
                    dve.tensor_scalar(y[:, i, :], y[:, i, :], rrms[:, i:i + 1], None, ALU.mult).then_inc(s_yn, 1)
                for k in range(KD):
                    n = b * KD + k
                    xk = xnT[:, k, TAPS - 1:]
                    dve.wait_ge(s_sc, n + 1)
                    dve.tensor_scalar(xk, xk, -60000.0, 60000.0, ALU.max, ALU.min).then_inc(s_conv, 1)
                    dve.wait_ge(s_tap, n + 1)
                    for tap in range(1, TAPS):
                        dve.wait_ge(s_conv, CONV * n + tap)
                        dve.scalar_tensor_tensor(xc[:, k, :], xnT[:, k, tap:tap + N], cols[:, 3 + tap, k:k + 1],
                                                 xc[:, k, :], ALU.mult, ALU.add).then_inc(s_conv, 1)
                for j in range(KD):
                    n = b * KD + j
                    dve.wait_ge(s_pdt, n + 1)
                    dve.tensor_scalar(arg[:, :], ps_dt[:, :], cols[:, 2, j:j + 1], 20.0,
                                      ALU.add, ALU.min).then_inc(s_arg, 1)
                    dve.wait_ge(s_ex, 2 * n + 2)
                    dve.wait_ge(s_va, 2 * n)
                    dve.tensor_scalar(dt[:, :], ex[:, :], 0.001, 2.0, ALU.max, ALU.min).then_inc(s_dt, 1)
                    dve.wait_ge(s_dt, n + 1)
                    dve.tensor_tensor_scan(decs[:, :], within[:, :], dt[:, :], 0.0,
                                           ALU.mult, ALU.subtract).then_inc(s_dec, 1)
                    dve.wait_ge(s_dec, 3 * n + 1)
                    dve.tensor_scalar(dec[:, :], decs[:, :], -20.0, 0.0, ALU.max, ALU.min).then_inc(s_dec, 1)
                    dve.wait_ge(s_dec, 3 * n + 2)
                    dch = dec[:, :].rearrange("p (c t) -> p c t", t=CH)
                    dve.tensor_tensor(decs[:, :].rearrange("p (c t) -> p c t", t=CH), dch,
                                      dch[:, :, 0:1].to_broadcast([P, NCH, CH]), ALU.subtract).then_inc(s_dec, 1)
                    dve.tensor_tensor_scan(cd[:, :], ones[:, :], dec[:, CH - 1:N:CH], 0.0,
                                           ALU.mult, ALU.add).then_inc(s_cd, 1)
                    dve.wait_ge(s_cd, 3 * n + 1)
                    dve.tensor_scalar(cdc[:, :], cd[:, :], -80.0, 0.0, ALU.max, ALU.min).then_inc(s_cd, 1)
                    dve.wait_ge(s_cd, 3 * n + 2)
                    dve.tensor_scalar(ncd[:, :], cdc[:, :], cdc[:, 0:1], -20.0,
                                      ALU.subtract, ALU.max).then_inc(s_cd, 1)
                    dve.wait_ge(s_pp, n + 1)
                    dve.tensor_tensor(vb[:, :], ps_p[:, :], sin[:, :], ALU.mult).then_inc(s_vb, 1)
                    dve.wait_ge(s_vb, 2 * n + 1)
                    dve.wait_ge(s_va, 2 * n + 1)
                    dve.tensor_tensor(vb[:, :], vb[:, :], va[:, :], ALU.add).then_inc(s_vb, 1)
                    dve.wait_ge(s_exps, 3 * n + 3)
                    dve.wait_ge(s_va, 2 * n + 2)
                    dve.tensor_tensor(vb[:, :], grow[:, :], va[:, :], ALU.mult).then_inc(s_cum, 1)
                    dve.wait_ge(s_cum, 3 * n + 1)
                    dve.tensor_tensor_scan(grow[:, :], within[:, :], vb[:, :], 0.0, ALU.mult, ALU.add).then_inc(s_cum, 1)
                    dve.wait_ge(s_cum, 3 * n + 2)
                    dve.tensor_tensor(final[:, j, :], fade0[:, :], grow[:, :], ALU.mult).then_inc(s_cum, 1)
                    dve.wait_ge(s_cum, 3 * n + 3)
                    dve.wait_ge(s_cexp, 2 * n + 2)
                    dve.tensor_tensor(seeds[:, :], final[:, j, CH - 1:N:CH], up[:, :], ALU.mult).then_inc(s_car, 1)
                    dve.wait_ge(s_car, 3 * n + 1)
                    dve.tensor_tensor_scan(csum[:, :], ones[:, :], seeds[:, :], 0.0, ALU.mult, ALU.add).then_inc(s_car, 1)
                    dve.wait_ge(s_car, 3 * n + 2)
                    dve.tensor_tensor(carry[:, 1:], csum[:, :NCH - 1], down[:, 1:], ALU.mult).then_inc(s_car, 1)
                    dve.wait_ge(s_car, 3 * n + 3)
                    dve.tensor_tensor(vb[:, :].rearrange("p (c t) -> p c t", t=CH),
                                      fade[:, :].rearrange("p (c t) -> p c t", t=CH),
                                      carry[:, :].rearrange("p (c t) -> p c t", t=1).to_broadcast([P, NCH, CH]),
                                      ALU.mult).then_inc(s_fin, 1)
                    dve.wait_ge(s_fin, 2 * n + 1)
                    dve.tensor_tensor(final[:, j, :], final[:, j, :], vb[:, :], ALU.add).then_inc(s_fin, 1)
                    dve.wait_ge(s_fin, 2 * n + 2)
                for m in range(KD):
                    dve.wait_ge(s_sig, KD * b + m + 1)
                    dve.wait_ge(s_pm, KD * b + m + 1)
                    dve.tensor_tensor(gate[:, m, :], banks[m][:, :], gate[:, m, :], ALU.mult).then_inc(s_gm, 1)
                for i in range(SUB):
                    dve.wait_ge(s_po, SUB * b + i + 1)
                    bank = banks[i // 2][:, (i % 2) * HALF:(i % 2 + 1) * HALF]
                    dve.tensor_tensor(x[:, i, :], x[:, i, :], bank, ALU.add).then_inc(s_res, 1)
                dve.wait_ge(s_res, SUB * (b + 1))

        @block.tensor
        def _(pe):
            halves = [slice(0, HALF), slice(HALF, N)]

            def project(bank, group, j, done):
                for hs in halves:
                    for k in range(KD):
                        mm = pe.matmul(bank[:, hs], w_in[:, k, group * D + j * P:group * D + (j + 1) * P],
                                       xc[:, k, hs], start=(k == 0), stop=(k == KD - 1))
                mm.then_inc(done, 1)

            pe.wait_ge(s_tab, 16 * 8)
            pe.wait_ge(s_w, 32)
            pe.wait_ge(s_mix, KD)
            with pe.Fori(0, BATCH) as b:
                pe.wait_ge(s_res, SUB * b)
                pe.wait_ge(s_yn, SUB * (b + 1))
                for k in range(KD):
                    for i in range(SUB):
                        mm = pe.transpose(banks[k][:, i * P:(i + 1) * P], y[:, i, k * P:(k + 1) * P], ident[:, :])
                    mm.then_inc(s_tr, 1)
                pe.wait_ge(s_xc, KD * (b + 1))
                for j in range(KD):
                    n = b * KD + j
                    pe.wait_ge(s_arg, n)
                    project(ps_dt, 0, j, s_pdt)
                    pe.wait_ge(s_v, n)
                    project(ps_v, 1, j, s_pv)
                    pe.wait_ge(s_gate, n)
                    project(ps_g, 2, j, s_pg)
                    pe.wait_ge(s_v, n + 1)
                    pe.wait_ge(s_vb, 2 * n)
                    for hs in halves:
                        mm = pe.matmul(ps_p[:, hs], rot[:, :], v[:, hs], start=True, stop=True)
                    mm.then_inc(s_pp, 1)
                pe.wait_ge(s_gate, KD * (b + 1))
                pe.wait_ge(s_fin, 2 * KD * (b + 1))
                for m in range(KD):
                    for hs in halves:
                        for k in range(KD):
                            mm = pe.matmul(banks[m][:, hs], mix[:, k, m * P:(m + 1) * P], final[:, k, hs],
                                           start=(k == 0), stop=(k == KD - 1))
                    mm.then_inc(s_pm, 1)
                pe.wait_ge(s_gm, KD * (b + 1))
                for i in range(SUB):
                    bank = banks[i // 2][:, (i % 2) * HALF:(i % 2 + 1) * HALF]
                    for k in range(KD):
                        mm = pe.matmul(bank, gate[:, k, i * P:(i + 1) * P], w_out[:, k, :],
                                       start=(k == 0), stop=(k == KD - 1))
                    mm.then_inc(s_po, 1)


def feed_forward(nc, psum, name, consts, x_in, x_out, w_gate, w_up, w_down):
    ROWS, D = x_in.shape
    HID = w_gate.shape[1]
    KD = D // P
    TT = 512
    SUB = TT // P
    TILES = ROWS // TT
    R = 4
    BLK = HID // (P * R)
    with ExitStack() as ctx:
        def sb(n, shape, dt=F32):
            return ctx.enter_context(nc.sbuf_tensor(f"{name}_{n}", shape, dt))

        sem = ctx.enter_context(cleared_semaphores(nc, name))

        ident = sb("ident", [P, P])
        mhalf = sb("mhalf", [P, SUB])
        wg = sb("wg", [P, KD, HID])
        wu = sb("wu", [P, KD, HID])
        wd = sb("wd", [P, BLK, R, D])
        x_tok = sb("x_tok", [P, SUB, D])
        x_res = sb("x_res", [P, SUB, D])
        xn = sb("xn", [P, SUB, D])
        xT = sb("xT", [P, KD, TT])
        stats = sb("stats", [P, SUB, 6])
        mean2, mean, gap, gap2, var, var_eps = (
            sb(n, [P, SUB]) for n in ("mean2", "mean", "gap", "gap2", "var", "var_eps"))
        rstd = sb("rstd", [P, SUB])
        silu = sb("silu", [P, 2, TT])
        h = sb("h", [P, R, TT])
        mag = sb("mag", [P, R, TT])
        wins = sb("wins", [P, 6, TT], BF16)
        score = sb("score", [P, R, TT], BF16)
        kept = sb("kept", [P, 2, R, TT])
        gate_ps, up_ps, *out_ps = (t[:, :].rearrange("p (r t) -> p r t", t=TT) for t in psum)

        s_const = sem("s_const")
        s_wup = sem("s_wup")
        s_wdown = sem("s_wdown")
        s_x = sem("s_x")
        s_res = sem("s_res")
        s_var = sem("s_var")
        s_half = sem("s_half")
        s_rstd = sem("s_rstd")
        s_ln = sem("s_ln")
        s_xn = sem("s_xn")
        s_tr = sem("s_tr")
        s_xT = sem("s_xT")
        s_gate = sem("s_gate")
        s_up = sem("s_up")
        s_silu = sem("s_silu")
        s_h = sem("s_h")
        s_mag = sem("s_mag")
        s_cmp = sem("s_cmp")
        s_kept = sem("s_kept")
        s_down = sem("s_down")
        s_sum = sem("s_sum")
        s_store = sem("s_store")
        CMP = 9
        LN = SUB + 6

        block = ctx.enter_context(nc.Block())

        def rows(ap, t):
            return ap.rearrange("(t s p) d -> t p s d", p=P, s=SUB)[t]

        @block.sync
        def _(sp):
            sp.dma_start(ident[:, :], consts["ident"]).then_inc(s_const, 16)
            sp.dma_start(x_tok[:, :, :], rows(x_in, 0)).then_inc(s_x, 16)
            for k in range(KD):
                sp.dma_start(wg[:, k, :], w_gate[k * P:(k + 1) * P, :]).then_inc(s_wup, 16)
                sp.dma_start(wu[:, k, :], w_up[k * P:(k + 1) * P, :]).then_inc(s_wup, 16)
            sp.dma_start(wd[:, :, :, :],
                         w_down.rearrange("(b g r) n -> g b (r n)", g=P, r=R)).then_inc(s_wdown, 16)

            def load_next(t):
                sp.wait_ge(s_xn, SUB * (t + 1))
                sp.dma_start(x_tok[:, :, :], x_in_t[t + 1]).then_inc(s_x, 16)

            def finish(t):
                sp.dma_start(x_res[:, :, :], x_in_t[t]).then_inc(s_res, 16)
                sp.wait_ge(s_sum, SUB * (t + 1))
                sp.dma_start(x_out_t[t], x_res[:, :, :]).then_inc(s_store, 16)
                sp.wait_ge(s_store, 16 * (t + 1))

            x_in_t = x_in.rearrange("(t s p) d -> t p s d", p=P, s=SUB)
            x_out_t = x_out.rearrange("(t s p) d -> t p s d", p=P, s=SUB)
            for t in range(TILES):
                if t < TILES - 1:
                    load_next(t)
                finish(t)

        @block.gpsimd
        def _(pool):
            pool.memset(mhalf[:, :], -0.5).then_inc(s_half, 1)
            pool.wait_ge(s_half, 1)

            def rstd_of(t):
                pool.wait_ge(s_var, t + 1)
                pool.tensor_tensor(rstd[:, :], var[:, :], mhalf[:, :], ALU.pow).then_inc(s_rstd, 1)

            rstd_of(0)
            with pool.Fori(0, TILES - 1) as t:
                rstd_of(t + 1)

        @block.scalar
        def _(act):
            def to_xT(t):
                for k in range(KD):
                    act.wait_ge(s_tr, KD * t + k + 1)
                    bank = (gate_ps if k < 2 else up_ps)[:, k % 2, :]
                    act.copy(xT[:, k, :], bank).then_inc(s_xT, 1)

            def magnitude(s, r):
                act.wait_ge(s_h, R * s + r + 1)
                if r == 0:
                    act.wait_ge(s_cmp, CMP * s)
                act.activation(mag[:, r, :], h[:, r, :], ACT.Abs).then_inc(s_mag, 1)

            def tile(t, more):
                for b in range(BLK):
                    s = t * BLK + b
                    for r in range(R):
                        n = R * s + r
                        act.wait_ge(s_gate, n + 1)
                        if r >= 2:
                            act.wait_ge(s_h, n - 1)
                        act.activation(silu[:, r % 2, :], gate_ps[:, r % 2, :], ACT.Silu).then_inc(s_silu, 1)
                        if r >= 1:
                            magnitude(s, r - 1)
                    magnitude(s, R - 1)
                if more:
                    to_xT(t + 1)

            to_xT(0)
            with act.Fori(0, TILES - 1) as t:
                tile(t, True)
            tile(TILES - 1, False)

        @block.vector
        def _(dve):
            def layer_norm(t):
                dve.wait_ge(s_x, 16 * (t + 1))
                for i in range(SUB):
                    dve.bn_stats(stats[:, i, :], x_tok[:, i, :]).then_inc(s_ln, 1)
                c = LN * t + SUB
                dve.wait_ge(s_ln, c)
                dve.tensor_tensor(mean2[:, :], stats[:, :, 1], stats[:, :, 4], ALU.add).then_inc(s_ln, 1)
                dve.tensor_tensor(gap[:, :], stats[:, :, 1], stats[:, :, 4], ALU.subtract).then_inc(s_ln, 1)
                dve.tensor_tensor(var[:, :], stats[:, :, 2], stats[:, :, 5], ALU.add).then_inc(s_ln, 1)
                dve.wait_ge(s_ln, c + 3)
                dve.tensor_scalar(mean[:, :], mean2[:, :], 0.5, None, ALU.mult).then_inc(s_ln, 1)
                dve.scalar_tensor_tensor(gap2[:, :], gap[:, :], 0.25, gap[:, :], ALU.mult, ALU.mult).then_inc(s_ln, 1)
                dve.tensor_scalar(var_eps[:, :], var[:, :], 1.0 / D, LN_EPS, ALU.mult, ALU.add).then_inc(s_ln, 1)
                dve.wait_ge(s_ln, c + 6)
                dve.tensor_tensor(var[:, :], var_eps[:, :], gap2[:, :], ALU.add).then_inc(s_var, 1)
                dve.wait_ge(s_rstd, t + 1)
                for i in range(SUB):
                    if i == 0:
                        dve.wait_ge(s_tr, KD * t)
                    dve.tensor_scalar(xn[:, i, :], x_tok[:, i, :], mean[:, i:i + 1], rstd[:, i:i + 1],
                                      ALU.subtract, ALU.mult).then_inc(s_xn, 1)

            def prune(s, b):
                c = CMP * s
                dve.wait_ge(s_kept, R * s)
                for r in range(R):
                    dve.wait_ge(s_silu, R * s + r + 1)
                    dve.wait_ge(s_up, R * s + r + 1)
                    dve.tensor_tensor(h[:, r, :], up_ps[:, r % 2, :], silu[:, r % 2, :], ALU.mult).then_inc(s_h, 1)
                dve.wait_ge(s_mag, R * (s + 1))
                dve.tensor_tensor(wins[:, 0:4:3, :], mag[:, 0:4:2, :], mag[:, 1:4:2, :], ALU.is_ge).then_inc(s_cmp, 1)
                dve.tensor_tensor(wins[:, 1:3, :], mag[:, 0:2, :], mag[:, 2:4, :], ALU.is_ge).then_inc(s_cmp, 1)
                dve.tensor_tensor(wins[:, 4, :], mag[:, 0, :], mag[:, 3, :], ALU.is_ge).then_inc(s_cmp, 1)
                dve.tensor_tensor(wins[:, 5, :], mag[:, 1, :], mag[:, 2, :], ALU.is_ge).then_inc(s_cmp, 1)
                dve.wait_ge(s_cmp, c + 2)
                dve.tensor_tensor(score[:, 0:4:3, :], wins[:, 0:4:3, :], wins[:, 1:3, :], ALU.add).then_inc(s_cmp, 1)
                dve.tensor_tensor(score[:, 1:3, :], wins[:, 2:4, :], wins[:, 0:2, :], ALU.subtract).then_inc(s_cmp, 1)
                dve.wait_ge(s_cmp, c + 6)
                dve.tensor_tensor(score[:, 0:4:3, :], score[:, 0:4:3, :],
                                  wins[:, 4:5, :].to_broadcast([P, 2, TT]), ALU.add).then_inc(s_cmp, 1)
                dve.tensor_tensor(score[:, 1, :], score[:, 1, :], wins[:, 5, :], ALU.add).then_inc(s_cmp, 1)
                dve.tensor_tensor(score[:, 2, :], score[:, 2, :], wins[:, 5, :], ALU.subtract).then_inc(s_cmp, 1)
                dve.wait_ge(s_cmp, c + CMP)
                if b >= 2:
                    dve.wait_ge(s_down, s - 1)
                for r, (least, op) in enumerate(((2.0, ALU.is_ge), (1.0, ALU.is_ge), (0.0, ALU.is_ge), (1.0, ALU.is_le))):
                    dve.scalar_tensor_tensor(kept[:, b % 2, r, :], score[:, r, :], least, h[:, r, :],
                                             op, ALU.mult).then_inc(s_kept, 1)

            def tile(t, more):
                for b in range(BLK):
                    prune(t * BLK + b, b)
                    if b == 1 and more:
                        layer_norm(t + 1)
                dve.wait_ge(s_res, 16 * (t + 1))
                dve.wait_ge(s_down, BLK * (t + 1))
                for i in range(SUB):
                    dve.tensor_tensor(x_res[:, i, :], x_res[:, i, :], out_ps[i // 2][:, i % 2, :], ALU.add).then_inc(s_sum, 1)

            layer_norm(0)
            with dve.Fori(0, TILES - 1) as t:
                tile(t, True)
            tile(TILES - 1, False)

        @block.tensor
        def _(pe):
            def transposes(t):
                for i in range(SUB):
                    pe.wait_ge(s_xn, SUB * t + i + 1)
                for k in range(KD):
                    bank = (gate_ps if k < 2 else up_ps)[:, k % 2, :]
                    for i in range(SUB):
                        mm = pe.transpose(bank[:, i * P:(i + 1) * P], xn[:, i, k * P:(k + 1) * P], ident[:, :])
                    mm.then_inc(s_tr, 1)

            def products_up(s, b):
                for r in range(R):
                    n = R * s + r
                    lo = b * P * R + r
                    if b > 0 or r >= 2:
                        pe.wait_ge(s_silu, n - 1)
                    for k in range(KD):
                        mm = pe.matmul(gate_ps[:, r % 2, :], wg[:, k, lo:lo + (P - 1) * R + 1:R], xT[:, k, :],
                                       start=(k == 0), stop=(k == KD - 1))
                    mm.then_inc(s_gate, 1)
                    if b > 0 or r >= 2:
                        pe.wait_ge(s_h, n - 1)
                    for k in range(KD):
                        mm = pe.matmul(up_ps[:, r % 2, :], wu[:, k, lo:lo + (P - 1) * R + 1:R], xT[:, k, :],
                                       start=(k == 0), stop=(k == KD - 1))
                    mm.then_inc(s_up, 1)

            def products_down(t, s, b):
                pe.wait_ge(s_kept, R * (s + 1))
                if b == 0:
                    pe.wait_ge(s_sum, SUB * t)
                for i in range(SUB):
                    for r in range(R):
                        mm = pe.matmul(out_ps[i // 2][:, i % 2, :], kept[:, b % 2, r, i * P:(i + 1) * P], wd[:, b, r, :],
                                       start=(b == 0 and r == 0), stop=(b == BLK - 1 and r == R - 1))
                mm.then_inc(s_down, 1)

            def tile(t, more):
                pe.wait_ge(s_xT, KD * (t + 1))
                for b in range(BLK):
                    products_up(t * BLK + b, b)
                    if b > 0:
                        products_down(t, t * BLK + b - 1, b - 1)
                if more:
                    pe.wait_ge(s_silu, R * BLK * (t + 1))
                    pe.wait_ge(s_h, R * BLK * (t + 1))
                    transposes(t + 1)
                products_down(t, (t + 1) * BLK - 1, BLK - 1)
            pe.wait_ge(s_const, 16)
            transposes(0)
            pe.wait_ge(s_wup, 32 * KD)
            pe.wait_ge(s_wdown, 16)
            with pe.Fori(0, TILES - 1) as t:
                tile(t, True)
            tile(TILES - 1, False)


def delta_mixer(nc, psum, consts, x_in, x_out, w):
    ROWS, D = x_in.shape
    BATCH = 2
    KD = D // P
    SUBS = ROWS // P
    CHUNKS = SUBS // BATCH
    KH = 8
    VH = 16
    U = 4
    TAPS = 4
    HALO = TAPS - 1
    QK = 6 * P
    LEVELS = (1, 2, 4, 8, 16, 32, 64)
    LV = len(LEVELS) - 1
    TN = 1 + 2 * LV
    GROUPS = 4
    GS = SUBS // GROUPS
    SCALE = float(P) ** -0.5
    G_MIN = -104.0
    with ExitStack() as ctx:
        def sb(n, shape, dt=F32):
            return ctx.enter_context(nc.sbuf_tensor(f"b_{n}", shape, dt))

        sem = ctx.enter_context(cleared_semaphores(nc, "b"))

        ident = sb("ident", [P, P])
        upto = sb("upto", [P, P])
        after = sb("after", [P, P])
        below = sb("below", [P, P])
        full = sb("full", [P, P])
        joins = sb("joins", [P, len(LEVELS), P])
        mhalf = sb("mhalf", [P, U])
        rows = sb("rows", [P, 2, VH])
        norm_w = sb("norm_w", [P, 1])
        w_ba = sb("w_ba", [P, KD, 2 * VH])
        acc = sb("acc", [P, SUBS, D])
        xT = sb("xT", [P, KD, BATCH, CHUNKS * P])
        tab = sb("tab", [P, 5, BATCH, CHUNKS, VH])
        w_load = sb("w_load", [P, KD, QK])
        w_cur = sb("w_cur", [P, KD, QK])
        o_load = sb("o_load", [P, 2, D])
        o_cur = sb("o_cur", [P, 2, D])
        taps_all = sb("taps_all", [P, KH, 4, TAPS])
        taps = sb("taps", [P, 4, TAPS])
        state = sb("state", [P, U, P])
        y = sb("y", [P, GS, D])
        stats = sb("stats", [P, SUBS, 6])
        mean2, mean, gap, gap2, var, var_eps, rstd, mhalf16 = (
            sb(n, [P, SUBS]) for n in ("mean2", "mean", "gap", "gap2", "var", "var_eps", "rstd", "mhalf16"))
        sp_x, sp_abs, sp_e, sp_w, sp_l, sp_r = (
            sb(n, [P, SUBS, VH]) for n in ("sp_x", "sp_abs", "sp_e", "sp_w", "sp_l", "sp_r"))
        x_cur = sb("x_cur", [P, KD, BATCH, P])
        raw = sb("raw", [P, 4, BATCH, HALO + P])
        conv = sb("conv", [P, 4, BATCH, P])
        qkv = sb("qkv", [P, 4, BATCH, P])
        z_raw = sb("z_raw", [P, U, P])
        z_act = sb("z_act", [P, U, P])
        sq = sb("sq", [P, 2, BATCH, P])
        cur = sb("cur", [P, 5, U])
        ss, rr = sb("ss", [P, U]), sb("rr", [P, U])
        brk, cc, ngr, rqs = (sb(n, [P, U]) for n in ("brk", "cc", "ngr", "rqs"))
        gU = sb("gU", [P, U, P])
        em, em_s, em_i = sb("em", [P, U, P]), sb("em_s", [P, U, P]), sb("em_i", [P, U, P])
        k_tok = sb("k_tok", [P, BATCH, P])
        v_tok = sb("v_tok", [P, U, P])
        kb = sb("kb", [P, U, P])
        kbT = sb("kbT", [P, U, P])
        qs = sb("qs", [P, U, P])
        At = sb("At", [P, U, P])
        Pt = sb("Pt", [P, U, P])
        Aj = sb("Aj", [P, len(LEVELS), U, P])
        T, Tt, X = sb("T", [P, U, P]), sb("Tt", [P, U, P]), sb("X", [P, U, P])
        rhs, d, d_end = sb("rhs", [P, U, P]), sb("d", [P, U, P]), sb("d_end", [P, U, P])
        o, xf, xf2, xn = sb("o", [P, U, P]), sb("xf", [P, U, P]), sb("xf2", [P, U, P]), sb("xn", [P, U, P])
        ssq, ssq_eps, rn = sb("ssq", [P, U]), sb("ssq_eps", [P, U]), sb("rn", [P, U])
        xnT = sb("xnT", [P, U, P])
        bank = [t[:, lo:lo + U * P].rearrange("p (u t) -> p u t", t=P) for t in psum for lo in (0, U * P)]

        s = {n: sem(n) for n in (
            "const", "set", "ln", "var", "rstd", "y", "trx", "xT", "ba", "soft", "sums", "tab",
            "w", "ocp", "wcp", "zero",
            "xcur", "pqk", "pv", "pz", "raw", "halo", "zraw", "tap", "conv",
            "cur", "silu", "zact", "sq", "ss", "sse", "rr", "scal", "gU", "dt", "em", "emm", "ktok", "vtok",
            "ktoks", "vtoks", "ks", "kqs", "qss", "kb", "kbt", "kbT", "at", "atm", "joined", "T0", "T", "Tps",
            "px", "X", "py", "rhs", "pd", "d", "pod", "dend", "ps", "S", "o", "xf", "sqs", "sse2", "rn", "xn",
            "txn", "xnT", "po", "acc", "store", "sums_dve", "tset", "gate")}

        s_x = [sem(f"x{g}") for g in range(GROUPS)]

        block = ctx.enter_context(nc.Block())

        @block.sync
        def _(sp):
            xr = x_in.rearrange("(s p) d -> p s d", p=P)
            for g in range(GROUPS):
                part = slice(g * GS, (g + 1) * GS)
                sp.dma_start(acc[:, part, :], xr[:, part, :]).then_inc(s_x[g], 16)
            for tile, src in ((ident, "ident"), (upto, "upto"), (after, "after"), (below, "below"),
                              (joins, "joins"), (rows, "rows"), (norm_w, "norm_w"), (w_ba, "w_ba"),
                              (taps_all, "taps")):
                sp.dma_start(tile[:], w[src] if src in w else consts[src]).then_inc(s["const"], 16)
            for h in range(KH):
                if h > 0:
                    sp.wait_ge(s["wcp"], h)
                    sp.wait_ge(s["ocp"], h)
                sp.dma_start(w_load[:, :, :], w["b_qkvz"].rearrange("(k p) n -> p k n", p=P)
                             [:, :, h * QK:(h + 1) * QK]).then_inc(s["w"], 16)
                sp.dma_start(o_load[:, :, :], w["b_out"].rearrange("(h i p) n -> h p i n", p=P, i=2)[h]
                             ).then_inc(s["w"], 16)
            outr = x_out.rearrange("(s p) d -> p s d", p=P)
            sp.wait_ge(s["acc"], 2 * KH * CHUNKS)
            sp.dma_start(outr, acc[:, :, :]).then_inc(s["store"], 16)
            sp.wait_ge(s["store"], 16)

        @block.gpsimd
        def _(pool):
            pool.memset(mhalf[:, :], -0.5).then_inc(s["set"], 1)
            pool.memset(mhalf16[:, :], -0.5).then_inc(s["set"], 1)
            pool.memset(full[:, :], 1.0).then_inc(s["set"], 1)
            pool.wait_ge(s["const"], 16 * 9)
            pool.wait_ge(s["set"], 3)
            pool.wait_ge(s["var"], 1)
            pool.tensor_tensor(rstd[:, :], var[:, :], mhalf16[:, :], ALU.pow).then_inc(s["rstd"], 1)
            pool.wait_ge(s["xT"], GROUPS * KD)

            def chunk_of_x(c, n):
                pool.wait_ge(s["pz"], n)
                pool.sem_inc(s["gate"], 1)
                pool.tensor_copy(x_cur[:, :, :, :], xT[:, :, :, bass.ds(c * P, P)]).then_inc(s["xcur"], 1)

            def step(q, c, more):
                pool.wait_ge(s["sse"], q + 1)
                pool.tensor_tensor(rr[:, :], ss[:, :], mhalf[:, :], ALU.pow).then_inc(s["rr"], 1)
                pool.wait_ge(s["em"], q + 1)
                pool.wait_ge(s["atm"], 2 * q)
                for out, mask in ((em_s, below), (em_i, upto)):
                    pool.tensor_tensor(out[:, :, :], em[:, :, :],
                                       mask[:, :].rearrange("p (u t) -> p u t", u=1).to_broadcast([P, U, P]),
                                       ALU.mult).then_inc(s["emm"], 1)
                if more:
                    chunk_of_x(c + 1, q + 1)
                pool.wait_ge(s["atm"], 2 * q + 1)
                for i in range(1, len(LEVELS)):
                    pool.tensor_tensor(Aj[:, i, :, :], At[:, :, :],
                                       joins[:, i:i + 1, :].to_broadcast([P, U, P]), ALU.mult).then_inc(s["joined"], 1)
                pool.wait_ge(s["sse2"], q + 1)
                pool.tensor_tensor(rn[:, :], ssq_eps[:, :], mhalf[:, :], ALU.pow).then_inc(s["rn"], 1)

            with pool.Fori(0, KH) as h:
                pool.wait_ge(s["S"], U * h * CHUNKS)
                pool.sem_inc(s["gate"], 1)
                pool.memset(state[:, :, :], 0.0).then_inc(s["zero"], 1)
                pool.wait_ge(s["w"], 32 * (h + 1))
                pool.wait_ge(s["po"], 2 * h * CHUNKS)
                pool.sem_inc(s["gate"], 1)
                pool.tensor_copy(o_cur[:, :, :], o_load[:, :, :]).then_inc(s["ocp"], 1)
                chunk_of_x(0, h * CHUNKS)
                with pool.Fori(0, CHUNKS - 1) as c:
                    step(h * CHUNKS + c, c, True)
                step(h * CHUNKS + CHUNKS - 1, CHUNKS - 1, False)

        @block.scalar
        def _(act):
            act.wait_ge(s["const"], 16 * 9)
            for g in range(GROUPS):
                for k in range(KD):
                    act.wait_ge(s["trx"], KD * g + k + 1)
                    b, t0 = divmod(g * GS * P, CHUNKS * P)
                    act.copy(xT[:, k, b, t0:t0 + GS * P], bank[k][:, :, :].rearrange("p u t -> p (u t)")
                             ).then_inc(s["xT"], 1)
            ba = bank[4][:, :, :].rearrange("p u t -> p (u t)").rearrange("p (s n) -> p s n", n=2 * VH)
            act.wait_ge(s["ba"], 1)
            act.activation(tab[:, 1, :, :, :].rearrange("p b c v -> p (b c) v"), ba[:, :, 0:VH],
                           ACT.Sigmoid).then_inc(s["soft"], 1)
            act.activation(rows[:, 1, :], rows[:, 1, :], ACT.Exp).then_inc(s["soft"], 1)
            act.wait_ge(s["tab"], 1)
            act.activation(sp_e[:, :, :], sp_abs[:, :, :], ACT.Exp, scale=-1.0).then_inc(s["soft"], 1)
            act.wait_ge(s["tab"], 2)
            act.activation(sp_l[:, :, :], sp_w[:, :, :], ACT.Ln).then_inc(s["soft"], 1)
            act.wait_ge(s["sums"], 3)
            for i in range(3):
                act.activation(tab[:, 2 + i, :, :, :].rearrange("p b c v -> p (b c v)"),
                               bank[5 + i][:, 0:2, :].rearrange("p u t -> p (u t)"), ACT.Exp).then_inc(s["soft"], 1)

            def projected(n):
                for i, (p, b0) in enumerate((("pqk", 0), ("pv", 1))):
                    act.wait_ge(s[p], n + 1)
                    if i == 0:
                        act.wait_ge(s["halo"], n + 1)
                    act.copy(raw[:, 2 * i:2 * i + 2, :, HALO:],
                             bank[b0][:, :, :].rearrange("p (a b) t -> p a b t", b=BATCH)).then_inc(s["raw"], 1)
                act.wait_ge(s["raw"], 2 * (n + 1))
                act.wait_ge(s["silu"], n)
                for i in range(4):
                    act.activation(conv[:, i, :, :], raw[:, i, :, 0:P], ACT.Copy,
                                   scale=taps[:, i, 0:1]).then_inc(s["tap"], 1)
                act.wait_ge(s["pz"], n + 1)
                act.wait_ge(s["zact"], n)
                act.copy(z_raw[:, :, :], bank[0][:, :, :]).then_inc(s["zraw"], 1)

            def step(q, more):
                act.wait_ge(s["conv"], 12 * (q + 1))
                act.wait_ge(s["kqs"], q)
                act.wait_ge(s["at"], 2 * q)
                act.activation(qkv[:, :, :, :], conv[:, :, :, :], ACT.Silu).then_inc(s["silu"], 1)
                act.wait_ge(s["zraw"], q + 1)
                act.wait_ge(s["xf"], U * q)
                act.activation(z_act[:, :, :], z_raw[:, :, :], ACT.Silu).then_inc(s["zact"], 1)
                act.wait_ge(s["silu"], q + 1)
                act.wait_ge(s["ss"], q)
                act.activation(sq[:, :, :, :], qkv[:, 0:2, :, :], ACT.Square).then_inc(s["sq"], 1)
                act.wait_ge(s["dt"], q + 1)
                act.wait_ge(s["emm"], 2 * q)
                act.activation(em[:, :, :], bank[2][:, :, :], ACT.Exp).then_inc(s["em"], 1)
                act.wait_ge(s["ktok"], q + 1)
                act.wait_ge(s["kb"], U * q)
                act.wait_ge(s["ps"], q)
                act.copy(k_tok[:, :, :], bank[3][:, 0:2, :]).then_inc(s["ktoks"], 1)
                act.wait_ge(s["vtok"], q + 1)
                act.wait_ge(s["rhs"], 2 * U * q)
                act.copy(v_tok[:, :, :], bank[4][:, :, :]).then_inc(s["vtoks"], 1)
                act.wait_ge(s["kqs"], q + 1)
                act.wait_ge(s["cur"], q + 1)
                act.wait_ge(s["o"], q)
                for u in range(U):
                    act.activation(qs[:, u, :], bank[6][:, u, :], ACT.Copy, scale=cur[:, 2, u:u + 1]
                                   ).then_inc(s["qss"], 1)
                act.wait_ge(s["kbt"], q + 1)
                act.wait_ge(s["at"], 2 * q)
                act.copy(kbT[:, :, :], bank[7][:, :, :]).then_inc(s["kbT"], 1)
                act.wait_ge(s["Tps"], q + 1)
                act.wait_ge(s["py"], LV * q)
                act.copy(T[:, :, :], bank[5][:, :, :]).then_inc(s["T0"], 1)
                for i in range(LV):
                    act.wait_ge(s["px"], LV * q + i + 1)
                    act.wait_ge(s["py"], LV * q + i)
                    act.copy(X[:, :, :], bank[2][:, :, :]).then_inc(s["X"], 1)
                if more:
                    projected(q + 1)
                act.wait_ge(s["txn"], q + 1)
                act.wait_ge(s["po"], 2 * q)
                act.activation(xnT[:, :, :], bank[2][:, :, :], ACT.Copy, scale=norm_w[:, 0:1]).then_inc(s["xnT"], 1)

            with act.Fori(0, KH) as h:
                act.wait_ge(s["w"], 32 * (h + 1))
                act.wait_ge(s["pz"], h * CHUNKS)
                act.copy(w_cur[:, :, :], w_load[:, :, :]).then_inc(s["wcp"], 1)
                projected(h * CHUNKS)
                with act.Fori(0, CHUNKS - 1) as c:
                    step(h * CHUNKS + c, True)
                step(h * CHUNKS + CHUNKS - 1, False)

        @block.vector
        def _(dve):
            for g in range(GROUPS):
                dve.wait_ge(s_x[g], 16)
                for i in range(g * GS, (g + 1) * GS):
                    dve.bn_stats(stats[:, i, :], acc[:, i, :]).then_inc(s["ln"], 1)
            c = SUBS
            dve.wait_ge(s["ln"], c)
            dve.tensor_tensor(mean2[:, :], stats[:, :, 1], stats[:, :, 4], ALU.add).then_inc(s["ln"], 1)
            dve.tensor_tensor(gap[:, :], stats[:, :, 1], stats[:, :, 4], ALU.subtract).then_inc(s["ln"], 1)
            dve.tensor_tensor(var[:, :], stats[:, :, 2], stats[:, :, 5], ALU.add).then_inc(s["ln"], 1)
            dve.wait_ge(s["ln"], c + 3)
            dve.tensor_scalar(mean[:, :], mean2[:, :], 0.5, None, ALU.mult).then_inc(s["ln"], 1)
            dve.scalar_tensor_tensor(gap2[:, :], gap[:, :], 0.25, gap[:, :], ALU.mult, ALU.mult).then_inc(s["ln"], 1)
            dve.tensor_scalar(var_eps[:, :], var[:, :], 1.0 / D, LN_EPS, ALU.mult, ALU.add).then_inc(s["ln"], 1)
            dve.wait_ge(s["ln"], c + 6)
            dve.tensor_tensor(var[:, :], var_eps[:, :], gap2[:, :], ALU.add).then_inc(s["var"], 1)
            dve.wait_ge(s["rstd"], 1)
            for g in range(GROUPS):
                dve.wait_ge(s["trx"], KD * g)
                for i in range(GS):
                    n = g * GS + i
                    dve.tensor_scalar(y[:, i, :], acc[:, n, :], mean[:, n:n + 1], rstd[:, n:n + 1],
                                      ALU.subtract, ALU.mult).then_inc(s["y"], 1)
            ba = bank[4][:, :, :].rearrange("p u t -> p (u t)").rearrange("p (s n) -> p s n", n=2 * VH)
            dve.wait_ge(s["const"], 16 * 9)
            dve.wait_ge(s["ba"], 1)
            dve.wait_ge(s["soft"], 1)
            dt_bias = rows[:, 0:1, :].to_broadcast([P, SUBS, VH])
            step_no = [0]

            def chain(ins):
                step_no[0] += 1
                ins.then_inc(s["sums_dve"], 1)
                dve.wait_ge(s["sums_dve"], step_no[0])

            chain(dve.tensor_tensor(sp_x[:, :, :], ba[:, :, VH:2 * VH], dt_bias, ALU.add))
            chain(dve.tensor_scalar(sp_r[:, :, :], sp_x[:, :, :], -1.0, None, ALU.mult))
            dve.tensor_tensor(sp_abs[:, :, :], sp_x[:, :, :], sp_r[:, :, :], ALU.max).then_inc(s["tab"], 1)
            dve.wait_ge(s["soft"], 3)
            dve.tensor_scalar(sp_w[:, :, :], sp_e[:, :, :], 1.0, None, ALU.add).then_inc(s["tab"], 1)
            dve.wait_ge(s["tab"], 2)
            chain(dve.tensor_scalar(sp_r[:, :, :], sp_w[:, :, :], 1.0, None, ALU.subtract))
            chain(dve.tensor_scalar(sp_abs[:, :, :], sp_r[:, :, :], 0.0, None, ALU.is_equal))
            chain(dve.tensor_tensor(sp_r[:, :, :], sp_r[:, :, :], sp_abs[:, :, :], ALU.add))
            chain(dve.reciprocal(sp_r[:, :, :], sp_r[:, :, :]))
            dve.wait_ge(s["soft"], 4)
            chain(dve.tensor_tensor(sp_l[:, :, :], sp_l[:, :, :], sp_abs[:, :, :], ALU.add))
            chain(dve.tensor_tensor(sp_l[:, :, :], sp_l[:, :, :], sp_e[:, :, :], ALU.mult))
            chain(dve.tensor_tensor(sp_l[:, :, :], sp_l[:, :, :], sp_r[:, :, :], ALU.mult))
            chain(dve.scalar_tensor_tensor(sp_l[:, :, :], sp_x[:, :, :], 0.0, sp_l[:, :, :], ALU.max, ALU.add))
            chain(dve.tensor_tensor(sp_l[:, :, :], sp_l[:, :, :],
                                    rows[:, 1:2, :].to_broadcast([P, SUBS, VH]), ALU.mult))
            dve.tensor_scalar(tab[:, 0, :, :, :].rearrange("p b c v -> p (b c) v"), sp_l[:, :, :],
                              -1.0, G_MIN, ALU.mult, ALU.max).then_inc(s["tab"], 1)
            dve.wait_ge(s["soft"], 7)
            dve.wait_ge(s["tab"], 3)

            def halo(n):
                dve.wait_ge(s["tap"], 4 * n)
                dve.wait_ge(s["conv"], 12 * n)
                dve.tensor_copy(raw[:, :, :, 0:HALO], raw[:, :, :, P:P + HALO]).then_inc(s["halo"], 1)

            def convolve(n):
                for i in range(4):
                    for tap in range(1, TAPS):
                        if tap == 1:
                            dve.wait_ge(s["tap"], 4 * n + i + 1)
                        else:
                            dve.wait_ge(s["conv"], 12 * n + 3 * i + tap - 1)
                        dve.scalar_tensor_tensor(conv[:, i, :, :], raw[:, i, :, tap:tap + P], taps[:, i, tap:tap + 1],
                                                 conv[:, i, :, :], ALU.mult, ALU.add).then_inc(s["conv"], 1)

            def b4(ap):
                return ap.rearrange("p (b i) -> p b i", i=1).to_broadcast([P, BATCH, 2])

            def u4(ap):
                return ap.rearrange("p (b i) -> p b i", i=2)

            def step(q, h, c, more):
                dve.wait_ge(s["S"], U * q)
                dve.wait_ge(s["xn"], U * q)
                dve.wait_ge(s["qss"], U * q)
                dve.tensor_copy(cur[:, :, :].rearrange("p n (b i) -> p n b i", i=2),
                                tab[:, :, :, bass.ds(c, 1), bass.ds(2 * h, 2)].rearrange("p n b c i -> p n (b c) i")
                                ).then_inc(s["cur"], 1)
                dve.wait_ge(s["cur"], q + 1)
                dve.wait_ge(s["dt"], q)
                for u in range(U):
                    dve.tensor_scalar(gU[:, u, :], upto[:, :], cur[:, 0, u:u + 1], None, ALU.mult).then_inc(s["gU"], 1)
                if more:
                    halo(q + 1)
                dve.wait_ge(s["ss"], q + 1)
                dve.tensor_scalar(ss[:, :], bank[7][:, 0, 0:U], 1e-6, None, ALU.add).then_inc(s["sse"], 1)
                dve.wait_ge(s["rr"], q + 1)
                dve.wait_ge(s["kb"], U * q)
                dve.wait_ge(s["rhs"], 2 * U * q)
                k0 = 5 * q
                dve.tensor_scalar(rqs[:, 0:2], rr[:, 0:2], SCALE, None, ALU.mult).then_inc(s["scal"], 1)
                dve.tensor_tensor(u4(brk[:, :]), u4(cur[:, 1, :]), b4(rr[:, 2:4]), ALU.mult).then_inc(s["scal"], 1)
                dve.tensor_tensor(u4(ngr[:, :]), u4(cur[:, 2, :]), b4(rr[:, 2:4]), ALU.mult).then_inc(s["scal"], 1)
                dve.wait_ge(s["scal"], k0 + 3)
                dve.tensor_tensor(u4(cc[:, :]), u4(brk[:, :]), b4(rr[:, 2:4]), ALU.mult).then_inc(s["scal"], 1)
                dve.tensor_scalar(ngr[:, :], ngr[:, :], -1.0, None, ALU.mult).then_inc(s["scal"], 1)
                dve.wait_ge(s["scal"], k0 + 5)
                dve.wait_ge(s["ktoks"], q + 1)
                dve.wait_ge(s["kbt"], q)
                for u in range(U):
                    dve.tensor_scalar(kb[:, u, :], k_tok[:, u // 2, :], cc[:, u:u + 1], None, ALU.mult
                                      ).then_inc(s["kb"], 1)
                dve.wait_ge(s["kqs"], q + 1)
                dve.wait_ge(s["vtoks"], q + 1)
                dve.wait_ge(s["pd"], q)
                for u in range(U):
                    dve.scalar_tensor_tensor(rhs[:, u, :], bank[5][:, u, :], ngr[:, u:u + 1], v_tok[:, u, :],
                                             ALU.mult, ALU.add).then_inc(s["rhs"], 1)
                dve.wait_ge(s["rhs"], 2 * U * q + U)
                for u in range(U):
                    dve.tensor_scalar(rhs[:, u, :], rhs[:, u, :], brk[:, u:u + 1], None, ALU.mult).then_inc(s["rhs"], 1)
                dve.wait_ge(s["emm"], 2 * q + 2)
                dve.wait_ge(s["at"], 2 * q + 1)
                dve.wait_ge(s["joined"], LV * q)
                dve.tensor_tensor(At[:, :, :], bank[2][:, :, :], em_s[:, :, :], ALU.mult).then_inc(s["atm"], 1)
                dve.wait_ge(s["at"], 2 * q + 2)
                dve.wait_ge(s["pod"], q)
                qk = bank[3][:, 0:2, :].rearrange("p b (i t) -> p b i t", i=1).to_broadcast([P, BATCH, 2, P])
                dve.tensor_tensor(Pt[:, :, :].rearrange("p (b i) t -> p b i t", i=2), qk,
                                  em_i[:, :, :].rearrange("p (b i) t -> p b i t", i=2), ALU.mult).then_inc(s["atm"], 1)
                dve.wait_ge(s["atm"], 2 * q + 1)
                dve.wait_ge(s["T"], TN * q)
                dve.tensor_tensor(Aj[:, 0, :, :], At[:, :, :], joins[:, 0:1, :].to_broadcast([P, U, P]),
                                  ALU.mult).then_inc(s["T"], 1)
                dve.wait_ge(s["T"], TN * q + 1)
                dve.tensor_tensor(Tt[:, :, :], Aj[:, 0, :, :],
                                  ident[:, :].rearrange("p (u t) -> p u t", u=1).to_broadcast([P, U, P]),
                                  ALU.add).then_inc(s["T"], 1)
                dve.wait_ge(s["T0"], q + 1)
                for i in range(LV):
                    dve.wait_ge(s["py"], LV * q + i + 1)
                    dve.wait_ge(s["T"], TN * q + 2 + 2 * i)
                    if i < LV - 1:
                        dve.tensor_tensor(T[:, :, :], T[:, :, :], bank[5][:, :, :], ALU.add).then_inc(s["T"], 1)
                    dve.tensor_tensor(Tt[:, :, :], Tt[:, :, :], bank[7][:, :, :], ALU.add).then_inc(s["T"], 1)
                if more:
                    convolve(q + 1)
                dve.wait_ge(s["pd"], q + 1)
                dve.wait_ge(s["pod"], q)
                dve.tensor_copy(d[:, :, :], bank[4][:, :, :]).then_inc(s["d"], 1)
                dve.wait_ge(s["d"], q + 1)
                dve.wait_ge(s["ps"], q)
                for u in range(U):
                    dve.tensor_scalar(d_end[:, u, :], d[:, u, :], cur[:, 3, u:u + 1], None, ALU.mult
                                      ).then_inc(s["dend"], 1)
                dve.wait_ge(s["pod"], q + 1)
                dve.wait_ge(s["qss"], U * (q + 1))
                dve.wait_ge(s["xf"], U * q)
                dve.tensor_tensor(o[:, :, :], bank[6][:, :, :], qs[:, :, :], ALU.add).then_inc(s["o"], 1)
                dve.wait_ge(s["ps"], q + 1)
                dve.wait_ge(s["zero"], h + 1)
                for u in range(U):
                    dve.scalar_tensor_tensor(state[:, u, :], state[:, u, :], cur[:, 4, u:u + 1], bank[5][:, u, :],
                                             ALU.mult, ALU.add).then_inc(s["S"], 1)
                dve.wait_ge(s["o"], q + 1)
                dve.wait_ge(s["zact"], q + 1)
                dve.wait_ge(s["xn"], U * q)
                for u in range(U):
                    dve.scalar_tensor_tensor(xf[:, u, :], o[:, u, :], rqs[:, u // 2:u // 2 + 1], z_act[:, u, :],
                                             ALU.mult, ALU.mult).then_inc(s["xf"], 1)
                dve.wait_ge(s["xf"], U * (q + 1))
                dve.tensor_tensor(xf2[:, :, :], xf[:, :, :], xf[:, :, :], ALU.mult).then_inc(s["sqs"], 1)
                dve.wait_ge(s["sqs"], 2 * q + 1)
                dve.tensor_reduce(ssq[:, :], xf2[:, :, :], AX.X, ALU.add).then_inc(s["sqs"], 1)
                dve.wait_ge(s["sqs"], 2 * q + 2)
                dve.tensor_scalar(ssq_eps[:, :], ssq[:, :], 1.0 / P, 1e-6, ALU.mult, ALU.add).then_inc(s["sse2"], 1)
                dve.wait_ge(s["rn"], q + 1)
                dve.wait_ge(s["txn"], q)
                for u in range(U):
                    dve.tensor_scalar(xn[:, u, :], xf[:, u, :], rn[:, u:u + 1], None, ALU.mult).then_inc(s["xn"], 1)
                for b in range(BATCH):
                    dve.wait_ge(s["po"], 2 * q + b + 1)
                    dst = acc[:, bass.ds(c + b * CHUNKS, 1), :].rearrange("p c d -> p (c d)")
                    dve.tensor_tensor(dst, dst, bank[3 if b == 0 else 7][:, :, :].rearrange("p u t -> p (u t)"),
                                      ALU.add).then_inc(s["acc"], 1)

            with dve.Fori(0, KH) as h:
                dve.wait_ge(s["conv"], 12 * h * CHUNKS)
                dve.wait_ge(s["tap"], 4 * h * CHUNKS)
                dve.tensor_copy(taps[:, :, :], taps_all[:, bass.ds(h, 1), :, :].rearrange("p h a b -> p (h a) b")
                                ).then_inc(s["tset"], 1)
                dve.wait_ge(s["tset"], 2 * h + 1)
                dve.memset(raw[:, :, :, P:P + HALO], 0.0).then_inc(s["tset"], 1)
                dve.wait_ge(s["tset"], 2 * h + 2)
                halo(h * CHUNKS)
                convolve(h * CHUNKS)
                with dve.Fori(0, CHUNKS - 1) as c:
                    step(h * CHUNKS + c, h, c, True)
                step(h * CHUNKS + CHUNKS - 1, h, CHUNKS - 1, False)

        @block.tensor
        def _(pe):
            pe.wait_ge(s["const"], 16 * 9)
            pe.wait_ge(s["set"], 3)
            for g in range(GROUPS):
                pe.wait_ge(s["y"], GS * (g + 1))
                pe.wait_ge(s["xT"], KD * g)
                for k in range(KD):
                    for i in range(GS):
                        mm = pe.transpose(bank[k][:, i, :], y[:, i, k * P:(k + 1) * P], ident[:, :])
                    mm.then_inc(s["trx"], 1)
            pe.wait_ge(s["xT"], KD * GROUPS)
            ba = bank[4][:, :, :].rearrange("p u t -> p (u t)").rearrange("p (s n) -> p s n", n=2 * VH)
            for n in range(SUBS):
                b, c = divmod(n, CHUNKS)
                for k in range(KD):
                    mm = pe.matmul(ba[:, n, :], xT[:, k, b, c * P:(c + 1) * P], w_ba[:, k, :],
                                   start=(k == 0), stop=(k == KD - 1))
            mm.then_inc(s["ba"], 1)
            pe.wait_ge(s["tab"], 3)
            for i, sums in enumerate((upto, after, full)):
                pe.matmul(bank[5 + i][:, 0:2, :].rearrange("p u t -> p (u t)"), sums[:, :],
                          tab[:, 0, :, :, :].rearrange("p b c v -> p (b c v)"),
                          start=True, stop=True).then_inc(s["sums"], 1)
            pe.wait_ge(s["soft"], 7)

            def project(n):
                pe.wait_ge(s["xcur"], n + 1)
                pe.wait_ge(s["zraw"], n)
                for i, done in enumerate(("pqk", "pv")):
                    if i == 1:
                        pe.wait_ge(s["raw"], 2 * n)
                    for a in range(2):
                        col = (2 * i + a) * P
                        for k in range(KD):
                            mm = pe.matmul(bank[i][:, 2 * a:2 * a + 2, :], w_cur[:, k, col:col + P],
                                           x_cur[:, k, :, :], start=(k == 0), stop=(k == KD - 1))
                    mm.then_inc(s[done], 1)
                pe.wait_ge(s["raw"], 2 * n + 1)
                for b in range(BATCH):
                    for k in range(KD):
                        mm = pe.matmul(bank[0][:, 2 * b:2 * b + 2, :], x_cur[:, k, b, :], w_cur[:, k, 4 * P:6 * P],
                                       start=(k == 0), stop=(k == KD - 1))
                mm.then_inc(s["pz"], 1)

            def step(q, more):
                pe.wait_ge(s["gU"], U * (q + 1))
                pe.wait_ge(s["xnT"], q)
                pe.matmul(bank[2][:, :, :], after[:, :], gU[:, :, :], start=True, stop=True).then_inc(s["dt"], 1)
                pe.wait_ge(s["acc"], 2 * q)
                pe.wait_ge(s["silu"], q + 1)
                for b in range(BATCH):
                    mm = pe.transpose(bank[3][:, b, :], qkv[:, 1, b, :], ident[:, :])
                mm.then_inc(s["ktok"], 1)
                pe.wait_ge(s["d"], q)
                for u in range(U):
                    mm = pe.transpose(bank[4][:, u, :], qkv[:, 2 + u % 2, u // 2, :], ident[:, :])
                mm.then_inc(s["vtok"], 1)
                pe.wait_ge(s["sq"], q + 1)
                for a in range(2):
                    for b in range(BATCH):
                        mm = pe.matmul(bank[7][:, 0, 2 * a + b:2 * a + b + 1], sq[:, a, b, :], full[:, 0:1],
                                       start=True, stop=True)
                mm.then_inc(s["ss"], 1)
                pe.wait_ge(s["S"], U * q)
                pe.wait_ge(s["o"], q)
                for a, bk in ((1, 5), (0, 6)):
                    for b in range(BATCH):
                        mm = pe.matmul(bank[bk][:, 2 * b:2 * b + 2, :], qkv[:, a, b, :], state[:, 2 * b:2 * b + 2, :],
                                       start=True, stop=True)
                mm.then_inc(s["kqs"], 1)
                pe.wait_ge(s["kb"], U * (q + 1))
                for u in range(U):
                    mm = pe.transpose(bank[7][:, u, :], kb[:, u, :], ident[:, :])
                mm.then_inc(s["kbt"], 1)
                pe.wait_ge(s["kbT"], q + 1)
                pe.wait_ge(s["em"], q + 1)
                for b in range(BATCH):
                    mm = pe.matmul(bank[2][:, 2 * b:2 * b + 2, :], qkv[:, 1, b, :], kbT[:, 2 * b:2 * b + 2, :],
                                   start=True, stop=True)
                mm.then_inc(s["at"], 1)
                pe.wait_ge(s["ktoks"], q + 1)
                pe.wait_ge(s["sse"], q + 1)
                for b in range(BATCH):
                    mm = pe.matmul(bank[3][:, b, :], qkv[:, 1, b, :], qkv[:, 0, b, :], start=True, stop=True)
                mm.then_inc(s["at"], 1)
                pe.wait_ge(s["T"], TN * q + 2)
                pe.wait_ge(s["rhs"], 2 * U * (q + 1))
                for u in range(U):
                    mm = pe.transpose(bank[5][:, u, :], Tt[:, u, :], ident[:, :])
                mm.then_inc(s["Tps"], 1)
                for i in range(LV):
                    if i == 0:
                        pe.wait_ge(s["T0"], q + 1)
                        pe.wait_ge(s["atm"], 2 * q + 1)
                    pe.wait_ge(s["joined"], LV * q + i + 1)
                    pe.wait_ge(s["T"], TN * q + 2 + 2 * i)
                    for u in range(U):
                        mm = pe.matmul(bank[2][:, u, :], Aj[:, i + 1, u, :], T[:, u, :], start=True, stop=True)
                    mm.then_inc(s["px"], 1)
                    pe.wait_ge(s["X"], LV * q + i + 1)
                    for u in range(U):
                        if i < LV - 1:
                            pe.matmul(bank[5][:, u, :], Tt[:, u, :], X[:, u, :], start=True, stop=True)
                        mm = pe.matmul(bank[7][:, u, :], X[:, u, :], Tt[:, u, :], start=True, stop=True)
                    mm.then_inc(s["py"], 1)
                if more:
                    project(q + 1)
                pe.wait_ge(s["T"], TN * (q + 1))
                pe.wait_ge(s["vtoks"], q + 1)
                for u in range(U):
                    mm = pe.matmul(bank[4][:, u, :], Tt[:, u, :], rhs[:, u, :], start=True, stop=True)
                mm.then_inc(s["pd"], 1)
                pe.wait_ge(s["d"], q + 1)
                pe.wait_ge(s["atm"], 2 * q + 2)
                pe.wait_ge(s["qss"], U * (q + 1))
                for u in range(U):
                    mm = pe.matmul(bank[6][:, u, :], Pt[:, u, :], d[:, u, :], start=True, stop=True)
                mm.then_inc(s["pod"], 1)
                pe.wait_ge(s["dend"], U * (q + 1))
                for b in range(BATCH):
                    mm = pe.matmul(bank[5][:, 2 * b:2 * b + 2, :], k_tok[:, b, :], d_end[:, 2 * b:2 * b + 2, :],
                                   start=True, stop=True)
                mm.then_inc(s["ps"], 1)
                pe.wait_ge(s["xn"], U * (q + 1))
                for u in range(U):
                    mm = pe.transpose(bank[2][:, u, :], xn[:, u, :], ident[:, :])
                mm.then_inc(s["txn"], 1)
                pe.wait_ge(s["xnT"], q + 1)
                for b in range(BATCH):
                    out = bank[3 if b == 0 else 7][:, :, :].rearrange("p u t -> p (u t)")
                    for i in range(2):
                        mm = pe.matmul(out, xnT[:, 2 * b + i, :], o_cur[:, i, :], start=(i == 0), stop=(i == 1))
                    mm.then_inc(s["po"], 1)

            with pe.Fori(0, KH) as h:
                pe.wait_ge(s["wcp"], h + 1)
                pe.wait_ge(s["zero"], h + 1)
                pe.wait_ge(s["ocp"], h + 1)
                project(h * CHUNKS)
                with pe.Fori(0, CHUNKS - 1) as c:
                    step(h * CHUNKS + c, True)
                step(h * CHUNKS + CHUNKS - 1, False)


def layer_stack(nc, ins, out):
    rows = out.shape[0] * out.shape[1]
    dim = out.shape[2]
    x1, x2, x3 = (nc.dram_tensor(f"rows_{i}", (rows, dim), F32, kind="Internal").ap() for i in (1, 2, 3))
    with ExitStack() as ctx:
        psum = [ctx.enter_context(nc.psum_tensor(f"banks_{i}", (P, 1024), F32)) for i in range(4)]
        decay_mixer(nc, psum, ins, ins["x"], x1, ins)
        ffn = (ins["ffn_gate"], ins["ffn_up"], ins["ffn_down"])
        feed_forward(nc, psum, "f1", ins, x1, x2, *ffn)
        delta_mixer(nc, psum, ins, x2, x3, ins)
        feed_forward(nc, psum, "f2", ins, x3, out.rearrange("b n d -> (b n) d"), *ffn)


def _laid_out(i):
    import numpy as np
    heads_a, key_heads = 16, 8
    width = i["L0_attn_a_in_proj_w"].shape[1]
    tiles = width // P
    column = lambda a: a.reshape(tiles, P, -1)
    cols = np.concatenate([column(i[f"L0_attn_a_{n}"]) for n in ("norm_scale", "conv_b", "dt_bias", "conv_w")], 2)
    ba = i["L0_attn_b_w_ba"].reshape(key_heads, 2, 2, width)
    taps = i["L0_attn_b_conv_w"]
    keys = key_heads * P
    per_head = [taps[:keys].reshape(key_heads, 1, P, -1), taps[keys:2 * keys].reshape(key_heads, 1, P, -1),
                taps[2 * keys:].reshape(key_heads, 2, P, -1)]
    rows = np.stack([i["L0_attn_b_dt_bias"], i["L0_attn_b_A_log"]])
    return {
        "x": i["L0_attn_a_x"],
        "cols": cols.transpose(1, 2, 0),
        "mix_rows": np.repeat(i["L0_attn_a_head_mix"], width // heads_a, axis=0).reshape(tiles, P, heads_a)
        .transpose(1, 0, 2),
        "a_in": i["L0_attn_a_in_proj_w"].T,
        "a_out": i["L0_attn_a_out_proj_w"].T,
        "ffn_gate": i["L0_ffn_w_gate"], "ffn_up": i["L0_ffn_w_up"], "ffn_down": i["L0_ffn_w_down"],
        "rows": np.broadcast_to(rows[None], (P, *rows.shape)),
        "norm_w": i["L0_attn_b_norm_weight"].reshape(P, 1),
        "w_ba": ba.transpose(1, 0, 2, 3).reshape(-1, width).T.reshape(tiles, P, -1).transpose(1, 0, 2),
        "b_qkvz": i["L0_attn_b_w_qkvz"].T,
        "b_out": i["L0_attn_b_w_out"].T,
        "taps": np.concatenate(per_head, 1).transpose(2, 0, 1, 3),
    }


def kernel(**inputs):
    import numpy as np
    import concourse.bacc as bacc
    from concourse.bass_utils import run_bass_kernel_spmd

    arrays = {**_laid_out({k: np.asarray(v) for k, v in inputs.items()}), **layer_a_tables(), **layer_b_tables()}
    arrays = {f"in_{k}": np.ascontiguousarray(v) for k, v in arrays.items()}
    nc = bacc.Bacc("TRN2", target_bir_lowering=False, num_devices=1)
    ins = {k[3:]: nc.dram_tensor(k, v.shape, mybir.dt.from_np(v.dtype), kind="ExternalInput").ap()
           for k, v in arrays.items()}
    shape = inputs["L0_attn_a_x"].shape
    out = nc.dram_tensor("out_rows", shape, F32, kind="ExternalOutput").ap()
    layer_stack(nc, ins, out)
    r = run_bass_kernel_spmd(nc, [arrays], core_ids=[0])
    return r.results[0]["out_rows"]
```

```python
from contextlib import ExitStack, contextmanager

import concourse.bass as bass
from concourse import mybir

P = 128
LN_EPS = 1e-5
F32 = mybir.dt.float32
F32R = mybir.dt.float32r
BF16 = mybir.dt.bfloat16
ALU = mybir.AluOpType
ACT = mybir.ActivationFunctionType
AX = mybir.AxisListType


@contextmanager
def cleared_semaphores(nc, prefix):
    taken = []

    def sem(name):
        taken.append(nc.alloc_semaphore(f"{prefix}_{name}"))
        return taken[-1]

    yield sem
    nc.clear_and_free_semaphores(taken)
    nc.all_engine_barrier()


def layer_a_tables():
    import numpy as np
    tokens, head = 1024, 32
    inv = (1.0 / 10000.0 ** (np.arange(0, head, 2, dtype=np.float32) / np.float32(head))).astype(np.float32)
    angle = np.arange(tokens, dtype=np.float32)[None, :] * inv[:, None]
    row = np.arange(P) % (head // 2)
    rot = np.zeros((P, P), np.float32)
    for m in range(P):
        h, e = divmod(m, head)
        if e < head // 2:
            rot[h * head + e + head // 2, m] = -1.0
        else:
            rot[h * head + e - head // 2, m] = 1.0
    within = np.ones((P, tokens), np.float32)
    within[:, ::64] = 0.0
    eye = (np.arange(P)[:, None] % head == np.arange(head)[None, :]).astype(np.float32)
    return {"ident": np.eye(P, dtype=np.float32), "rot": rot, "cos": np.cos(angle)[row], "sin": np.sin(angle)[row],
            "within": within, "eye_head": eye}


def layer_b_tables():
    import numpy as np
    r, c = np.arange(P)[:, None], np.arange(P)[None, :]
    joins = [-((r // (2 * n) == c // (2 * n)) & ((c // n) % 2 == 1) & ((r // n) % 2 == 0)).astype(np.float32)
             for n in (1, 2, 4, 8, 16, 32, 64)]
    lower = np.stack([(np.arange(P) // n) % 2 == 0 for n in (1, 2, 4, 8, 16, 32, 64)], 1).astype(np.float32)
    return {"lower": lower, "ident": np.eye(P, dtype=np.float32), "upto": (r <= c).astype(np.float32),
            "after": (r > c).astype(np.float32), "below": (r < c).astype(np.float32),
            "joins": np.ascontiguousarray(np.stack(joins, 1))}


def decay_mixer(nc, psum, consts, x_in, x_out, w):
    BATCH, N, D = x_in.shape
    KD = D // P
    SUB = N // P
    HALF = N // 2
    TAPS = 4
    CH = 64
    NCH = N // CH
    with ExitStack() as ctx:
        def sb(n, shape, dt=F32):
            return ctx.enter_context(nc.sbuf_tensor(f"a_{n}", shape, dt))

        sem = ctx.enter_context(cleared_semaphores(nc, "a"))

        ident = sb("ident", [P, P])
        rot = sb("rot", [P, P])
        cos, sin = sb("cos", [P, N]), sb("sin", [P, N])
        within = sb("within", [P, N])
        ones = sb("ones", [P, NCH])
        mhalf = sb("mhalf", [P, SUB])
        w_in = sb("w_in", [P, KD, 3 * D])
        w_out = sb("w_out", [P, KD, D])
        mix = sb("mix", [P, KD, D])
        mix_rows = sb("mix_rows", [P, KD, D // 32])
        eye_head = sb("eye_head", [P, 32])
        cols = sb("cols", [P, 3 + TAPS, KD])
        x = sb("x", [P, SUB, D])
        y = sb("y", [P, SUB, D])
        stats = sb("stats", [P, SUB, 6])
        mean2, mean, gap, gap2, var, var_eps, rstd, msq, msq_eps, rrms = (
            sb(n, [P, SUB]) for n in ("mean2", "mean", "gap", "gap2", "var", "var_eps", "rstd", "msq", "msq_eps",
                                      "rrms"))
        xnT = sb("xnT", [P, KD, TAPS - 1 + N])
        xc = sb("xc", [P, KD, N])
        gate = sb("gate", [P, KD, N])
        final = sb("final", [P, KD, N])
        arg, ex, dt, dec, decs, grow, fade, fade0, v, va, vb = (
            sb(n, [P, N]) for n in ("arg", "ex", "dt", "dec", "decs", "grow", "fade", "fade0", "v", "va", "vb"))
        cd, cdc, ncd, up, down, seeds, csum, carry = (
            sb(n, [P, NCH]) for n in ("cd", "cdc", "ncd", "up", "down", "seeds", "csum", "carry"))
        ps_dt, ps_v, ps_g, ps_p = banks = psum

        s_tab = sem("s_tab")
        s_w = sem("s_w")
        s_set = sem("s_set")
        s_mix = sem("s_mix")
        s_x = sem("s_x")
        s_ln = sem("s_ln")
        s_var = sem("s_var")
        s_rstd = sem("s_rstd")
        s_y = sem("s_y")
        s_sq = sem("s_sq")
        s_msq = sem("s_msq")
        s_rrms = sem("s_rrms")
        s_xy = sem("s_xy")
        s_yn = sem("s_yn")
        s_tr = sem("s_tr")
        s_sc = sem("s_sc")
        s_conv = sem("s_conv")
        s_tap = sem("s_tap")
        s_xc = sem("s_xc")
        s_pdt, s_pv, s_pg, s_pp = sem("s_pdt"), sem("s_pv"), sem("s_pg"), sem("s_pp")
        s_arg = sem("s_arg")
        s_ex = sem("s_ex")
        s_dt = sem("s_dt")
        s_dec = sem("s_dec")
        s_exps = sem("s_exps")
        s_v = sem("s_v")
        s_gate = sem("s_gate")
        s_va = sem("s_va")
        s_vb = sem("s_vb")
        s_cum = sem("s_cum")
        s_cd = sem("s_cd")
        s_cexp = sem("s_cexp")
        s_car = sem("s_car")
        s_fin = sem("s_fin")
        s_sig = sem("s_sig")
        s_pm = sem("s_pm")
        s_gm = sem("s_gm")
        s_po = sem("s_po")
        s_res = sem("s_res")
        s_store = sem("s_store")
        LN = SUB + 6
        CONV = TAPS

        block = ctx.enter_context(nc.Block())

        @block.sync
        def _(sp):
            xr = x_in.rearrange("b (s p) d -> b p s d", p=P)
            outr = x_out.rearrange("(b s p) d -> b p s d", p=P, b=BATCH)
            for s in range(2):
                part = slice(s * SUB // 2, (s + 1) * SUB // 2)
                sp.dma_start(x[:, part, :], xr[0, :, part, :]).then_inc(s_x, 16)
            for tile, src in ((ident, "ident"), (cols, "cols"), (within, "within"), (rot, "rot"),
                              (cos, "cos"), (sin, "sin"), (mix_rows, "mix_rows"), (eye_head, "eye_head")):
                full = tile[:, :] if len(tile.shape) == 2 else tile[:, :, :]
                sp.dma_start(full, w[src] if src in w else consts[src]).then_inc(s_tab, 16)
            sp.dma_start(w_in[:, :, :], w["a_in"].rearrange("(k p) n -> p k n", p=P)).then_inc(s_w, 16)
            sp.dma_start(w_out[:, :, :], w["a_out"].rearrange("(k p) n -> p k n", p=P)).then_inc(s_w, 16)
            for b in range(BATCH):
                for s in range(2):
                    part = slice(s * SUB // 2, (s + 1) * SUB // 2)
                    sp.wait_ge(s_res, SUB * b + (s + 1) * SUB // 2)
                    sp.dma_start(outr[b][:, part, :], x[:, part, :]).then_inc(s_store, 16)
                if b < BATCH - 1:
                    sp.wait_ge(s_store, 32 * (b + 1))
                    for s in range(2):
                        part = slice(s * SUB // 2, (s + 1) * SUB // 2)
                        sp.dma_start(x[:, part, :], xr[b + 1, :, part, :]).then_inc(s_x, 16)
            sp.wait_ge(s_store, 32 * BATCH)

        @block.gpsimd
        def _(pool):
            pool.memset(mhalf[:, :], -0.5).then_inc(s_set, 1)
            pool.memset(ones[:, :], 1.0).then_inc(s_set, 1)
            pool.memset(carry[:, 0:1], 0.0).then_inc(s_set, 1)
            pool.memset(xnT[:, :, 0:TAPS - 1], 0.0).then_inc(s_set, 1)
            pool.wait_ge(s_set, 4)
            pool.wait_ge(s_tab, 16 * 8)
            with pool.Fori(0, BATCH) as b:
                pool.wait_ge(s_var, b + 1)
                pool.tensor_tensor(rstd[:, :], var[:, :], mhalf[:, :], ALU.pow).then_inc(s_rstd, 1)
                pool.wait_ge(s_msq, b + 1)
                pool.tensor_tensor(rrms[:, :], msq_eps[:, :], mhalf[:, :], ALU.pow).then_inc(s_rrms, 1)
                for j in range(KD):
                    n = b * KD + j
                    pool.wait_ge(s_v, n + 1)
                    pool.wait_ge(s_cum, 3 * n)
                    pool.tensor_tensor(va[:, :], v[:, :], cos[:, :], ALU.mult).then_inc(s_va, 1)
                    pool.wait_ge(s_dt, n + 1)
                    pool.wait_ge(s_vb, 2 * n + 2)
                    pool.tensor_tensor(va[:, :], vb[:, :], dt[:, :], ALU.mult).then_inc(s_va, 1)

        @block.scalar
        def _(act):
            act.wait_ge(s_tab, 16 * 8)
            with act.Fori(0, BATCH) as b:
                for i in range(SUB):
                    act.wait_ge(s_y, SUB * b + i + 1)
                    act.wait_ge(s_sq, SUB * b + i)
                    act.activation(final[:, 0, 0:D], y[:, i, :], ACT.Square,
                                   accum_out=msq[:, i:i + 1]).then_inc(s_sq, 1)
                for k in range(KD):
                    act.wait_ge(s_tr, KD * b + k + 1)
                    act.activation(xnT[:, k, TAPS - 1:], banks[k][:, :], ACT.Copy,
                                   scale=cols[:, 0, k:k + 1]).then_inc(s_sc, 1)
                for k in range(KD):
                    n = b * KD + k
                    act.wait_ge(s_conv, CONV * n + 1)
                    act.activation(xc[:, k, :], xnT[:, k, 0:N], ACT.Copy, scale=cols[:, 3, k:k + 1]).then_inc(s_tap, 1)
                for k in range(KD):
                    n = b * KD + k
                    act.wait_ge(s_conv, CONV * (n + 1))
                    act.activation(xc[:, k, :], xc[:, k, :], ACT.Silu, bias=cols[:, 1, k:k + 1]).then_inc(s_xc, 1)
                for j in range(KD):
                    n = b * KD + j
                    act.wait_ge(s_arg, n + 1)
                    act.activation(ex[:, :], arg[:, :], ACT.Exp).then_inc(s_ex, 1)
                    act.wait_ge(s_ex, 2 * n + 1)
                    act.activation(ex[:, :], ex[:, :], ACT.Ln, bias=1.0).then_inc(s_ex, 1)
                    act.wait_ge(s_pv, n + 1)
                    act.wait_ge(s_va, 2 * n)
                    act.wait_ge(s_pp, n)
                    act.copy(v[:, :], ps_v[:, :]).then_inc(s_v, 1)
                    act.wait_ge(s_dec, 3 * n + 3)
                    act.activation(grow[:, :], decs[:, :], ACT.Exp, scale=-1.0).then_inc(s_exps, 1)
                    act.activation(fade0[:, :], decs[:, :], ACT.Exp).then_inc(s_exps, 1)
                    act.activation(fade[:, :], dec[:, :], ACT.Exp).then_inc(s_exps, 1)
                    act.wait_ge(s_cd, 3 * n + 3)
                    act.activation(up[:, :], ncd[:, :], ACT.Exp, scale=-1.0).then_inc(s_cexp, 1)
                    act.activation(down[:, :], ncd[:, :], ACT.Exp).then_inc(s_cexp, 1)
                    act.wait_ge(s_pg, n + 1)
                    act.wait_ge(s_po, SUB * b)
                    act.copy(gate[:, j, :], ps_g[:, :]).then_inc(s_gate, 1)
                act.wait_ge(s_gate, KD * (b + 1))
                for j in range(KD):
                    act.activation(gate[:, j, :], gate[:, j, :], ACT.Sigmoid).then_inc(s_sig, 1)

        @block.vector
        def _(dve):
            dve.wait_ge(s_tab, 16 * 8)
            dve.wait_ge(s_set, 4)
            for k in range(KD):
                dve.tensor_tensor(mix[:, k, :].rearrange("p (m e) -> p m e", e=32),
                                  mix_rows[:, k, :].rearrange("p (m e) -> p m e", e=1).to_broadcast([P, D // 32, 32]),
                                  eye_head[:, :].rearrange("p (m e) -> p m e", m=1).to_broadcast([P, D // 32, 32]),
                                  ALU.mult).then_inc(s_mix, 1)
            with dve.Fori(0, BATCH) as b:
                dve.wait_ge(s_x, 32 * (b + 1))
                for i in range(SUB):
                    dve.bn_stats(stats[:, i, :], x[:, i, :]).then_inc(s_ln, 1)
                c = LN * b + SUB
                dve.wait_ge(s_ln, c)
                dve.tensor_tensor(mean2[:, :], stats[:, :, 1], stats[:, :, 4], ALU.add).then_inc(s_ln, 1)
                dve.tensor_tensor(gap[:, :], stats[:, :, 1], stats[:, :, 4], ALU.subtract).then_inc(s_ln, 1)
                dve.tensor_tensor(var[:, :], stats[:, :, 2], stats[:, :, 5], ALU.add).then_inc(s_ln, 1)
                dve.wait_ge(s_ln, c + 3)
                dve.tensor_scalar(mean[:, :], mean2[:, :], 0.5, None, ALU.mult).then_inc(s_ln, 1)
                dve.scalar_tensor_tensor(gap2[:, :], gap[:, :], 0.25, gap[:, :], ALU.mult, ALU.mult).then_inc(s_ln, 1)
                dve.tensor_scalar(var_eps[:, :], var[:, :], 1.0 / D, LN_EPS, ALU.mult, ALU.add).then_inc(s_ln, 1)
                dve.wait_ge(s_ln, c + 6)
                dve.tensor_tensor(var[:, :], var_eps[:, :], gap2[:, :], ALU.add).then_inc(s_var, 1)
                dve.wait_ge(s_tr, KD * b)
                dve.wait_ge(s_rstd, b + 1)
                for i in range(SUB):
                    dve.tensor_scalar(y[:, i, :], x[:, i, :], mean[:, i:i + 1], rstd[:, i:i + 1],
                                      ALU.subtract, ALU.mult).then_inc(s_y, 1)
                dve.wait_ge(s_y, SUB * (b + 1))
                for i in range(SUB):
                    dve.tensor_tensor(x[:, i, :], x[:, i, :], y[:, i, :], ALU.add).then_inc(s_xy, 1)
                dve.wait_ge(s_sq, SUB * (b + 1))
                dve.tensor_scalar(msq_eps[:, :], msq[:, :], 1.0 / D, 1e-6, ALU.mult, ALU.add).then_inc(s_msq, 1)
                dve.wait_ge(s_xy, SUB * (b + 1))
                dve.wait_ge(s_rrms, b + 1)
                for i in range(SUB):
                    dve.tensor_scalar(y[:, i, :], y[:, i, :], rrms[:, i:i + 1], None, ALU.mult).then_inc(s_yn, 1)
                for k in range(KD):
                    n = b * KD + k
                    xk = xnT[:, k, TAPS - 1:]
                    dve.wait_ge(s_sc, n + 1)
                    dve.tensor_scalar(xk, xk, -60000.0, 60000.0, ALU.max, ALU.min).then_inc(s_conv, 1)
                    dve.wait_ge(s_tap, n + 1)
                    for tap in range(1, TAPS):
                        dve.wait_ge(s_conv, CONV * n + tap)
                        dve.scalar_tensor_tensor(xc[:, k, :], xnT[:, k, tap:tap + N], cols[:, 3 + tap, k:k + 1],
                                                 xc[:, k, :], ALU.mult, ALU.add).then_inc(s_conv, 1)
                for j in range(KD):
                    n = b * KD + j
                    dve.wait_ge(s_pdt, n + 1)
                    dve.tensor_scalar(arg[:, :], ps_dt[:, :], cols[:, 2, j:j + 1], 20.0,
                                      ALU.add, ALU.min).then_inc(s_arg, 1)
                    dve.wait_ge(s_ex, 2 * n + 2)
                    dve.wait_ge(s_va, 2 * n)
                    dve.tensor_scalar(dt[:, :], ex[:, :], 0.001, 2.0, ALU.max, ALU.min).then_inc(s_dt, 1)
                    dve.wait_ge(s_dt, n + 1)
                    dve.tensor_tensor_scan(decs[:, :], within[:, :], dt[:, :], 0.0,
                                           ALU.mult, ALU.subtract).then_inc(s_dec, 1)
                    dve.wait_ge(s_dec, 3 * n + 1)
                    dve.tensor_scalar(dec[:, :], decs[:, :], -20.0, 0.0, ALU.max, ALU.min).then_inc(s_dec, 1)
                    dve.wait_ge(s_dec, 3 * n + 2)
                    dch = dec[:, :].rearrange("p (c t) -> p c t", t=CH)
                    dve.tensor_tensor(decs[:, :].rearrange("p (c t) -> p c t", t=CH), dch,
                                      dch[:, :, 0:1].to_broadcast([P, NCH, CH]), ALU.subtract).then_inc(s_dec, 1)
                    dve.tensor_tensor_scan(cd[:, :], ones[:, :], dec[:, CH - 1:N:CH], 0.0,
                                           ALU.mult, ALU.add).then_inc(s_cd, 1)
                    dve.wait_ge(s_cd, 3 * n + 1)
                    dve.tensor_scalar(cdc[:, :], cd[:, :], -80.0, 0.0, ALU.max, ALU.min).then_inc(s_cd, 1)
                    dve.wait_ge(s_cd, 3 * n + 2)
                    dve.tensor_scalar(ncd[:, :], cdc[:, :], cdc[:, 0:1], -20.0,
                                      ALU.subtract, ALU.max).then_inc(s_cd, 1)
                    dve.wait_ge(s_pp, n + 1)
                    dve.tensor_tensor(vb[:, :], ps_p[:, :], sin[:, :], ALU.mult).then_inc(s_vb, 1)
                    dve.wait_ge(s_vb, 2 * n + 1)
                    dve.wait_ge(s_va, 2 * n + 1)
                    dve.tensor_tensor(vb[:, :], vb[:, :], va[:, :], ALU.add).then_inc(s_vb, 1)
                    dve.wait_ge(s_exps, 3 * n + 3)
                    dve.wait_ge(s_va, 2 * n + 2)
                    dve.tensor_tensor(vb[:, :], grow[:, :], va[:, :], ALU.mult).then_inc(s_cum, 1)
                    dve.wait_ge(s_cum, 3 * n + 1)
                    dve.tensor_tensor_scan(grow[:, :], within[:, :], vb[:, :], 0.0, ALU.mult, ALU.add).then_inc(s_cum, 1)
                    dve.wait_ge(s_cum, 3 * n + 2)
                    dve.tensor_tensor(final[:, j, :], fade0[:, :], grow[:, :], ALU.mult).then_inc(s_cum, 1)
                    dve.wait_ge(s_cum, 3 * n + 3)
                    dve.wait_ge(s_cexp, 2 * n + 2)
                    dve.tensor_tensor(seeds[:, :], final[:, j, CH - 1:N:CH], up[:, :], ALU.mult).then_inc(s_car, 1)
                    dve.wait_ge(s_car, 3 * n + 1)
                    dve.tensor_tensor_scan(csum[:, :], ones[:, :], seeds[:, :], 0.0, ALU.mult, ALU.add).then_inc(s_car, 1)
                    dve.wait_ge(s_car, 3 * n + 2)
                    dve.tensor_tensor(carry[:, 1:], csum[:, :NCH - 1], down[:, 1:], ALU.mult).then_inc(s_car, 1)
                    dve.wait_ge(s_car, 3 * n + 3)
                    dve.tensor_tensor(vb[:, :].rearrange("p (c t) -> p c t", t=CH),
                                      fade[:, :].rearrange("p (c t) -> p c t", t=CH),
                                      carry[:, :].rearrange("p (c t) -> p c t", t=1).to_broadcast([P, NCH, CH]),
                                      ALU.mult).then_inc(s_fin, 1)
                    dve.wait_ge(s_fin, 2 * n + 1)
                    dve.tensor_tensor(final[:, j, :], final[:, j, :], vb[:, :], ALU.add).then_inc(s_fin, 1)
                    dve.wait_ge(s_fin, 2 * n + 2)
                for m in range(KD):
                    dve.wait_ge(s_sig, KD * b + m + 1)
                    dve.wait_ge(s_pm, KD * b + m + 1)
                    dve.tensor_tensor(gate[:, m, :], banks[m][:, :], gate[:, m, :], ALU.mult).then_inc(s_gm, 1)
                for i in range(SUB):
                    dve.wait_ge(s_po, SUB * b + i + 1)
                    bank = banks[i // 2][:, (i % 2) * HALF:(i % 2 + 1) * HALF]
                    dve.tensor_tensor(x[:, i, :], x[:, i, :], bank, ALU.add).then_inc(s_res, 1)
                dve.wait_ge(s_res, SUB * (b + 1))

        @block.tensor
        def _(pe):
            halves = [slice(0, HALF), slice(HALF, N)]

            def project(bank, group, j, done):
                for hs in halves:
                    for k in range(KD):
                        mm = pe.matmul(bank[:, hs], w_in[:, k, group * D + j * P:group * D + (j + 1) * P],
                                       xc[:, k, hs], start=(k == 0), stop=(k == KD - 1))
                mm.then_inc(done, 1)

            pe.wait_ge(s_tab, 16 * 8)
            pe.wait_ge(s_w, 32)
            pe.wait_ge(s_mix, KD)
            with pe.Fori(0, BATCH) as b:
                pe.wait_ge(s_res, SUB * b)
                pe.wait_ge(s_yn, SUB * (b + 1))
                for k in range(KD):
                    for i in range(SUB):
                        mm = pe.transpose(banks[k][:, i * P:(i + 1) * P], y[:, i, k * P:(k + 1) * P], ident[:, :])
                    mm.then_inc(s_tr, 1)
                pe.wait_ge(s_xc, KD * (b + 1))
                for j in range(KD):
                    n = b * KD + j
                    pe.wait_ge(s_arg, n)
                    project(ps_dt, 0, j, s_pdt)
                    pe.wait_ge(s_v, n)
                    project(ps_v, 1, j, s_pv)
                    pe.wait_ge(s_gate, n)
                    project(ps_g, 2, j, s_pg)
                    pe.wait_ge(s_v, n + 1)
                    pe.wait_ge(s_vb, 2 * n)
                    for hs in halves:
                        mm = pe.matmul(ps_p[:, hs], rot[:, :], v[:, hs], start=True, stop=True)
                    mm.then_inc(s_pp, 1)
                pe.wait_ge(s_gate, KD * (b + 1))
                pe.wait_ge(s_fin, 2 * KD * (b + 1))
                for m in range(KD):
                    for hs in halves:
                        for k in range(KD):
                            mm = pe.matmul(banks[m][:, hs], mix[:, k, m * P:(m + 1) * P], final[:, k, hs],
                                           start=(k == 0), stop=(k == KD - 1))
                    mm.then_inc(s_pm, 1)
                pe.wait_ge(s_gm, KD * (b + 1))
                for i in range(SUB):
                    bank = banks[i // 2][:, (i % 2) * HALF:(i % 2 + 1) * HALF]
                    for k in range(KD):
                        mm = pe.matmul(bank, gate[:, k, i * P:(i + 1) * P], w_out[:, k, :],
                                       start=(k == 0), stop=(k == KD - 1))
                    mm.then_inc(s_po, 1)


def feed_forward(nc, psum, name, consts, x_in, x_out, w_gate, w_up, w_down):
    ROWS, D = x_in.shape
    HID = w_gate.shape[1]
    KD = D // P
    TT = 512
    SUB = TT // P
    TILES = ROWS // TT
    R = 4
    BLK = HID // (P * R)
    with ExitStack() as ctx:
        def sb(n, shape, dt=F32):
            return ctx.enter_context(nc.sbuf_tensor(f"{name}_{n}", shape, dt))

        sem = ctx.enter_context(cleared_semaphores(nc, name))

        ident = sb("ident", [P, P])
        mhalf = sb("mhalf", [P, SUB])
        wg = sb("wg", [P, KD, HID])
        wu = sb("wu", [P, KD, HID])
        wd = sb("wd", [P, BLK, R, D])
        x_tok = sb("x_tok", [P, SUB, D])
        x_res = sb("x_res", [P, SUB, D])
        xn = sb("xn", [P, SUB, D])
        xT = sb("xT", [P, KD, TT])
        stats = sb("stats", [P, SUB, 6])
        mean2, mean, gap, gap2, var, var_eps = (
            sb(n, [P, SUB]) for n in ("mean2", "mean", "gap", "gap2", "var", "var_eps"))
        rstd = sb("rstd", [P, SUB])
        silu = sb("silu", [P, 2, TT])
        h = sb("h", [P, R, TT])
        mag = sb("mag", [P, R, TT])
        wins = sb("wins", [P, 6, TT], BF16)
        score = sb("score", [P, R, TT], BF16)
        kept = sb("kept", [P, 2, R, TT])
        gate_ps, up_ps, *out_ps = (t[:, :].rearrange("p (r t) -> p r t", t=TT) for t in psum)

        s_const = sem("s_const")
        s_wup = sem("s_wup")
        s_wdown = sem("s_wdown")
        s_x = sem("s_x")
        s_res = sem("s_res")
        s_var = sem("s_var")
        s_half = sem("s_half")
        s_rstd = sem("s_rstd")
        s_ln = sem("s_ln")
        s_xn = sem("s_xn")
        s_tr = sem("s_tr")
        s_xT = sem("s_xT")
        s_gate = sem("s_gate")
        s_up = sem("s_up")
        s_silu = sem("s_silu")
        s_h = sem("s_h")
        s_mag = sem("s_mag")
        s_cmp = sem("s_cmp")
        s_kept = sem("s_kept")
        s_down = sem("s_down")
        s_sum = sem("s_sum")
        s_store = sem("s_store")
        CMP = 9
        LN = SUB + 6

        block = ctx.enter_context(nc.Block())

        def rows(ap, t):
            return ap.rearrange("(t s p) d -> t p s d", p=P, s=SUB)[t]

        @block.sync
        def _(sp):
            sp.dma_start(ident[:, :], consts["ident"]).then_inc(s_const, 16)
            sp.dma_start(x_tok[:, :, :], rows(x_in, 0)).then_inc(s_x, 16)
            for k in range(KD):
                sp.dma_start(wg[:, k, :], w_gate[k * P:(k + 1) * P, :]).then_inc(s_wup, 16)
                sp.dma_start(wu[:, k, :], w_up[k * P:(k + 1) * P, :]).then_inc(s_wup, 16)
            sp.dma_start(wd[:, :, :, :],
                         w_down.rearrange("(b g r) n -> g b (r n)", g=P, r=R)).then_inc(s_wdown, 16)

            def load_next(t):
                sp.wait_ge(s_xn, SUB * (t + 1))
                sp.dma_start(x_tok[:, :, :], x_in_t[t + 1]).then_inc(s_x, 16)

            def finish(t):
                sp.dma_start(x_res[:, :, :], x_in_t[t]).then_inc(s_res, 16)
                sp.wait_ge(s_sum, SUB * (t + 1))
                sp.dma_start(x_out_t[t], x_res[:, :, :]).then_inc(s_store, 16)
                sp.wait_ge(s_store, 16 * (t + 1))

            x_in_t = x_in.rearrange("(t s p) d -> t p s d", p=P, s=SUB)
            x_out_t = x_out.rearrange("(t s p) d -> t p s d", p=P, s=SUB)
            for t in range(TILES):
                if t < TILES - 1:
                    load_next(t)
                finish(t)

        @block.gpsimd
        def _(pool):
            pool.memset(mhalf[:, :], -0.5).then_inc(s_half, 1)
            pool.wait_ge(s_half, 1)

            def rstd_of(t):
                pool.wait_ge(s_var, t + 1)
                pool.tensor_tensor(rstd[:, :], var[:, :], mhalf[:, :], ALU.pow).then_inc(s_rstd, 1)

            rstd_of(0)
            with pool.Fori(0, TILES - 1) as t:
                rstd_of(t + 1)

        @block.scalar
        def _(act):
            def to_xT(t):
                for k in range(KD):
                    act.wait_ge(s_tr, KD * t + k + 1)
                    bank = (gate_ps if k < 2 else up_ps)[:, k % 2, :]
                    act.copy(xT[:, k, :], bank).then_inc(s_xT, 1)

            def magnitude(s, r):
                act.wait_ge(s_h, R * s + r + 1)
                if r == 0:
                    act.wait_ge(s_cmp, CMP * s)
                act.activation(mag[:, r, :], h[:, r, :], ACT.Abs).then_inc(s_mag, 1)

            def tile(t, more):
                for b in range(BLK):
                    s = t * BLK + b
                    for r in range(R):
                        n = R * s + r
                        act.wait_ge(s_gate, n + 1)
                        if r >= 2:
                            act.wait_ge(s_h, n - 1)
                        act.activation(silu[:, r % 2, :], gate_ps[:, r % 2, :], ACT.Silu).then_inc(s_silu, 1)
                        if r >= 1:
                            magnitude(s, r - 1)
                    magnitude(s, R - 1)
                if more:
                    to_xT(t + 1)

            to_xT(0)
            with act.Fori(0, TILES - 1) as t:
                tile(t, True)
            tile(TILES - 1, False)

        @block.vector
        def _(dve):
            def layer_norm(t):
                dve.wait_ge(s_x, 16 * (t + 1))
                for i in range(SUB):
                    dve.bn_stats(stats[:, i, :], x_tok[:, i, :]).then_inc(s_ln, 1)
                c = LN * t + SUB
                dve.wait_ge(s_ln, c)
                dve.tensor_tensor(mean2[:, :], stats[:, :, 1], stats[:, :, 4], ALU.add).then_inc(s_ln, 1)
                dve.tensor_tensor(gap[:, :], stats[:, :, 1], stats[:, :, 4], ALU.subtract).then_inc(s_ln, 1)
                dve.tensor_tensor(var[:, :], stats[:, :, 2], stats[:, :, 5], ALU.add).then_inc(s_ln, 1)
                dve.wait_ge(s_ln, c + 3)
                dve.tensor_scalar(mean[:, :], mean2[:, :], 0.5, None, ALU.mult).then_inc(s_ln, 1)
                dve.scalar_tensor_tensor(gap2[:, :], gap[:, :], 0.25, gap[:, :], ALU.mult, ALU.mult).then_inc(s_ln, 1)
                dve.tensor_scalar(var_eps[:, :], var[:, :], 1.0 / D, LN_EPS, ALU.mult, ALU.add).then_inc(s_ln, 1)
                dve.wait_ge(s_ln, c + 6)
                dve.tensor_tensor(var[:, :], var_eps[:, :], gap2[:, :], ALU.add).then_inc(s_var, 1)
                dve.wait_ge(s_rstd, t + 1)
                for i in range(SUB):
                    if i == 0:
                        dve.wait_ge(s_tr, KD * t)
                    dve.tensor_scalar(xn[:, i, :], x_tok[:, i, :], mean[:, i:i + 1], rstd[:, i:i + 1],
                                      ALU.subtract, ALU.mult).then_inc(s_xn, 1)

            def prune(s, b):
                c = CMP * s
                dve.wait_ge(s_kept, R * s)
                for r in range(R):
                    dve.wait_ge(s_silu, R * s + r + 1)
                    dve.wait_ge(s_up, R * s + r + 1)
                    dve.tensor_tensor(h[:, r, :], up_ps[:, r % 2, :], silu[:, r % 2, :], ALU.mult).then_inc(s_h, 1)
                dve.wait_ge(s_mag, R * (s + 1))
                dve.tensor_tensor(wins[:, 0:4:3, :], mag[:, 0:4:2, :], mag[:, 1:4:2, :], ALU.is_ge).then_inc(s_cmp, 1)
                dve.tensor_tensor(wins[:, 1:3, :], mag[:, 0:2, :], mag[:, 2:4, :], ALU.is_ge).then_inc(s_cmp, 1)
                dve.tensor_tensor(wins[:, 4, :], mag[:, 0, :], mag[:, 3, :], ALU.is_ge).then_inc(s_cmp, 1)
                dve.tensor_tensor(wins[:, 5, :], mag[:, 1, :], mag[:, 2, :], ALU.is_ge).then_inc(s_cmp, 1)
                dve.wait_ge(s_cmp, c + 2)
                dve.tensor_tensor(score[:, 0:4:3, :], wins[:, 0:4:3, :], wins[:, 1:3, :], ALU.add).then_inc(s_cmp, 1)
                dve.tensor_tensor(score[:, 1:3, :], wins[:, 2:4, :], wins[:, 0:2, :], ALU.subtract).then_inc(s_cmp, 1)
                dve.wait_ge(s_cmp, c + 6)
                dve.tensor_tensor(score[:, 0:4:3, :], score[:, 0:4:3, :],
                                  wins[:, 4:5, :].to_broadcast([P, 2, TT]), ALU.add).then_inc(s_cmp, 1)
                dve.tensor_tensor(score[:, 1, :], score[:, 1, :], wins[:, 5, :], ALU.add).then_inc(s_cmp, 1)
                dve.tensor_tensor(score[:, 2, :], score[:, 2, :], wins[:, 5, :], ALU.subtract).then_inc(s_cmp, 1)
                dve.wait_ge(s_cmp, c + CMP)
                if b >= 2:
                    dve.wait_ge(s_down, s - 1)
                for r, (least, op) in enumerate(((2.0, ALU.is_ge), (1.0, ALU.is_ge), (0.0, ALU.is_ge), (1.0, ALU.is_le))):
                    dve.scalar_tensor_tensor(kept[:, b % 2, r, :], score[:, r, :], least, h[:, r, :],
                                             op, ALU.mult).then_inc(s_kept, 1)

            def tile(t, more):
                for b in range(BLK):
                    prune(t * BLK + b, b)
                    if b == 1 and more:
                        layer_norm(t + 1)
                dve.wait_ge(s_res, 16 * (t + 1))
                dve.wait_ge(s_down, BLK * (t + 1))
                for i in range(SUB):
                    dve.tensor_tensor(x_res[:, i, :], x_res[:, i, :], out_ps[i // 2][:, i % 2, :], ALU.add).then_inc(s_sum, 1)

            layer_norm(0)
            with dve.Fori(0, TILES - 1) as t:
                tile(t, True)
            tile(TILES - 1, False)

        @block.tensor
        def _(pe):
            def transposes(t):
                for i in range(SUB):
                    pe.wait_ge(s_xn, SUB * t + i + 1)
                for k in range(KD):
                    bank = (gate_ps if k < 2 else up_ps)[:, k % 2, :]
                    for i in range(SUB):
                        mm = pe.transpose(bank[:, i * P:(i + 1) * P], xn[:, i, k * P:(k + 1) * P], ident[:, :])
                    mm.then_inc(s_tr, 1)

            def products_up(s, b):
                for r in range(R):
                    n = R * s + r
                    lo = b * P * R + r
                    if b > 0 or r >= 2:
                        pe.wait_ge(s_silu, n - 1)
                    for k in range(KD):
                        mm = pe.matmul(gate_ps[:, r % 2, :], wg[:, k, lo:lo + (P - 1) * R + 1:R], xT[:, k, :],
                                       start=(k == 0), stop=(k == KD - 1))
                    mm.then_inc(s_gate, 1)
                    if b > 0 or r >= 2:
                        pe.wait_ge(s_h, n - 1)
                    for k in range(KD):
                        mm = pe.matmul(up_ps[:, r % 2, :], wu[:, k, lo:lo + (P - 1) * R + 1:R], xT[:, k, :],
                                       start=(k == 0), stop=(k == KD - 1))
                    mm.then_inc(s_up, 1)

            def products_down(t, s, b):
                pe.wait_ge(s_kept, R * (s + 1))
                if b == 0:
                    pe.wait_ge(s_sum, SUB * t)
                for i in range(SUB):
                    for r in range(R):
                        mm = pe.matmul(out_ps[i // 2][:, i % 2, :], kept[:, b % 2, r, i * P:(i + 1) * P], wd[:, b, r, :],
                                       start=(b == 0 and r == 0), stop=(b == BLK - 1 and r == R - 1))
                mm.then_inc(s_down, 1)

            def tile(t, more):
                pe.wait_ge(s_xT, KD * (t + 1))
                for b in range(BLK):
                    products_up(t * BLK + b, b)
                    if b > 0:
                        products_down(t, t * BLK + b - 1, b - 1)
                if more:
                    pe.wait_ge(s_silu, R * BLK * (t + 1))
                    pe.wait_ge(s_h, R * BLK * (t + 1))
                    transposes(t + 1)
                products_down(t, (t + 1) * BLK - 1, BLK - 1)
            pe.wait_ge(s_const, 16)
            transposes(0)
            pe.wait_ge(s_wup, 32 * KD)
            pe.wait_ge(s_wdown, 16)
            with pe.Fori(0, TILES - 1) as t:
                tile(t, True)
            tile(TILES - 1, False)


def delta_mixer(nc, psum, consts, x_in, x_out, w):
    ROWS, D = x_in.shape
    BATCH = 2
    KD = D // P
    SUBS = ROWS // P
    CHUNKS = SUBS // BATCH
    KH = 8
    VH = 16
    PAIRS = CHUNKS // 2
    U = 4
    TAPS = 4
    HALO = TAPS - 1
    QK = 6 * P
    LEVELS = (1, 2, 4, 8, 16, 32, 64)
    LV = len(LEVELS) - 1
    TN = 1 + 2 * LV
    GROUPS = 4
    GS = SUBS // GROUPS
    SCALE = float(P) ** -0.5
    G_MIN = -104.0
    with ExitStack() as ctx:
        def sb(n, shape, dt=F32):
            return ctx.enter_context(nc.sbuf_tensor(f"b_{n}", shape, dt))

        sem = ctx.enter_context(cleared_semaphores(nc, "b"))

        ident = sb("ident", [P, P])
        upto = sb("upto", [P, P])
        after = sb("after", [P, P])
        below = sb("below", [P, P])
        full = sb("full", [P, P])
        joins = sb("joins", [P, len(LEVELS), P])
        lower = sb("lower", [P, len(LEVELS)])
        mhalf = sb("mhalf", [P, U])
        rows = sb("rows", [P, 2, VH])
        norm_w = sb("norm_w", [P, 1])
        w_ba = sb("w_ba", [P, KD, 2 * VH])
        acc = sb("acc", [P, SUBS, D])
        xT = sb("xT", [P, KD, BATCH, CHUNKS * P])
        tab = sb("tab", [P, 5, BATCH, CHUNKS, VH])
        w_load = sb("w_load", [P, KD, QK])
        w_cur = sb("w_cur", [P, KD, QK])
        o_cur = sb("o_cur", [P, 2, D])
        taps_all = sb("taps_all", [P, KH, 4, TAPS])
        taps = sb("taps", [P, 4, TAPS])
        state = sb("state", [P, U, P])
        stats = sb("stats", [P, SUBS, 6])
        mean2, mean, gap, gap2, var, var_eps, rstd, mhalf16 = (
            sb(n, [P, SUBS]) for n in ("mean2", "mean", "gap", "gap2", "var", "var_eps", "rstd", "mhalf16"))
        raw = sb("raw", [P, 4, BATCH, HALO + P])
        bank = [t[:, lo:lo + U * P].rearrange("p (u t) -> p u t", t=P) for t in psum for lo in (0, U * P)]

        class Flight:
            def __init__(self, g):
                self.i = g
                self.wide, self.left, self.right = bank[2 + 3 * g:5 + 3 * g]

                def buf(n, shape=(P, U, P)):
                    return sb(f"{n}{g}", list(shape))

                self.x_cur = buf("x_cur", (P, KD, BATCH, P))
                self.conv, self.qkv = buf("conv", (P, 4, BATCH, P)), buf("qkv", (P, 4, BATCH, P))
                self.z_raw, self.z_act, self.sq = buf("z_raw"), buf("z_act"), buf("sq", (P, 2, BATCH, P))
                self.cur, self.g = buf("cur", (P, 5, U)), buf("g", (P, U))
                self.ss, self.rr, self.brk, self.cc, self.ngr, self.bng, self.rqs, self.ssq, self.ssq_eps, self.rn = (
                    buf(n, (P, U)) for n in ("ss", "rr", "brk", "cc", "ngr", "bng", "rqs", "ssq", "ssq_eps", "rn"))
                self.gU, self.em, self.em_s, self.em_i = buf("gU"), buf("em"), buf("em_s"), buf("em_i")
                self.k_tok, self.v_tok = buf("k_tok", (P, BATCH, P)), buf("v_tok")
                self.kb, self.kbT, self.At, self.Pt = (buf(n) for n in ("kb", "kbT", "At", "Pt"))
                self.Aj = buf("Aj", (P, 2, U, P))
                self.T, self.Tt = buf("T"), buf("Tt")
                self.X, self.qs = self.em, self.T
                self.rhs = buf("rhs")
                self.d, self.d_end, self.xf, self.xn, self.xnT = self.kb, self.kbT, self.rhs, self.em_s, self.em_i
                self.o = self.sq[:, :, :, :].rearrange("p a b t -> p (a b) t")
                self.s = {n: sem(f"{n}{g}") for n in (
                    "g", "cur", "silu", "zact", "sq", "ss", "sse", "rr", "scal", "gU", "dt", "em", "emm",
                    "ktok", "vtok", "ktoks", "vtoks", "kqs", "qss", "kb", "kbt", "kbT", "at", "atm", "joined", "T0",
                    "T", "Tps", "px", "X", "py", "rhs", "pd", "d", "pod", "dend", "ps", "o", "xf", "sqs",
                    "sse2", "rn", "xn", "txn", "xnT", "po", "acc")}

        flights = A, B = Flight(0), Flight(1)

        def flat(b):
            return b[:, :, :].rearrange("p u t -> p (u t)")

        HP = P // 2

        def half(t, level, second):
            return t[:, :, :].rearrange("p u (k s n) -> p (u k) s n", s=2, n=LEVELS[level])[:, :, second, :]

        def half_of(t, u, level, second):
            return t[:, u, :].rearrange("p (k s n) -> p k s n", s=2, n=LEVELS[level])[:, :, second, :]

        def packed(b, level, u=None):
            part = flat(b)[:, 0:U * HP] if u is None else flat(b)[:, u * HP:(u + 1) * HP]
            return part.rearrange("p (a n) -> p a n", n=LEVELS[level])

        y = w_cur[:, :, :].rearrange("p k n -> p (k n)")[:, 0:GS * D].rearrange("p (s d) -> p s d", d=D)
        sp_x, sp_abs, sp_e, sp_w, sp_l, sp_r = (
            f.qkv[:, i, :, :].rearrange("p b t -> p (b t)").rearrange("p (s v) -> p s v", v=VH)
            for f in flights for i in range(3))
        ba = flat(bank[4]).rearrange("p (s n) -> p s n", n=2 * VH)

        s = {n: sem(n) for n in (
            "const", "set", "ln", "var", "rstd", "y", "trx", "xT", "ba", "soft", "sums", "tab", "chain", "gate", "dve_gate",
            "w", "ow", "wcp", "zero", "taps",
            "xcur", "pqk", "pv", "pz", "raw", "halo", "tap", "conv", "zraw", "S", "store")}
        s_x = [sem(f"x{g}") for g in range(GROUPS)]

        block = ctx.enter_context(nc.Block())

        @block.sync
        def _(sp):
            xr = x_in.rearrange("(s p) d -> p s d", p=P)
            for g in range(GROUPS):
                part = slice(g * GS, (g + 1) * GS)
                sp.dma_start(acc[:, part, :], xr[:, part, :]).then_inc(s_x[g], 16)
            for tile, src in ((ident, "ident"), (upto, "upto"), (after, "after"), (below, "below"),
                              (joins, "joins"), (lower, "lower"), (rows, "rows"), (norm_w, "norm_w"), (w_ba, "w_ba"),
                              (taps_all, "taps")):
                sp.dma_start(tile[:], w[src] if src in w else consts[src]).then_inc(s["const"], 16)
            for h in range(KH):
                if h > 0:
                    sp.wait_ge(s["wcp"], h)
                sp.dma_start(w_load[:, :, :], w["b_qkvz"].rearrange("(k p) n -> p k n", p=P)
                             [:, :, h * QK:(h + 1) * QK]).then_inc(s["w"], 16)
                if h > 0:
                    for f in flights:
                        sp.wait_ge(f.s["po"], 2 * h * PAIRS)
                sp.dma_start(o_cur[:, :, :], w["b_out"].rearrange("(h i p) n -> h p i n", p=P, i=2)[h]
                             ).then_inc(s["ow"], 16)
            outr = x_out.rearrange("(s p) d -> p s d", p=P)
            for f in flights:
                sp.wait_ge(f.s["acc"], 2 * KH * PAIRS)
            sp.dma_start(outr, acc[:, :, :]).then_inc(s["store"], 16)
            sp.wait_ge(s["store"], 16)

        @block.gpsimd
        def _(pool):
            pool.memset(mhalf[:, :], -0.5).then_inc(s["set"], 1)
            pool.memset(mhalf16[:, :], -0.5).then_inc(s["set"], 1)
            pool.memset(full[:, :], 1.0).then_inc(s["set"], 1)
            pool.wait_ge(s["const"], 16 * 10)
            pool.wait_ge(s["set"], 3)
            pool.wait_ge(s["var"], 1)
            pool.tensor_tensor(rstd[:, :], var[:, :], mhalf16[:, :], ALU.pow).then_inc(s["rstd"], 1)
            pool.wait_ge(s["xT"], GROUPS * KD)

            def chunk_of_x(f, c, before):
                pool.wait_ge(s["pz"], before)
                pool.sem_inc(s["gate"], 1)
                pool.tensor_copy(f.x_cur[:, :, :, :], xT[:, :, :, bass.ds(c * P, P)]).then_inc(s["xcur"], 1)

            def masked_decay(f, m, out, mask):
                pool.wait_ge(f.s["em"], m + 1)
                pool.wait_ge(f.s["txn"], m)
                pool.wait_ge(f.s["po"], 2 * m)
                pool.tensor_tensor(out[:, :, :], f.em[:, :, :],
                                   mask[:, :].rearrange("p (u t) -> p u t", u=1).to_broadcast([P, U, P]),
                                   ALU.mult).then_inc(f.s["emm"], 1)

            def rsqrt_of_keys(f, m):
                pool.wait_ge(f.s["sse"], m + 1)
                pool.wait_ge(f.s["xf"], U * m)
                pool.tensor_tensor(f.rr[:, :], f.ss[:, :], mhalf[:, :], ALU.pow).then_inc(f.s["rr"], 1)

            def join(f, m, i):
                if i == 1:
                    pool.wait_ge(f.s["atm"], 2 * m + 1)
                    pool.wait_ge(f.s["py"], LV * m)
                elif i == 2:
                    pool.wait_ge(f.s["T"], TN * m + 2)
                else:
                    pool.wait_ge(f.s["px"], LV * m + i - 2)
                pool.tensor_tensor(f.Aj[:, i % 2, :, :], f.At[:, :, :],
                                   joins[:, i:i + 1, :].to_broadcast([P, U, P]), ALU.mult).then_inc(f.s["joined"], 1)

            def rsqrt_of_output(f, m):
                pool.wait_ge(f.s["sse2"], m + 1)
                pool.tensor_tensor(f.rn[:, :], f.ssq_eps[:, :], mhalf[:, :], ALU.pow).then_inc(f.s["rn"], 1)

            def pair(h, mm, first=False, start=False, turn=False, last=False):
                m, c = h * PAIRS + mm, 2 * mm
                if start:
                    cleared_state(h)
                if not last:
                    chunk_of_x(A, 0 if turn else c + 2, 2 * m + 1)
                masked_decay(A, m, A.em_s, below)
                rsqrt_of_keys(A, m)
                if not first:
                    rsqrt_of_output(B, m - 1)
                masked_decay(A, m, A.em_i, upto)
                join(A, m, 1)
                masked_decay(B, m, B.em_s, below)
                rsqrt_of_keys(B, m)
                masked_decay(B, m, B.em_i, upto)
                join(A, m, 2)
                join(B, m, 1)
                for i in range(3, len(LEVELS) + 1):
                    if i < len(LEVELS):
                        join(A, m, i)
                    join(B, m, i - 1)
                    if i == 4 and not last:
                        chunk_of_x(B, 1 if turn else c + 3, 2 * m + 2)
                rsqrt_of_output(A, m)

            def cleared_state(h):
                pool.wait_ge(s["S"], U * h * CHUNKS)
                pool.sem_inc(s["gate"], 1)
                pool.memset(state[:, :, :], 0.0).then_inc(s["zero"], 1)

            pool.memset(state[:, :, :], 0.0).then_inc(s["zero"], 1)
            for f in flights:
                chunk_of_x(f, f.i, 0)
            pair(0, 0, first=True)
            with pool.Fori(0, KH - 1) as h:
                with pool.Fori(1, PAIRS - 1) as mm:
                    pair(h, mm)
                pair(h, PAIRS - 1, turn=True)
                pair(h + 1, 0, start=True)
            with pool.Fori(1, PAIRS - 1) as mm:
                pair(KH - 1, mm)
            pair(KH - 1, PAIRS - 1, last=True)
            rsqrt_of_output(B, KH * PAIRS - 1)

        @block.scalar
        def _(act):
            act.wait_ge(s["const"], 16 * 10)
            for g in range(GROUPS):
                for k in range(KD):
                    act.wait_ge(s["trx"], KD * g + k + 1)
                    b, t0 = divmod(g * GS * P, CHUNKS * P)
                    act.copy(xT[:, k, b, t0:t0 + GS * P], flat(bank[k])).then_inc(s["xT"], 1)
            act.wait_ge(s["ba"], 1)
            act.activation(tab[:, 1, :, :, :].rearrange("p b c v -> p (b c) v"), ba[:, :, 0:VH],
                           ACT.Sigmoid).then_inc(s["soft"], 1)
            act.activation(rows[:, 1, :], rows[:, 1, :], ACT.Exp).then_inc(s["soft"], 1)
            act.wait_ge(s["tab"], 1)
            act.activation(sp_e, sp_abs, ACT.Exp, scale=-1.0).then_inc(s["soft"], 1)
            act.wait_ge(s["tab"], 2)
            act.activation(sp_l, sp_w, ACT.Ln).then_inc(s["soft"], 1)
            act.wait_ge(s["sums"], 3)
            for i in range(3):
                act.activation(tab[:, 2 + i, :, :, :].rearrange("p b c v -> p (b c v)"),
                               flat(bank[5 + i])[:, 0:SUBS * VH], ACT.Exp).then_inc(s["soft"], 1)
            act.wait_ge(s["soft"], 7)

            def copy_qk_or_v(i, n):
                act.wait_ge(s[("pqk", "pv")[i]], n + 1)
                if i == 0:
                    act.wait_ge(s["halo"], n + 1)
                act.copy(raw[:, 2 * i:2 * i + 2, :, HALO:],
                         bank[i][:, :, :].rearrange("p (a b) t -> p a b t", b=BATCH)).then_inc(s["raw"], 1)

            def first_taps(f, m, n):
                act.wait_ge(s["raw"], 2 * (n + 1))
                act.wait_ge(f.s["silu"], m)
                for i in range(4):
                    act.activation(f.conv[:, i, :, :], raw[:, i, :, 0:P], ACT.Copy,
                                   scale=taps[:, i, 0:1]).then_inc(s["tap"], 1)

            def copy_z(f, m, n):
                act.wait_ge(s["pz"], n + 1)
                act.wait_ge(f.s["zact"], m)
                act.copy(f.z_raw[:, :, :], bank[0][:, :, :]).then_inc(s["zraw"], 1)

            def silus(f, m):
                q = 2 * m + f.i
                act.wait_ge(s["conv"], 12 * (q + 1))
                act.wait_ge(f.s["kqs"], m)
                act.activation(f.qkv[:, :, :, :], f.conv[:, :, :, :], ACT.Silu).then_inc(f.s["silu"], 1)
                act.wait_ge(s["zraw"], q + 1)
                act.wait_ge(f.s["xf"], U * m)
                act.activation(f.z_act[:, :, :], f.z_raw[:, :, :], ACT.Silu).then_inc(f.s["zact"], 1)

            def squares(f, m):
                act.wait_ge(f.s["silu"], m + 1)
                act.wait_ge(f.s["sqs"], 2 * m)
                act.activation(f.sq[:, :, :, :], f.qkv[:, 0:2, :, :], ACT.Square).then_inc(f.s["sq"], 1)

            def decay(f, m):
                act.wait_ge(f.s["dt"], m + 1)
                act.wait_ge(f.s["py"], LV * m)
                act.activation(f.em[:, :, :], f.wide[:, :, :], ACT.Exp).then_inc(f.s["em"], 1)

            def tokens(f, m):
                act.wait_ge(f.s["ktok"], m + 1)
                act.wait_ge(f.s["ps"], m)
                act.copy(f.k_tok[:, :, :], f.left[:, 0:2, :]).then_inc(f.s["ktoks"], 1)
                act.wait_ge(f.s["vtok"], m + 1)
                act.wait_ge(f.s["rhs"], U * m)
                act.copy(f.v_tok[:, :, :], f.right[:, :, :]).then_inc(f.s["vtoks"], 1)

            def scaled_keys(f, m):
                act.wait_ge(f.s["kbt"], m + 1)
                act.wait_ge(f.s["ps"], m)
                act.copy(f.kbT[:, :, :], f.wide[:, :, :]).then_inc(f.s["kbT"], 1)

            def first_blocks(f, m):
                act.wait_ge(f.s["Tps"], m + 1)
                act.wait_ge(f.s["o"], m)
                act.copy(f.T[:, :, :], f.right[:, :, :]).then_inc(f.s["T0"], 1)

            def level(f, m, i):
                act.wait_ge(f.s["px"], LV * m + i + 1)
                act.wait_ge(f.s["py"], LV * m + i)
                act.wait_ge(f.s["emm"], 2 * (m + 1))
                act.copy(half(f.X, i + 1, 0), packed(f.wide, i + 1)).then_inc(f.s["X"], 1)

            def from_state(f, m):
                act.wait_ge(f.s["kqs"], m + 1)
                for u in range(U):
                    act.activation(f.qs[:, u, :], f.right[:, u, :], ACT.Copy, scale=f.cur[:, 2, u:u + 1]
                                   ).then_inc(f.s["qss"], 1)

            def solved(f, m):
                act.wait_ge(f.s["pd"], m + 1)
                act.wait_ge(f.s["kbt"], m + 1)
                act.copy(f.d[:, :, :], f.wide[:, :, :]).then_inc(f.s["d"], 1)

            def output_T(f, m):
                act.wait_ge(f.s["txn"], m + 1)
                act.wait_ge(f.s["po"], 2 * m)
                act.activation(f.xnT[:, :, :], f.wide[:, :, :], ACT.Copy, scale=norm_w[:, 0:1]
                               ).then_inc(f.s["xnT"], 1)

            def project(f, m, n):
                copy_qk_or_v(0, n)
                copy_qk_or_v(1, n)
                first_taps(f, m, n)
                copy_z(f, m, n)

            def pair(h, mm, first=False, start=False, turn=False, last=False):
                m = h * PAIRS + mm
                silus(A, m)
                squares(A, m)
                decay(A, m)
                if turn:
                    head_weights(h + 1)
                tokens(A, m)
                scaled_keys(A, m)
                if not first:
                    output_T(B, m - 1)
                if not last:
                    copy_qk_or_v(0, 2 * m + 2)
                silus(B, m)
                squares(B, m)
                decay(B, m)
                tokens(B, m)
                first_blocks(A, m)
                if not last:
                    copy_qk_or_v(1, 2 * m + 2)
                scaled_keys(B, m)
                level(A, m, 0)
                if not last:
                    first_taps(A, m + 1, 2 * m + 2)
                first_blocks(B, m)
                if not last:
                    copy_z(A, m + 1, 2 * m + 2)
                for i in range(1, LV):
                    level(A, m, i)
                    level(B, m, i - 1)
                from_state(A, m)
                level(B, m, LV - 1)
                if not last:
                    copy_qk_or_v(0, 2 * m + 3)
                solved(A, m)
                if not last:
                    copy_qk_or_v(1, 2 * m + 3)
                    first_taps(B, m + 1, 2 * m + 3)
                from_state(B, m)
                solved(B, m)
                if not last:
                    copy_z(B, m + 1, 2 * m + 3)
                output_T(A, m)

            def head_weights(h):
                act.wait_ge(s["w"], 16 * (h + 1))
                act.wait_ge(s["pz"], h * CHUNKS)
                act.copy(w_cur[:, :, :], w_load[:, :, :]).then_inc(s["wcp"], 1)

            head_weights(0)
            for f in flights:
                project(f, 0, f.i)
            pair(0, 0, first=True)
            with act.Fori(0, KH - 1) as h:
                with act.Fori(1, PAIRS - 1) as mm:
                    pair(h, mm)
                pair(h, PAIRS - 1, turn=True)
                pair(h + 1, 0, start=True)
            with act.Fori(1, PAIRS - 1) as mm:
                pair(KH - 1, mm)
            pair(KH - 1, PAIRS - 1, last=True)
            output_T(B, KH * PAIRS - 1)

        @block.vector
        def _(dve):
            for g in range(GROUPS):
                dve.wait_ge(s_x[g], 16)
                for i in range(g * GS, (g + 1) * GS):
                    dve.bn_stats(stats[:, i, :], acc[:, i, :]).then_inc(s["ln"], 1)
            c = SUBS
            dve.wait_ge(s["ln"], c)
            dve.tensor_tensor(mean2[:, :], stats[:, :, 1], stats[:, :, 4], ALU.add).then_inc(s["ln"], 1)
            dve.tensor_tensor(gap[:, :], stats[:, :, 1], stats[:, :, 4], ALU.subtract).then_inc(s["ln"], 1)
            dve.tensor_tensor(var[:, :], stats[:, :, 2], stats[:, :, 5], ALU.add).then_inc(s["ln"], 1)
            dve.wait_ge(s["ln"], c + 3)
            dve.tensor_scalar(mean[:, :], mean2[:, :], 0.5, None, ALU.mult).then_inc(s["ln"], 1)
            dve.scalar_tensor_tensor(gap2[:, :], gap[:, :], 0.25, gap[:, :], ALU.mult, ALU.mult).then_inc(s["ln"], 1)
            dve.tensor_scalar(var_eps[:, :], var[:, :], 1.0 / D, LN_EPS, ALU.mult, ALU.add).then_inc(s["ln"], 1)
            dve.wait_ge(s["ln"], c + 6)
            dve.tensor_tensor(var[:, :], var_eps[:, :], gap2[:, :], ALU.add).then_inc(s["var"], 1)
            dve.wait_ge(s["rstd"], 1)
            for g in range(GROUPS):
                dve.wait_ge(s["trx"], KD * g)
                for i in range(GS):
                    n = g * GS + i
                    dve.tensor_scalar(y[:, i, :], acc[:, n, :], mean[:, n:n + 1], rstd[:, n:n + 1],
                                      ALU.subtract, ALU.mult).then_inc(s["y"], 1)
            dve.wait_ge(s["const"], 16 * 10)
            dve.wait_ge(s["ba"], 1)
            dve.wait_ge(s["soft"], 1)
            dt_bias = rows[:, 0:1, :].to_broadcast([P, SUBS, VH])
            step_no = [0]

            def chain(ins):
                step_no[0] += 1
                ins.then_inc(s["chain"], 1)
                dve.wait_ge(s["chain"], step_no[0])

            chain(dve.tensor_tensor(sp_x, ba[:, :, VH:2 * VH], dt_bias, ALU.add))
            chain(dve.tensor_scalar(sp_r, sp_x, -1.0, None, ALU.mult))
            dve.tensor_tensor(sp_abs, sp_x, sp_r, ALU.max).then_inc(s["tab"], 1)
            dve.wait_ge(s["soft"], 3)
            dve.tensor_scalar(sp_w, sp_e, 1.0, None, ALU.add).then_inc(s["tab"], 1)
            dve.wait_ge(s["tab"], 2)
            chain(dve.tensor_scalar(sp_r, sp_w, 1.0, None, ALU.subtract))
            chain(dve.tensor_scalar(sp_abs, sp_r, 0.0, None, ALU.is_equal))
            chain(dve.tensor_tensor(sp_r, sp_r, sp_abs, ALU.add))
            chain(dve.reciprocal(sp_r, sp_r))
            dve.wait_ge(s["soft"], 4)
            chain(dve.tensor_tensor(sp_l, sp_l, sp_abs, ALU.add))
            chain(dve.tensor_tensor(sp_l, sp_l, sp_e, ALU.mult))
            chain(dve.tensor_tensor(sp_l, sp_l, sp_r, ALU.mult))
            chain(dve.scalar_tensor_tensor(sp_l, sp_x, 0.0, sp_l, ALU.max, ALU.add))
            chain(dve.tensor_tensor(sp_l, sp_l, rows[:, 1:2, :].to_broadcast([P, SUBS, VH]), ALU.mult))
            dve.tensor_scalar(tab[:, 0, :, :, :].rearrange("p b c v -> p (b c) v"), sp_l,
                              -1.0, G_MIN, ALU.mult, ALU.max).then_inc(s["tab"], 1)
            dve.wait_ge(s["soft"], 7)
            dve.wait_ge(s["tab"], 3)

            def halo(n):
                dve.wait_ge(s["tap"], 4 * n)
                dve.wait_ge(s["conv"], 12 * n)
                dve.tensor_copy(raw[:, :, :, 0:HALO], raw[:, :, :, P:P + HALO]).then_inc(s["halo"], 1)

            def convolve(f, n, tap):
                for i in range(4):
                    if tap == 1:
                        dve.wait_ge(s["tap"], 4 * n + i + 1)
                    else:
                        dve.wait_ge(s["conv"], 12 * n + 4 * (tap - 2) + i + 1)
                    dve.scalar_tensor_tensor(f.conv[:, i, :, :], raw[:, i, :, tap:tap + P],
                                             taps[:, i, tap:tap + 1], f.conv[:, i, :, :],
                                             ALU.mult, ALU.add).then_inc(s["conv"], 1)

            def b4(ap):
                return ap.rearrange("p (b i) -> p b i", i=1).to_broadcast([P, BATCH, 2])

            def u4(ap):
                return ap.rearrange("p (b i) -> p b i", i=2)

            def log_decays(f, m, h, c):
                dve.wait_ge(f.s["dt"], m)
                dve.wait_ge(f.s["gU"], U * m)
                dve.sem_inc(s["dve_gate"], 1)
                dve.tensor_copy(f.g[:, :].rearrange("p (b i) -> p b i", i=2),
                                tab[:, 0, :, bass.ds(c + f.i, 1), bass.ds(2 * h, 2)].rearrange("p b c i -> p (b c) i")
                                ).then_inc(f.s["g"], 1)
                dve.wait_ge(f.s["g"], m + 1)
                for u in range(U):
                    dve.tensor_scalar(f.gU[:, u, :], upto[:, :], f.g[:, u:u + 1], None, ALU.mult
                                      ).then_inc(f.s["gU"], 1)

            def factors(f, m, h, c):
                dve.wait_ge(s["S"], U * 2 * m)
                dve.wait_ge(f.s["qss"], U * m)
                dve.sem_inc(s["dve_gate"], 1)
                dve.tensor_copy(f.cur[:, :, :].rearrange("p n (b i) -> p n b i", i=2),
                                tab[:, :, :, bass.ds(c + f.i, 1), bass.ds(2 * h, 2)]
                                .rearrange("p n b c i -> p n (b c) i")).then_inc(f.s["cur"], 1)
                dve.wait_ge(f.s["cur"], m + 1)

            def key_scales(f, m):
                dve.wait_ge(f.s["ss"], m + 1)
                dve.tensor_scalar(f.ss[:, :], f.wide[:, 0, 0:U], 1e-6, None, ALU.add).then_inc(f.s["sse"], 1)

            def scaled_keys(f, m):
                dve.wait_ge(f.s["rr"], m + 1)
                dve.wait_ge(f.s["rhs"], 2 * U * m)
                k0 = 5 * m
                dve.tensor_scalar(f.rqs[:, 0:2], f.rr[:, 0:2], SCALE, None, ALU.mult).then_inc(f.s["scal"], 1)
                dve.tensor_tensor(u4(f.brk[:, :]), u4(f.cur[:, 1, :]), b4(f.rr[:, 2:4]), ALU.mult
                                  ).then_inc(f.s["scal"], 1)
                dve.tensor_tensor(u4(f.ngr[:, :]), u4(f.cur[:, 2, :]), b4(f.rr[:, 2:4]), ALU.mult
                                  ).then_inc(f.s["scal"], 1)
                dve.wait_ge(f.s["scal"], k0 + 3)
                dve.tensor_tensor(u4(f.cc[:, :]), u4(f.brk[:, :]), b4(f.rr[:, 2:4]), ALU.mult).then_inc(f.s["scal"], 1)
                dve.scalar_tensor_tensor(f.bng[:, :], f.ngr[:, :], -1.0, f.brk[:, :], ALU.mult, ALU.mult
                                         ).then_inc(f.s["scal"], 1)
                dve.wait_ge(f.s["scal"], k0 + 5)
                dve.wait_ge(f.s["ktoks"], m + 1)
                dve.wait_ge(f.s["dend"], U * m)
                dve.wait_ge(f.s["pod"], m)
                for u in range(U):
                    dve.tensor_scalar(f.kb[:, u, :], f.k_tok[:, u // 2, :], f.cc[:, u:u + 1], None, ALU.mult
                                      ).then_inc(f.s["kb"], 1)
                dve.wait_ge(f.s["vtoks"], m + 1)
                dve.wait_ge(f.s["xn"], U * m)
                for u in range(U):
                    dve.tensor_scalar(f.rhs[:, u, :], f.v_tok[:, u, :], f.brk[:, u:u + 1], None, ALU.mult
                                      ).then_inc(f.s["rhs"], 1)

            def matrices(f, m):
                dve.wait_ge(f.s["emm"], 2 * m + 1)
                dve.wait_ge(f.s["at"], 2 * m + 1)
                dve.wait_ge(f.s["joined"], LV * m)
                dve.tensor_tensor(f.At[:, :, :], f.wide[:, :, :], f.em_s[:, :, :], ALU.mult).then_inc(f.s["atm"], 1)
                dve.wait_ge(f.s["atm"], 2 * m + 1)
                dve.wait_ge(f.s["px"], LV * m)
                dve.wait_ge(f.s["pd"], m)
                dve.tensor_tensor(f.Aj[:, 0, :, :], f.At[:, :, :], joins[:, 0:1, :].to_broadcast([P, U, P]),
                                  ALU.mult).then_inc(f.s["T"], 1)
                dve.wait_ge(f.s["T"], TN * m + 1)
                dve.tensor_tensor(f.Tt[:, :, :], f.Aj[:, 0, :, :],
                                  ident[:, :].rearrange("p (u t) -> p u t", u=1).to_broadcast([P, U, P]),
                                  ALU.add).then_inc(f.s["T"], 1)

            def within_chunk(f, m):
                dve.wait_ge(f.s["emm"], 2 * m + 2)
                dve.wait_ge(f.s["at"], 2 * m + 2)
                dve.wait_ge(f.s["pod"], m)
                qk = f.left[:, 0:2, :].rearrange("p b (i t) -> p b i t", i=1).to_broadcast([P, BATCH, 2, P])
                dve.tensor_tensor(f.Pt[:, :, :].rearrange("p (b i) t -> p b i t", i=2), qk,
                                  f.em_i[:, :, :].rearrange("p (b i) t -> p b i t", i=2), ALU.mult
                                  ).then_inc(f.s["atm"], 1)

            def level(f, m, i):
                dve.wait_ge(f.s["py"], LV * m + i + 1)
                dve.wait_ge(f.s["T"], TN * m + 2 + 2 * i)
                if i == 0:
                    dve.wait_ge(f.s["T0"], m + 1)
                if i < LV - 1:
                    dst = half(f.T, i + 1, 0)
                    dve.tensor_tensor(dst, dst, packed(f.left, i + 1), ALU.add).then_inc(f.s["T"], 1)
                dst = half(f.Tt, i + 1, 1)
                dve.scalar_tensor_tensor(dst, packed(f.right, i + 1), lower[:, i + 1:i + 2], dst,
                                         ALU.mult, ALU.add).then_inc(f.s["T"], 1)

            def right_side(f, m):
                dve.wait_ge(f.s["kqs"], m + 1)
                dve.wait_ge(f.s["rhs"], 2 * U * m + U)
                for u in range(U):
                    dve.scalar_tensor_tensor(f.rhs[:, u, :], f.left[:, u, :], f.bng[:, u:u + 1], f.rhs[:, u, :],
                                             ALU.mult, ALU.add).then_inc(f.s["rhs"], 1)

            def to_the_end(f, m):
                dve.wait_ge(f.s["d"], m + 1)
                dve.wait_ge(f.s["at"], 2 * m + 2)
                for u in range(U):
                    dve.tensor_scalar(f.d_end[:, u, :], f.d[:, u, :], f.cur[:, 3, u:u + 1], None, ALU.mult
                                      ).then_inc(f.s["dend"], 1)

            def new_state(f, m, h):
                q = 2 * m + f.i
                dve.wait_ge(f.s["ps"], m + 1)
                dve.wait_ge(s["zero"], h + 1)
                dve.wait_ge(s["S"], U * q)
                for u in range(U):
                    dve.scalar_tensor_tensor(state[:, u, :], state[:, u, :], f.cur[:, 4, u:u + 1], f.left[:, u, :],
                                             ALU.mult, ALU.add).then_inc(s["S"], 1)

            def gated(f, m):
                dve.wait_ge(f.s["pod"], m + 1)
                dve.wait_ge(f.s["qss"], U * (m + 1))
                dve.wait_ge(f.s["ss"], m + 1)
                dve.tensor_tensor(f.o, f.right[:, :, :], f.qs[:, :, :], ALU.add).then_inc(f.s["o"], 1)
                dve.wait_ge(f.s["o"], m + 1)
                dve.wait_ge(f.s["zact"], m + 1)
                dve.wait_ge(f.s["pd"], m + 1)
                for u in range(U):
                    dve.scalar_tensor_tensor(f.xf[:, u, :], f.o[:, u, :], f.rqs[:, u // 2:u // 2 + 1],
                                             f.z_act[:, u, :], ALU.mult, ALU.mult).then_inc(f.s["xf"], 1)

            def mean_square(f, m):
                dve.wait_ge(f.s["xf"], U * (m + 1))
                dve.tensor_tensor(f.o, f.xf[:, :, :], f.xf[:, :, :], ALU.mult).then_inc(f.s["sqs"], 1)
                dve.wait_ge(f.s["sqs"], 2 * m + 1)
                dve.tensor_reduce(f.ssq[:, :], f.o, AX.X, ALU.add).then_inc(f.s["sqs"], 1)
                dve.wait_ge(f.s["sqs"], 2 * m + 2)
                dve.tensor_scalar(f.ssq_eps[:, :], f.ssq[:, :], 1.0 / P, 1e-6, ALU.mult, ALU.add
                                  ).then_inc(f.s["sse2"], 1)

            def normalised(f, m):
                dve.wait_ge(f.s["rn"], m + 1)
                dve.wait_ge(f.s["atm"], 2 * (m + 1))
                for u in range(U):
                    dve.tensor_scalar(f.xn[:, u, :], f.xf[:, u, :], f.rn[:, u:u + 1], None, ALU.mult
                                      ).then_inc(f.s["xn"], 1)

            def add_up(f, m, c):
                for b in range(BATCH):
                    dve.wait_ge(f.s["po"], 2 * m + b + 1)
                    dst = acc[:, bass.ds(c + b * CHUNKS, 1), :].rearrange("p c d -> p (c d)")
                    dve.tensor_tensor(dst, dst, flat(f.left if b == 0 else f.right), ALU.add
                                      ).then_inc(f.s["acc"], 1)

            def pair(h, mm, first=False, start=False, turn=False, last=False):
                m, c = h * PAIRS + mm, 2 * mm
                factors(A, m, h, c)
                factors(B, m, h, c)
                if turn:
                    head_taps(h + 1)
                elif not last:
                    halo(2 * m + 2)
                key_scales(A, m)
                if not first:
                    mean_square(B, m - 1)
                scaled_keys(A, m)
                if not first:
                    normalised(B, m - 1)
                matrices(A, m)
                within_chunk(A, m)
                if not first:
                    add_up(B, m - 1, CHUNKS - 1 if start else c - 1)
                key_scales(B, m)
                scaled_keys(B, m)
                matrices(B, m)
                level(A, m, 0)
                within_chunk(B, m)
                for i in range(1, LV):
                    level(A, m, i)
                    level(B, m, i - 1)
                    if i < TAPS and not last:
                        convolve(A, 2 * m + 2, i)
                right_side(A, m)
                level(B, m, LV - 1)
                if not last:
                    halo(2 * m + 3)
                to_the_end(A, m)
                new_state(A, m, h)
                right_side(B, m)
                gated(A, m)
                to_the_end(B, m)
                mean_square(A, m)
                if not last:
                    convolve(B, 2 * m + 3, 1)
                normalised(A, m)
                new_state(B, m, h)
                if not last:
                    log_decays(A, m + 1, h + 1 if turn else h, 0 if turn else c + 2)
                    convolve(B, 2 * m + 3, 2)
                add_up(A, m, c)
                if not last:
                    convolve(B, 2 * m + 3, 3)
                gated(B, m)
                if not last:
                    log_decays(B, m + 1, h + 1 if turn else h, 0 if turn else c + 2)

            def head_taps(h):
                dve.wait_ge(s["conv"], 12 * h * CHUNKS)
                dve.wait_ge(s["tap"], 4 * h * CHUNKS)
                dve.sem_inc(s["dve_gate"], 1)
                dve.tensor_copy(taps[:, :, :], taps_all[:, bass.ds(h, 1), :, :].rearrange("p h a b -> p (h a) b")
                                ).then_inc(s["taps"], 1)
                dve.wait_ge(s["taps"], h + 1)
                dve.sem_inc(s["dve_gate"], 1)
                dve.memset(raw[:, :, :, 0:HALO], 0.0).then_inc(s["halo"], 1)

            head_taps(0)
            for f in flights:
                if f.i > 0:
                    halo(f.i)
                dve.wait_ge(s["halo"], f.i + 1)
                for tap in range(1, TAPS):
                    convolve(f, f.i, tap)
            for f in flights:
                log_decays(f, 0, 0, 0)
            pair(0, 0, first=True)
            with dve.Fori(0, KH - 1) as h:
                with dve.Fori(1, PAIRS - 1) as mm:
                    pair(h, mm)
                pair(h, PAIRS - 1, turn=True)
                pair(h + 1, 0, start=True)
            with dve.Fori(1, PAIRS - 1) as mm:
                pair(KH - 1, mm)
            pair(KH - 1, PAIRS - 1, last=True)
            end = KH * PAIRS - 1
            mean_square(B, end)
            normalised(B, end)
            add_up(B, end, CHUNKS - 1)

        @block.tensor
        def _(pe):
            pe.wait_ge(s["const"], 16 * 10)
            pe.wait_ge(s["set"], 3)
            for g in range(GROUPS):
                pe.wait_ge(s["y"], GS * (g + 1))
                pe.wait_ge(s["xT"], KD * g)
                for k in range(KD):
                    for i in range(GS):
                        mm = pe.transpose(bank[k][:, i, :], y[:, i, k * P:(k + 1) * P], ident[:, :])
                    mm.then_inc(s["trx"], 1)
            pe.wait_ge(s["xT"], KD * GROUPS)
            for n in range(SUBS):
                b, c = divmod(n, CHUNKS)
                for k in range(KD):
                    mm = pe.matmul(ba[:, n, :], xT[:, k, b, c * P:(c + 1) * P], w_ba[:, k, :],
                                   start=(k == 0), stop=(k == KD - 1))
            mm.then_inc(s["ba"], 1)
            pe.wait_ge(s["tab"], 3)
            for i, sums in enumerate((upto, after, full)):
                pe.matmul(flat(bank[5 + i])[:, 0:SUBS * VH], sums[:, :],
                          tab[:, 0, :, :, :].rearrange("p b c v -> p (b c v)"),
                          start=True, stop=True).then_inc(s["sums"], 1)
            pe.wait_ge(s["soft"], 7)

            def project_qk(f, n):
                pe.wait_ge(s["xcur"], n + 1)
                pe.wait_ge(s["zraw"], n)
                project_part(f, 0, s["pqk"])

            def project_v(f, n):
                pe.wait_ge(s["raw"], 2 * n)
                project_part(f, 1, s["pv"])

            def project_part(f, i, done):
                for a in range(2):
                    col = (2 * i + a) * P
                    for k in range(KD):
                        mm = pe.matmul(bank[i][:, 2 * a:2 * a + 2, :], w_cur[:, k, col:col + P],
                                       f.x_cur[:, k, :, :], start=(k == 0), stop=(k == KD - 1))
                mm.then_inc(done, 1)

            def project_z(f, n, parts=range(BATCH)):
                pe.wait_ge(s["raw"], 2 * n + 1)
                for b in parts:
                    for k in range(KD):
                        mm = pe.matmul(bank[0][:, 2 * b:2 * b + 2, :], f.x_cur[:, k, b, :], w_cur[:, k, 4 * P:6 * P],
                                       start=(k == 0), stop=(k == KD - 1))
                if BATCH - 1 in parts:
                    mm.then_inc(s["pz"], 1)

            def decays(f, m):
                pe.wait_ge(f.s["gU"], U * (m + 1))
                pe.wait_ge(f.s["xnT"], m)
                pe.matmul(f.wide[:, :, :], after[:, :], f.gU[:, :, :], start=True, stop=True).then_inc(f.s["dt"], 1)

            def tokens(f, m):
                pe.wait_ge(f.s["acc"], 2 * m)
                pe.wait_ge(f.s["silu"], m + 1)
                for b in range(BATCH):
                    mm = pe.transpose(f.left[:, b, :], f.qkv[:, 1, b, :], ident[:, :])
                mm.then_inc(f.s["ktok"], 1)
                for u in range(U):
                    mm = pe.transpose(f.right[:, u, :], f.qkv[:, 2 + u % 2, u // 2, :], ident[:, :])
                mm.then_inc(f.s["vtok"], 1)

            def lengths(f, m):
                pe.wait_ge(f.s["sq"], m + 1)
                pe.wait_ge(f.s["em"], m + 1)
                for a in range(2):
                    for b in range(BATCH):
                        mm = pe.matmul(f.wide[:, 0, 2 * a + b:2 * a + b + 1], f.sq[:, a, b, :], full[:, 0:1],
                                       start=True, stop=True)
                mm.then_inc(f.s["ss"], 1)

            def keys(f, m):
                pe.wait_ge(f.s["kb"], U * (m + 1))
                for u in range(U):
                    mm = pe.transpose(f.wide[:, u, :], f.kb[:, u, :], ident[:, :])
                mm.then_inc(f.s["kbt"], 1)

            def products(f, m):
                pe.wait_ge(f.s["ktoks"], m + 1)
                pe.wait_ge(f.s["kbT"], m + 1)
                for b in range(BATCH):
                    mm = pe.matmul(f.wide[:, 2 * b:2 * b + 2, :], f.qkv[:, 1, b, :], f.kbT[:, 2 * b:2 * b + 2, :],
                                   start=True, stop=True)
                mm.then_inc(f.s["at"], 1)
                for b in range(BATCH):
                    mm = pe.matmul(f.left[:, b, :], f.qkv[:, 1, b, :], f.qkv[:, 0, b, :], start=True, stop=True)
                mm.then_inc(f.s["at"], 1)

            def first_blocks(f, m):
                pe.wait_ge(f.s["T"], TN * m + 2)
                pe.wait_ge(f.s["vtoks"], m + 1)
                for u in range(U):
                    mm = pe.transpose(f.right[:, u, :], f.Tt[:, u, :], ident[:, :])
                mm.then_inc(f.s["Tps"], 1)

            def level_x(f, m, i):
                if i == 0:
                    pe.wait_ge(f.s["T0"], m + 1)
                    pe.wait_ge(f.s["atm"], 2 * m + 2)
                pe.wait_ge(f.s["joined"], LV * m + i + 1)
                pe.wait_ge(f.s["T"], TN * m + (1 + 2 * i if i > 0 else 2))
                for u in range(U):
                    mm = pe.matmul(packed(f.wide, i + 1, u), f.Aj[:, (i + 1) % 2, u, :], half_of(f.T, u, i + 1, 0),
                                   start=True, stop=True)
                mm.then_inc(f.s["px"], 1)

            def level_y(f, m, i):
                pe.wait_ge(f.s["X"], LV * m + i + 1)
                pe.wait_ge(f.s["T"], TN * m + 2 + 2 * i)
                for u in range(U):
                    if i < LV - 1:
                        pe.matmul(packed(f.left, i + 1, u), f.Tt[:, u, :], half_of(f.X, u, i + 1, 0),
                                  start=True, stop=True)
                    mm = pe.matmul(packed(f.right, i + 1, u), f.X[:, u, :], half_of(f.Tt, u, i + 1, 1),
                                   start=True, stop=True)
                mm.then_inc(f.s["py"], 1)

            def from_state(f, m):
                pe.wait_ge(s["S"], U * (2 * m + f.i))
                pe.wait_ge(f.s["T"], TN * (m + 1))
                for a, bk in ((1, f.left), (0, f.right)):
                    for b in range(BATCH):
                        mm = pe.matmul(bk[:, 2 * b:2 * b + 2, :], f.qkv[:, a, b, :], state[:, 2 * b:2 * b + 2, :],
                                       start=True, stop=True)
                mm.then_inc(f.s["kqs"], 1)

            def solve(f, m):
                pe.wait_ge(f.s["rhs"], 2 * U * (m + 1))
                for u in range(U):
                    mm = pe.matmul(f.wide[:, u, :], f.Tt[:, u, :], f.rhs[:, u, :], start=True, stop=True)
                mm.then_inc(f.s["pd"], 1)

            def within_chunk(f, m):
                pe.wait_ge(f.s["qss"], U * (m + 1))
                pe.wait_ge(f.s["d"], m + 1)
                for u in range(U):
                    mm = pe.matmul(f.right[:, u, :], f.Pt[:, u, :], f.d[:, u, :], start=True, stop=True)
                mm.then_inc(f.s["pod"], 1)

            def to_state(f, m):
                pe.wait_ge(f.s["dend"], U * (m + 1))
                for b in range(BATCH):
                    mm = pe.matmul(f.left[:, 2 * b:2 * b + 2, :], f.k_tok[:, b, :], f.d_end[:, 2 * b:2 * b + 2, :],
                                   start=True, stop=True)
                mm.then_inc(f.s["ps"], 1)

            def output_T(f, m):
                pe.wait_ge(f.s["xn"], U * (m + 1))
                for u in range(U):
                    mm = pe.transpose(f.wide[:, u, :], f.xn[:, u, :], ident[:, :])
                mm.then_inc(f.s["txn"], 1)

            def project_out(f, m):
                pe.wait_ge(f.s["xnT"], m + 1)
                pe.wait_ge(s["S"], U * (2 * m + f.i + 1))
                for b in range(BATCH):
                    out = flat(f.left if b == 0 else f.right)
                    for i in range(2):
                        mm = pe.matmul(out, f.xnT[:, 2 * b + i, :], o_cur[:, i, :], start=(i == 0), stop=(i == 1))
                    mm.then_inc(f.s["po"], 1)

            def pair(h, mm, first=False, start=False, turn=False, last=False):
                m = h * PAIRS + mm
                decays(A, m)
                if turn:
                    pe.wait_ge(s["wcp"], h + 2)
                if start:
                    pe.wait_ge(s["zero"], h + 1)
                if not last:
                    project_qk(A, 2 * m + 2)
                tokens(A, m)
                lengths(A, m)
                if not last:
                    project_v(A, 2 * m + 2)
                keys(A, m)
                if not first:
                    output_T(B, m - 1)
                products(A, m)
                if not first:
                    project_out(B, m - 1)
                decays(B, m)
                tokens(B, m)
                lengths(B, m)
                first_blocks(A, m)
                if not last:
                    project_z(A, 2 * m + 2, (0,))
                keys(B, m)
                level_x(A, m, 0)
                products(B, m)
                level_y(A, m, 0)
                if not last:
                    project_z(A, 2 * m + 2, (1,))
                first_blocks(B, m)
                for i in range(1, LV):
                    level_x(A, m, i)
                    level_x(B, m, i - 1)
                    level_y(A, m, i)
                    level_y(B, m, i - 1)
                from_state(A, m)
                level_x(B, m, LV - 1)
                if not last:
                    project_qk(B, 2 * m + 3)
                level_y(B, m, LV - 1)
                solve(A, m)
                if not last:
                    project_v(B, 2 * m + 3)
                to_state(A, m)
                within_chunk(A, m)
                if not last:
                    project_z(B, 2 * m + 3, (0,))
                from_state(B, m)
                if not last:
                    project_z(B, 2 * m + 3, (1,))
                solve(B, m)
                to_state(B, m)
                within_chunk(B, m)
                output_T(A, m)
                if first or start:
                    pe.wait_ge(s["ow"], 16 * (h + 1))
                project_out(A, m)

            pe.wait_ge(s["wcp"], 1)
            pe.wait_ge(s["zero"], 1)
            for f in flights:
                project_qk(f, f.i)
                project_v(f, f.i)
                project_z(f, f.i)
            pair(0, 0, first=True)
            with pe.Fori(0, KH - 1) as h:
                with pe.Fori(1, PAIRS - 1) as mm:
                    pair(h, mm)
                pair(h, PAIRS - 1, turn=True)
                pair(h + 1, 0, start=True)
            with pe.Fori(1, PAIRS - 1) as mm:
                pair(KH - 1, mm)
            pair(KH - 1, PAIRS - 1, last=True)
            output_T(B, KH * PAIRS - 1)
            project_out(B, KH * PAIRS - 1)


def layer_stack(nc, ins, out):
    rows = out.shape[0] * out.shape[1]
    dim = out.shape[2]
    x1, x2, x3 = (nc.dram_tensor(f"rows_{i}", (rows, dim), F32, kind="Internal").ap() for i in (1, 2, 3))
    with ExitStack() as ctx:
        psum = [ctx.enter_context(nc.psum_tensor(f"banks_{i}", (P, 1024), F32)) for i in range(4)]
        decay_mixer(nc, psum, ins, ins["x"], x1, ins)
        ffn = (ins["ffn_gate"], ins["ffn_up"], ins["ffn_down"])
        feed_forward(nc, psum, "f1", ins, x1, x2, *ffn)
        delta_mixer(nc, psum, ins, x2, x3, ins)
        feed_forward(nc, psum, "f2", ins, x3, out.rearrange("b n d -> (b n) d"), *ffn)


def _laid_out(i):
    import numpy as np
    heads_a, key_heads = 16, 8
    width = i["L0_attn_a_in_proj_w"].shape[1]
    tiles = width // P
    column = lambda a: a.reshape(tiles, P, -1)
    cols = np.concatenate([column(i[f"L0_attn_a_{n}"]) for n in ("norm_scale", "conv_b", "dt_bias", "conv_w")], 2)
    ba = i["L0_attn_b_w_ba"].reshape(key_heads, 2, 2, width)
    taps = i["L0_attn_b_conv_w"]
    keys = key_heads * P
    per_head = [taps[:keys].reshape(key_heads, 1, P, -1), taps[keys:2 * keys].reshape(key_heads, 1, P, -1),
                taps[2 * keys:].reshape(key_heads, 2, P, -1)]
    rows = np.stack([i["L0_attn_b_dt_bias"], i["L0_attn_b_A_log"]])
    return {
        "x": i["L0_attn_a_x"],
        "cols": cols.transpose(1, 2, 0),
        "mix_rows": np.repeat(i["L0_attn_a_head_mix"], width // heads_a, axis=0).reshape(tiles, P, heads_a)
        .transpose(1, 0, 2),
        "a_in": i["L0_attn_a_in_proj_w"].T,
        "a_out": i["L0_attn_a_out_proj_w"].T,
        "ffn_gate": i["L0_ffn_w_gate"], "ffn_up": i["L0_ffn_w_up"], "ffn_down": i["L0_ffn_w_down"],
        "rows": np.broadcast_to(rows[None], (P, *rows.shape)),
        "norm_w": i["L0_attn_b_norm_weight"].reshape(P, 1),
        "w_ba": ba.transpose(1, 0, 2, 3).reshape(-1, width).T.reshape(tiles, P, -1).transpose(1, 0, 2),
        "b_qkvz": i["L0_attn_b_w_qkvz"].T,
        "b_out": i["L0_attn_b_w_out"].T,
        "taps": np.concatenate(per_head, 1).transpose(2, 0, 1, 3),
    }


def kernel(**inputs):
    import numpy as np
    import concourse.bacc as bacc
    from concourse.bass_utils import run_bass_kernel_spmd

    arrays = {**_laid_out({k: np.asarray(v) for k, v in inputs.items()}), **layer_a_tables(), **layer_b_tables()}
    arrays = {f"in_{k}": np.ascontiguousarray(v) for k, v in arrays.items()}
    nc = bacc.Bacc("TRN2", target_bir_lowering=False, num_devices=1)
    ins = {k[3:]: nc.dram_tensor(k, v.shape, mybir.dt.from_np(v.dtype), kind="ExternalInput").ap()
           for k, v in arrays.items()}
    shape = inputs["L0_attn_a_x"].shape
    out = nc.dram_tensor("out_rows", shape, F32, kind="ExternalOutput").ap()
    layer_stack(nc, ins, out)
    r = run_bass_kernel_spmd(nc, [arrays], core_ids=[0])
    return r.results[0]["out_rows"]
```

```python
from contextlib import ExitStack, contextmanager

import concourse.bass as bass
from concourse import mybir

P = 128
LN_EPS = 1e-5
F32 = mybir.dt.float32
F32R = mybir.dt.float32r
BF16 = mybir.dt.bfloat16
ALU = mybir.AluOpType
ACT = mybir.ActivationFunctionType
AX = mybir.AxisListType


@contextmanager
def cleared_semaphores(nc, prefix):
    taken = []

    def sem(name):
        taken.append(nc.alloc_semaphore(f"{prefix}_{name}"))
        return taken[-1]

    yield sem
    nc.clear_and_free_semaphores(taken)
    nc.all_engine_barrier()


def layer_a_tables():
    import numpy as np
    tokens, head = 1024, 32
    inv = (1.0 / 10000.0 ** (np.arange(0, head, 2, dtype=np.float32) / np.float32(head))).astype(np.float32)
    angle = np.arange(tokens, dtype=np.float32)[None, :] * inv[:, None]
    row = np.arange(P) % (head // 2)
    rot = np.zeros((P, P), np.float32)
    for m in range(P):
        h, e = divmod(m, head)
        if e < head // 2:
            rot[h * head + e + head // 2, m] = -1.0
        else:
            rot[h * head + e - head // 2, m] = 1.0
    within = np.ones((P, tokens), np.float32)
    within[:, ::64] = 0.0
    eye = (np.arange(P)[:, None] % head == np.arange(head)[None, :]).astype(np.float32)
    return {"ident": np.eye(P, dtype=np.float32), "rot": rot, "cos": np.cos(angle)[row], "sin": np.sin(angle)[row],
            "within": within, "eye_head": eye}


def layer_b_tables():
    import numpy as np
    r, c = np.arange(P)[:, None], np.arange(P)[None, :]
    joins = [-((r // (2 * n) == c // (2 * n)) & ((c // n) % 2 == 1) & ((r // n) % 2 == 0)).astype(np.float32)
             for n in (1, 2, 4, 8, 16, 32, 64)]
    lower = np.stack([(np.arange(P) // n) % 2 == 0 for n in (1, 2, 4, 8, 16, 32, 64)], 1).astype(np.float32)
    return {"lower": lower, "ident": np.eye(P, dtype=np.float32), "upto": (r <= c).astype(np.float32),
            "after": (r > c).astype(np.float32), "below": (r < c).astype(np.float32),
            "joins": np.ascontiguousarray(np.stack(joins, 1))}


def decay_mixer(nc, psum, consts, x_in, x_out, w):
    BATCH, N, D = x_in.shape
    KD = D // P
    SUB = N // P
    HALF = N // 2
    TAPS = 4
    CH = 64
    NCH = N // CH
    with ExitStack() as ctx:
        def sb(n, shape, dt=F32):
            return ctx.enter_context(nc.sbuf_tensor(f"a_{n}", shape, dt))

        sem = ctx.enter_context(cleared_semaphores(nc, "a"))

        ident = sb("ident", [P, P])
        rot = sb("rot", [P, P])
        cos, sin = sb("cos", [P, N]), sb("sin", [P, N])
        within = sb("within", [P, N])
        ones = sb("ones", [P, NCH])
        mhalf = sb("mhalf", [P, SUB])
        w_in = sb("w_in", [P, KD, 3 * D])
        w_out = sb("w_out", [P, KD, D])
        mix = sb("mix", [P, KD, D])
        mix_rows = sb("mix_rows", [P, KD, D // 32])
        eye_head = sb("eye_head", [P, 32])
        cols = sb("cols", [P, 3 + TAPS, KD])
        x = sb("x", [P, SUB, D])
        y = sb("y", [P, SUB, D])
        stats = sb("stats", [P, SUB, 6])
        mean2, mean, gap, gap2, var, var_eps, rstd, msq, msq_eps, rrms = (
            sb(n, [P, SUB]) for n in ("mean2", "mean", "gap", "gap2", "var", "var_eps", "rstd", "msq", "msq_eps",
                                      "rrms"))
        xnT = sb("xnT", [P, KD, TAPS - 1 + N])
        xc = sb("xc", [P, KD, N])
        gate = sb("gate", [P, KD, N])
        final = sb("final", [P, KD, N])
        arg, ex, dt, dec, decs, grow, fade, fade0, v, va, vb = (
            sb(n, [P, N]) for n in ("arg", "ex", "dt", "dec", "decs", "grow", "fade", "fade0", "v", "va", "vb"))
        cd, cdc, ncd, up, down, seeds, csum, carry = (
            sb(n, [P, NCH]) for n in ("cd", "cdc", "ncd", "up", "down", "seeds", "csum", "carry"))
        ps_dt, ps_v, ps_g, ps_p = banks = psum

        s_tab = sem("s_tab")
        s_w = sem("s_w")
        s_set = sem("s_set")
        s_mix = sem("s_mix")
        s_x = sem("s_x")
        s_ln = sem("s_ln")
        s_var = sem("s_var")
        s_rstd = sem("s_rstd")
        s_y = sem("s_y")
        s_sq = sem("s_sq")
        s_msq = sem("s_msq")
        s_rrms = sem("s_rrms")
        s_xy = sem("s_xy")
        s_yn = sem("s_yn")
        s_tr = sem("s_tr")
        s_sc = sem("s_sc")
        s_clip = sem("s_clip")
        s_conv = sem("s_conv")
        s_tap = sem("s_tap")
        s_xc = sem("s_xc")
        s_pdt, s_pv, s_pg, s_pp = sem("s_pdt"), sem("s_pv"), sem("s_pg"), sem("s_pp")
        s_arg = sem("s_arg")
        s_ex = sem("s_ex")
        s_dt = sem("s_dt")
        s_dec = sem("s_dec")
        s_exps = sem("s_exps")
        s_v = sem("s_v")
        s_gate = sem("s_gate")
        s_va = sem("s_va")
        s_vb = sem("s_vb")
        s_cum = sem("s_cum")
        s_cd = sem("s_cd")
        s_cexp = sem("s_cexp")
        s_car = sem("s_car")
        s_fin = sem("s_fin")
        s_sig = sem("s_sig")
        s_pm = sem("s_pm")
        s_gm = sem("s_gm")
        s_po = sem("s_po")
        s_res = sem("s_res")
        s_store = sem("s_store")
        LN = SUB + 6
        CONV = TAPS - 1

        block = ctx.enter_context(nc.Block())

        @block.sync
        def _(sp):
            xr = x_in.rearrange("b (s p) d -> b p s d", p=P)
            outr = x_out.rearrange("(b s p) d -> b p s d", p=P, b=BATCH)
            for s in range(2):
                part = slice(s * SUB // 2, (s + 1) * SUB // 2)
                sp.dma_start(x[:, part, :], xr[0, :, part, :]).then_inc(s_x, 16)
            for tile, src in ((ident, "ident"), (cols, "cols"), (within, "within"), (rot, "rot"),
                              (cos, "cos"), (sin, "sin"), (mix_rows, "mix_rows"), (eye_head, "eye_head")):
                full = tile[:, :] if len(tile.shape) == 2 else tile[:, :, :]
                sp.dma_start(full, w[src] if src in w else consts[src]).then_inc(s_tab, 16)
            sp.dma_start(w_in[:, :, :], w["a_in"].rearrange("(k p) n -> p k n", p=P)).then_inc(s_w, 16)
            sp.dma_start(w_out[:, :, :], w["a_out"].rearrange("(k p) n -> p k n", p=P)).then_inc(s_w, 16)
            for b in range(BATCH):
                for s in range(2):
                    part = slice(s * SUB // 2, (s + 1) * SUB // 2)
                    sp.wait_ge(s_res, SUB * b + (s + 1) * SUB // 2)
                    sp.dma_start(outr[b][:, part, :], x[:, part, :]).then_inc(s_store, 16)
                if b < BATCH - 1:
                    sp.wait_ge(s_store, 32 * (b + 1))
                    for s in range(2):
                        part = slice(s * SUB // 2, (s + 1) * SUB // 2)
                        sp.dma_start(x[:, part, :], xr[b + 1, :, part, :]).then_inc(s_x, 16)
            sp.wait_ge(s_store, 32 * BATCH)

        @block.gpsimd
        def _(pool):
            pool.memset(mhalf[:, :], -0.5).then_inc(s_set, 1)
            pool.memset(ones[:, :], 1.0).then_inc(s_set, 1)
            pool.memset(carry[:, 0:1], 0.0).then_inc(s_set, 1)
            pool.memset(xnT[:, :, 0:TAPS - 1], 0.0).then_inc(s_set, 1)
            pool.wait_ge(s_set, 4)
            pool.wait_ge(s_tab, 16 * 8)
            with pool.Fori(0, BATCH) as b:
                pool.wait_ge(s_var, b + 1)
                pool.tensor_tensor(rstd[:, :], var[:, :], mhalf[:, :], ALU.pow).then_inc(s_rstd, 1)
                pool.wait_ge(s_msq, b + 1)
                pool.tensor_tensor(rrms[:, :], msq_eps[:, :], mhalf[:, :], ALU.pow).then_inc(s_rrms, 1)
                for j in range(KD):
                    n = b * KD + j
                    pool.wait_ge(s_v, n + 1)
                    pool.wait_ge(s_cum, 3 * n)
                    pool.tensor_tensor(va[:, :], v[:, :], cos[:, :], ALU.mult).then_inc(s_va, 1)
                    pool.wait_ge(s_dt, n + 1)
                    pool.wait_ge(s_vb, 2 * n + 2)
                    pool.tensor_tensor(va[:, :], vb[:, :], dt[:, :], ALU.mult).then_inc(s_va, 1)

        @block.scalar
        def _(act):
            act.wait_ge(s_tab, 16 * 8)
            with act.Fori(0, BATCH) as b:
                for i in range(SUB):
                    act.wait_ge(s_y, SUB * b + i + 1)
                    act.wait_ge(s_sq, SUB * b + i)
                    act.activation(final[:, 0, 0:D], y[:, i, :], ACT.Square,
                                   accum_out=msq[:, i:i + 1]).then_inc(s_sq, 1)
                for k in range(KD):
                    act.wait_ge(s_tr, KD * b + k + 1)
                    act.activation(xnT[:, k, TAPS - 1:], banks[k][:, :], ACT.Copy,
                                   scale=cols[:, 0, k:k + 1]).then_inc(s_sc, 1)
                for k in range(KD):
                    n = b * KD + k
                    act.wait_ge(s_clip, n + 1)
                    act.activation(xc[:, k, :], xnT[:, k, 0:N], ACT.Copy, scale=cols[:, 3, k:k + 1]).then_inc(s_tap, 1)
                for k in range(KD):
                    n = b * KD + k
                    act.wait_ge(s_conv, CONV * (n + 1))
                    act.activation(xc[:, k, :], xc[:, k, :], ACT.Silu, bias=cols[:, 1, k:k + 1]).then_inc(s_xc, 1)
                for j in range(KD):
                    n = b * KD + j
                    act.wait_ge(s_arg, n + 1)
                    act.activation(ex[:, :], arg[:, :], ACT.Exp).then_inc(s_ex, 1)
                    act.wait_ge(s_ex, 2 * n + 1)
                    act.activation(ex[:, :], ex[:, :], ACT.Ln, bias=1.0).then_inc(s_ex, 1)
                    act.wait_ge(s_pv, n + 1)
                    act.wait_ge(s_va, 2 * n)
                    act.wait_ge(s_pp, n)
                    act.copy(v[:, :], ps_v[:, :]).then_inc(s_v, 1)
                    act.wait_ge(s_dec, 3 * n + 3)
                    act.activation(grow[:, :], decs[:, :], ACT.Exp, scale=-1.0).then_inc(s_exps, 1)
                    act.activation(fade0[:, :], decs[:, :], ACT.Exp).then_inc(s_exps, 1)
                    act.activation(fade[:, :], dec[:, :], ACT.Exp).then_inc(s_exps, 1)
                    act.wait_ge(s_cd, 3 * n + 3)
                    act.activation(up[:, :], ncd[:, :], ACT.Exp, scale=-1.0).then_inc(s_cexp, 1)
                    act.activation(down[:, :], ncd[:, :], ACT.Exp).then_inc(s_cexp, 1)
                    act.wait_ge(s_pg, n + 1)
                    act.wait_ge(s_po, SUB * b)
                    act.copy(gate[:, j, :], ps_g[:, :]).then_inc(s_gate, 1)
                act.wait_ge(s_gate, KD * (b + 1))
                for j in range(KD):
                    act.activation(gate[:, j, :], gate[:, j, :], ACT.Sigmoid).then_inc(s_sig, 1)

        @block.vector
        def _(dve):
            dve.wait_ge(s_tab, 16 * 8)
            dve.wait_ge(s_set, 4)
            for k in range(KD):
                dve.tensor_tensor(mix[:, k, :].rearrange("p (m e) -> p m e", e=32),
                                  mix_rows[:, k, :].rearrange("p (m e) -> p m e", e=1).to_broadcast([P, D // 32, 32]),
                                  eye_head[:, :].rearrange("p (m e) -> p m e", m=1).to_broadcast([P, D // 32, 32]),
                                  ALU.mult).then_inc(s_mix, 1)
            with dve.Fori(0, BATCH) as b:
                dve.wait_ge(s_x, 32 * (b + 1))
                for i in range(SUB):
                    dve.bn_stats(stats[:, i, :], x[:, i, :]).then_inc(s_ln, 1)
                c = LN * b + SUB
                dve.wait_ge(s_ln, c)
                dve.tensor_tensor(mean2[:, :], stats[:, :, 1], stats[:, :, 4], ALU.add).then_inc(s_ln, 1)
                dve.tensor_tensor(gap[:, :], stats[:, :, 1], stats[:, :, 4], ALU.subtract).then_inc(s_ln, 1)
                dve.tensor_tensor(var[:, :], stats[:, :, 2], stats[:, :, 5], ALU.add).then_inc(s_ln, 1)
                dve.wait_ge(s_ln, c + 3)
                dve.tensor_scalar(mean[:, :], mean2[:, :], 0.5, None, ALU.mult).then_inc(s_ln, 1)
                dve.scalar_tensor_tensor(gap2[:, :], gap[:, :], 0.25, gap[:, :], ALU.mult, ALU.mult).then_inc(s_ln, 1)
                dve.tensor_scalar(var_eps[:, :], var[:, :], 1.0 / D, LN_EPS, ALU.mult, ALU.add).then_inc(s_ln, 1)
                dve.wait_ge(s_ln, c + 6)
                dve.tensor_tensor(var[:, :], var_eps[:, :], gap2[:, :], ALU.add).then_inc(s_var, 1)
                dve.wait_ge(s_tr, KD * b)
                dve.wait_ge(s_rstd, b + 1)
                for i in range(SUB):
                    dve.tensor_scalar(y[:, i, :], x[:, i, :], mean[:, i:i + 1], rstd[:, i:i + 1],
                                      ALU.subtract, ALU.mult).then_inc(s_y, 1)
                dve.wait_ge(s_y, SUB * (b + 1))
                for i in range(SUB):
                    dve.tensor_tensor(x[:, i, :], x[:, i, :], y[:, i, :], ALU.add).then_inc(s_xy, 1)
                dve.wait_ge(s_sq, SUB * (b + 1))
                dve.tensor_scalar(msq_eps[:, :], msq[:, :], 1.0 / D, 1e-6, ALU.mult, ALU.add).then_inc(s_msq, 1)
                dve.wait_ge(s_xy, SUB * (b + 1))
                dve.wait_ge(s_rrms, b + 1)
                for i in range(SUB):
                    dve.tensor_scalar(y[:, i, :], y[:, i, :], rrms[:, i:i + 1], None, ALU.mult).then_inc(s_yn, 1)
                def clip(k):
                    xk = xnT[:, k, TAPS - 1:]
                    dve.wait_ge(s_sc, b * KD + k + 1)
                    dve.tensor_scalar(xk, xk, -60000.0, 60000.0, ALU.max, ALU.min).then_inc(s_clip, 1)

                clip(0)
                for k in range(KD):
                    n = b * KD + k
                    if k + 1 < KD:
                        clip(k + 1)
                    dve.wait_ge(s_tap, n + 1)
                    for tap in range(1, TAPS):
                        if tap > 1:
                            dve.wait_ge(s_conv, CONV * n + tap - 1)
                        dve.scalar_tensor_tensor(xc[:, k, :], xnT[:, k, tap:tap + N], cols[:, 3 + tap, k:k + 1],
                                                 xc[:, k, :], ALU.mult, ALU.add).then_inc(s_conv, 1)
                for j in range(KD):
                    n = b * KD + j
                    dve.wait_ge(s_pdt, n + 1)
                    dve.tensor_scalar(arg[:, :], ps_dt[:, :], cols[:, 2, j:j + 1], 20.0,
                                      ALU.add, ALU.min).then_inc(s_arg, 1)
                    dve.wait_ge(s_ex, 2 * n + 2)
                    dve.wait_ge(s_va, 2 * n)
                    dve.tensor_scalar(dt[:, :], ex[:, :], 0.001, 2.0, ALU.max, ALU.min).then_inc(s_dt, 1)
                    dve.wait_ge(s_dt, n + 1)
                    dve.tensor_tensor_scan(decs[:, :], within[:, :], dt[:, :], 0.0,
                                           ALU.mult, ALU.subtract).then_inc(s_dec, 1)
                    dve.wait_ge(s_dec, 3 * n + 1)
                    dve.tensor_scalar(dec[:, :], decs[:, :], -20.0, 0.0, ALU.max, ALU.min).then_inc(s_dec, 1)
                    dve.wait_ge(s_dec, 3 * n + 2)
                    dch = dec[:, :].rearrange("p (c t) -> p c t", t=CH)
                    dve.tensor_tensor(decs[:, :].rearrange("p (c t) -> p c t", t=CH), dch,
                                      dch[:, :, 0:1].to_broadcast([P, NCH, CH]), ALU.subtract).then_inc(s_dec, 1)
                    dve.tensor_tensor_scan(cd[:, :], ones[:, :], dec[:, CH - 1:N:CH], 0.0,
                                           ALU.mult, ALU.add).then_inc(s_cd, 1)
                    dve.wait_ge(s_cd, 3 * n + 1)
                    dve.tensor_scalar(cdc[:, :], cd[:, :], -80.0, 0.0, ALU.max, ALU.min).then_inc(s_cd, 1)
                    dve.wait_ge(s_cd, 3 * n + 2)
                    dve.tensor_scalar(ncd[:, :], cdc[:, :], cdc[:, 0:1], -20.0,
                                      ALU.subtract, ALU.max).then_inc(s_cd, 1)
                    dve.wait_ge(s_pp, n + 1)
                    dve.tensor_tensor(vb[:, :], ps_p[:, :], sin[:, :], ALU.mult).then_inc(s_vb, 1)
                    dve.wait_ge(s_vb, 2 * n + 1)
                    dve.wait_ge(s_va, 2 * n + 1)
                    dve.tensor_tensor(vb[:, :], vb[:, :], va[:, :], ALU.add).then_inc(s_vb, 1)
                    dve.wait_ge(s_exps, 3 * n + 3)
                    dve.wait_ge(s_va, 2 * n + 2)
                    dve.tensor_tensor(vb[:, :], grow[:, :], va[:, :], ALU.mult).then_inc(s_cum, 1)
                    dve.wait_ge(s_cum, 3 * n + 1)
                    dve.tensor_tensor_scan(grow[:, :], within[:, :], vb[:, :], 0.0, ALU.mult, ALU.add).then_inc(s_cum, 1)
                    dve.wait_ge(s_cum, 3 * n + 2)
                    dve.tensor_tensor(final[:, j, :], fade0[:, :], grow[:, :], ALU.mult).then_inc(s_cum, 1)
                    dve.wait_ge(s_cum, 3 * n + 3)
                    dve.wait_ge(s_cexp, 2 * n + 2)
                    dve.tensor_tensor(seeds[:, :], final[:, j, CH - 1:N:CH], up[:, :], ALU.mult).then_inc(s_car, 1)
                    dve.wait_ge(s_car, 3 * n + 1)
                    dve.tensor_tensor_scan(csum[:, :], ones[:, :], seeds[:, :], 0.0, ALU.mult, ALU.add).then_inc(s_car, 1)
                    dve.wait_ge(s_car, 3 * n + 2)
                    dve.tensor_tensor(carry[:, 1:], csum[:, :NCH - 1], down[:, 1:], ALU.mult).then_inc(s_car, 1)
                    dve.wait_ge(s_car, 3 * n + 3)
                    dve.tensor_tensor(vb[:, :].rearrange("p (c t) -> p c t", t=CH),
                                      fade[:, :].rearrange("p (c t) -> p c t", t=CH),
                                      carry[:, :].rearrange("p (c t) -> p c t", t=1).to_broadcast([P, NCH, CH]),
                                      ALU.mult).then_inc(s_fin, 1)
                    dve.wait_ge(s_fin, 2 * n + 1)
                    dve.tensor_tensor(final[:, j, :], final[:, j, :], vb[:, :], ALU.add).then_inc(s_fin, 1)
                    dve.wait_ge(s_fin, 2 * n + 2)
                for m in range(KD):
                    dve.wait_ge(s_sig, KD * b + m + 1)
                    dve.wait_ge(s_pm, KD * b + m + 1)
                    dve.tensor_tensor(gate[:, m, :], banks[m][:, :], gate[:, m, :], ALU.mult).then_inc(s_gm, 1)
                for i in range(SUB):
                    dve.wait_ge(s_po, SUB * b + i + 1)
                    bank = banks[i // 2][:, (i % 2) * HALF:(i % 2 + 1) * HALF]
                    dve.tensor_tensor(x[:, i, :], x[:, i, :], bank, ALU.add).then_inc(s_res, 1)
                dve.wait_ge(s_res, SUB * (b + 1))

        @block.tensor
        def _(pe):
            halves = [slice(0, HALF), slice(HALF, N)]

            def project(bank, group, j, done):
                for hs in halves:
                    for k in range(KD):
                        mm = pe.matmul(bank[:, hs], w_in[:, k, group * D + j * P:group * D + (j + 1) * P],
                                       xc[:, k, hs], start=(k == 0), stop=(k == KD - 1))
                mm.then_inc(done, 1)

            pe.wait_ge(s_tab, 16 * 8)
            pe.wait_ge(s_w, 32)
            pe.wait_ge(s_mix, KD)
            with pe.Fori(0, BATCH) as b:
                pe.wait_ge(s_res, SUB * b)
                pe.wait_ge(s_yn, SUB * (b + 1))
                for k in range(KD):
                    for i in range(SUB):
                        mm = pe.transpose(banks[k][:, i * P:(i + 1) * P], y[:, i, k * P:(k + 1) * P], ident[:, :])
                    mm.then_inc(s_tr, 1)
                pe.wait_ge(s_xc, KD * (b + 1))
                for j in range(KD):
                    n = b * KD + j
                    pe.wait_ge(s_arg, n)
                    project(ps_dt, 0, j, s_pdt)
                    pe.wait_ge(s_v, n)
                    project(ps_v, 1, j, s_pv)
                    pe.wait_ge(s_gate, n)
                    project(ps_g, 2, j, s_pg)
                    pe.wait_ge(s_v, n + 1)
                    pe.wait_ge(s_vb, 2 * n)
                    for hs in halves:
                        mm = pe.matmul(ps_p[:, hs], rot[:, :], v[:, hs], start=True, stop=True)
                    mm.then_inc(s_pp, 1)
                pe.wait_ge(s_gate, KD * (b + 1))
                pe.wait_ge(s_fin, 2 * KD * (b + 1))
                for m in range(KD):
                    for hs in halves:
                        for k in range(KD):
                            mm = pe.matmul(banks[m][:, hs], mix[:, k, m * P:(m + 1) * P], final[:, k, hs],
                                           start=(k == 0), stop=(k == KD - 1))
                    mm.then_inc(s_pm, 1)
                pe.wait_ge(s_gm, KD * (b + 1))
                for i in range(SUB):
                    bank = banks[i // 2][:, (i % 2) * HALF:(i % 2 + 1) * HALF]
                    for k in range(KD):
                        mm = pe.matmul(bank, gate[:, k, i * P:(i + 1) * P], w_out[:, k, :],
                                       start=(k == 0), stop=(k == KD - 1))
                    mm.then_inc(s_po, 1)


def feed_forward(nc, psum, name, consts, x_in, x_out, w_gate, w_up, w_down):
    ROWS, D = x_in.shape
    HID = w_gate.shape[1]
    KD = D // P
    TT = 512
    SUB = TT // P
    TILES = ROWS // TT
    R = 4
    BLK = HID // (P * R)
    HALVES = 2
    HB = BLK // HALVES
    STEPS = HALVES * TILES
    W = P * R
    with ExitStack() as ctx:
        def sb(n, shape, dt=F32):
            return ctx.enter_context(nc.sbuf_tensor(f"{name}_{n}", shape, dt))

        sem = ctx.enter_context(cleared_semaphores(nc, name))

        part = nc.dram_tensor(f"{name}_part", (ROWS, D), F32, kind="Internal").ap()
        ident = sb("ident", [P, P])
        mhalf = sb("mhalf", [P, SUB])
        stage = sb("stage", [P, 2, KD * W])
        w_hi = sb("w_hi", [P, HB, 3, KD * W], F32R)
        w_lo = sb("w_lo", [P, HB, 3, KD * W], F32R)
        x_tok = sb("x_tok", [P, SUB, D])
        x_res = sb("x_res", [P, SUB, D])
        xn = sb("xn", [P, SUB, D])
        x_hi = sb("x_hi", [P, KD, TT], F32R)
        x_lo = sb("x_lo", [P, KD, TT], F32R)
        stats = sb("stats", [P, SUB, 6])
        mean2, mean, gap, gap2, var, var_eps = (
            sb(n, [P, SUB]) for n in ("mean2", "mean", "gap", "gap2", "var", "var_eps"))
        rstd = sb("rstd", [P, SUB])
        silu = sb("silu", [P, 2, TT])
        h = sb("h", [P, R, TT])
        mag = sb("mag", [P, R, TT])
        wins = sb("wins", [P, 6, TT], BF16)
        score = sb("score", [P, R, TT], BF16)
        k_hi = sb("k_hi", [P, R, TT], F32R)
        k_lo = sb("k_lo", [P, R, TT], F32R)
        gate_ps, up_ps, *out_ps = (t[:, :].rearrange("p (r t) -> p r t", t=TT) for t in psum)

        s_const = sem("s_const")
        s_piece = [sem(f"s_piece{i}") for i in range(2)]
        s_hi = sem("s_hi")
        s_lo = sem("s_lo")
        s_x = sem("s_x")
        s_res = sem("s_res")
        s_var = sem("s_var")
        s_half = sem("s_half")
        s_rstd = sem("s_rstd")
        s_ln = sem("s_ln")
        s_xn = sem("s_xn")
        s_tr = sem("s_tr")
        s_xhi = sem("s_xhi")
        s_xlo = sem("s_xlo")
        s_gate = sem("s_gate")
        s_up = sem("s_up")
        s_silu = sem("s_silu")
        s_h = sem("s_h")
        s_mag = sem("s_mag")
        s_cmp = sem("s_cmp")
        s_kept = sem("s_kept")
        s_khi = sem("s_khi")
        s_klo = sem("s_klo")
        s_down = sem("s_down")
        s_sum = sem("s_sum")
        s_store = sem("s_store")
        CMP = 9

        GATE, UP, DOWN = range(3)
        pieces = [(0, GATE), (0, UP), (0, DOWN), (1, GATE), (1, UP), (1, DOWN),
                  (2, GATE), (2, UP), (3, GATE), (3, UP), (2, DOWN), (3, DOWN)]
        LAST = (TILES - 1) * HB

        def loaded(block, kind):
            return pieces.index((block, kind)) + 1

        def piece(q):
            j, kind = pieces[q]
            raw, hi, lo = stage[:, q % 2, :], w_hi[:, j % HB, kind, :], w_lo[:, j % HB, kind, :]
            if kind == DOWN:
                return raw, hi, lo
            return (raw.rearrange("p (k g r) -> p k r g", g=P, r=R),
                    *(part_.rearrange("p (k r g) -> p k r g", g=P, r=R) for part_ in (hi, lo)))

        block = ctx.enter_context(nc.Block())

        @block.sync
        def _(sp):
            def load_piece(q):
                j, kind = pieces[q]
                if q >= 2:
                    sp.wait_ge(s_hi, q - 1)
                    sp.wait_ge(s_lo, q - 1)
                if kind == DOWN:
                    src = w_down.rearrange("(b g r) n -> b g (r n)", g=P, r=R)[j]
                    dst = stage[:, q % 2, :]
                else:
                    src = (w_gate, w_up)[kind].rearrange("(k p) n -> p k n", p=P)[:, :, j * W:(j + 1) * W]
                    dst = stage[:, q % 2, :].rearrange("p (k n) -> p k n", n=W)
                sp.dma_start(dst, src).then_inc(s_piece[q % 2], 16)

            def load_next(t):
                sp.wait_ge(s_xn, SUB * (t + 1))
                sp.dma_start(x_tok[:, :, :], tiles(x_in)[(t + 1) % TILES]).then_inc(s_x, 16)

            def load_sum(t):
                sp.dma_start(x_res[:, :, :], tiles(x_in if t < TILES else part)[t % TILES]).then_inc(s_res, 16)

            def store_sum(t):
                sp.wait_ge(s_sum, SUB * (t + 1))
                sp.dma_start(tiles(part if t < TILES else x_out)[t % TILES], x_res[:, :, :]).then_inc(s_store, 16)
                sp.wait_ge(s_store, 16 * (t + 1))

            def tiles(ap):
                return ap.rearrange("(t s p) d -> t p s d", p=P, s=SUB)

            sp.dma_start(ident[:, :], consts["ident"]).then_inc(s_const, 16)
            sp.dma_start(x_tok[:, :, :], tiles(x_in)[0]).then_inc(s_x, 16)
            for q in range(3):
                load_piece(q)
            load_next(0)
            for q in range(3, 6):
                load_piece(q)
            for t in range(STEPS):
                if 0 < t < STEPS - 1:
                    load_next(t)
                if t > 0:
                    store_sum(t - 1)
                load_sum(t)
                if t == TILES - 1:
                    for q in range(6, 12):
                        load_piece(q)
            store_sum(STEPS - 1)

        @block.gpsimd
        def _(pool):
            pool.memset(mhalf[:, :], -0.5).then_inc(s_half, 1)
            pool.wait_ge(s_half, 1)

            def rstd_of(t):
                pool.wait_ge(s_var, t + 1)
                pool.tensor_tensor(rstd[:, :], var[:, :], mhalf[:, :], ALU.pow).then_inc(s_rstd, 1)

            def low_part(q):
                raw, hi, lo = piece(q)
                pool.wait_ge(s_hi, q + 1)
                pool.tensor_tensor(lo, raw, hi, ALU.subtract).then_inc(s_lo, 1)

            rstd_of(0)
            for q in range(6):
                low_part(q)
            with pool.Fori(1, TILES + 1) as t:
                rstd_of(t)
            for q in range(6, 11):
                low_part(q)
            rstd_of(TILES + 1)
            low_part(11)
            with pool.Fori(TILES + 2, STEPS) as t:
                rstd_of(t)

        @block.scalar
        def _(act):
            def high_part(q):
                raw, hi, _ = piece(q)
                act.wait_ge(s_piece[q % 2], 16 * (q // 2 + 1))
                if q >= 6:
                    used, kind = LAST + pieces[q][0] % HB + 1, pieces[q][1]
                    act.wait_ge((s_gate, s_up, s_down)[kind], used if kind == DOWN else R * used)
                act.copy(hi, raw).then_inc(s_hi, 1)

            def to_xT(t):
                for k in range(KD):
                    act.wait_ge(s_tr, KD * t + k + 1)
                    bank = (gate_ps if k < 2 else up_ps)[:, k % 2, :]
                    act.copy(x_hi[:, k, :], bank).then_inc(s_xhi, 1)

            def magnitude(s, r):
                act.wait_ge(s_h, R * s + r + 1)
                if r == 0:
                    act.wait_ge(s_cmp, CMP * s)
                act.activation(mag[:, r, :], h[:, r, :], ACT.Abs).then_inc(s_mag, 1)

            def split_kept(s):
                for r in range(R):
                    act.wait_ge(s_kept, R * s + r + 1)
                    if r == 0:
                        act.wait_ge(s_down, s)
                    act.copy(k_hi[:, r, :], h[:, r, :]).then_inc(s_khi, 1)

            def tile(t, more, between={}):
                for b in range(HB):
                    s = t * HB + b
                    for r in range(R):
                        n = R * s + r
                        act.wait_ge(s_gate, n + 1)
                        if r >= 2:
                            act.wait_ge(s_h, n - 1)
                        act.activation(silu[:, r % 2, :], gate_ps[:, r % 2, :], ACT.Silu).then_inc(s_silu, 1)
                        if r >= 1:
                            magnitude(s, r - 1)
                        for q in between.get((b, r), ()):
                            high_part(q)
                    magnitude(s, R - 1)
                    if b == HB - 1 and more:
                        to_xT(t + 1)
                    split_kept(s)
                for q in between.get("end", ()):
                    high_part(q)

            high_part(0)
            high_part(1)
            to_xT(0)
            high_part(2)
            tile(0, True, {(0, 0): (3,), (0, 1): (4,), (0, 2): (5,)})
            with act.Fori(1, TILES - 1) as t:
                tile(t, True)
            tile(TILES - 1, True, {(1, 2): (6,), (1, 3): (7,), "end": (8, 9)})
            tile(TILES, True, {(0, 0): (10,), (1, 1): (11,)})
            with act.Fori(TILES + 1, STEPS - 1) as t:
                tile(t, True)
            tile(STEPS - 1, False)

        @block.vector
        def _(dve):
            LN = SUB + 6

            def layer_norm(t):
                dve.wait_ge(s_x, 16 * (t + 1))
                for i in range(SUB):
                    dve.bn_stats(stats[:, i, :], x_tok[:, i, :]).then_inc(s_ln, 1)
                c = LN * t + SUB
                dve.wait_ge(s_ln, c)
                dve.tensor_tensor(mean2[:, :], stats[:, :, 1], stats[:, :, 4], ALU.add).then_inc(s_ln, 1)
                dve.tensor_tensor(gap[:, :], stats[:, :, 1], stats[:, :, 4], ALU.subtract).then_inc(s_ln, 1)
                dve.tensor_tensor(var[:, :], stats[:, :, 2], stats[:, :, 5], ALU.add).then_inc(s_ln, 1)
                dve.wait_ge(s_ln, c + 3)
                dve.tensor_scalar(mean[:, :], mean2[:, :], 0.5, None, ALU.mult).then_inc(s_ln, 1)
                dve.scalar_tensor_tensor(gap2[:, :], gap[:, :], 0.25, gap[:, :], ALU.mult, ALU.mult).then_inc(s_ln, 1)
                dve.tensor_scalar(var_eps[:, :], var[:, :], 1.0 / D, LN_EPS, ALU.mult, ALU.add).then_inc(s_ln, 1)
                dve.wait_ge(s_ln, c + 6)
                dve.tensor_tensor(var[:, :], var_eps[:, :], gap2[:, :], ALU.add).then_inc(s_var, 1)
                dve.wait_ge(s_rstd, t + 1)
                for i in range(SUB):
                    if i == 0:
                        dve.wait_ge(s_tr, KD * t)
                    dve.tensor_scalar(xn[:, i, :], x_tok[:, i, :], mean[:, i:i + 1], rstd[:, i:i + 1],
                                      ALU.subtract, ALU.mult).then_inc(s_xn, 1)

            def low_xT(t):
                for k in range(KD):
                    dve.wait_ge(s_xhi, KD * t + k + 1)
                    bank = (gate_ps if k < 2 else up_ps)[:, k % 2, :]
                    dve.tensor_tensor(x_lo[:, k, :], bank, x_hi[:, k, :], ALU.subtract).then_inc(s_xlo, 1)

            def prune(s, next_tile=None):
                c = CMP * s
                dve.wait_ge(s_klo, R * s)
                for r in range(R):
                    dve.wait_ge(s_silu, R * s + r + 1)
                    dve.wait_ge(s_up, R * s + r + 1)
                    dve.tensor_tensor(h[:, r, :], up_ps[:, r % 2, :], silu[:, r % 2, :], ALU.mult).then_inc(s_h, 1)
                dve.wait_ge(s_mag, R * (s + 1))
                dve.tensor_tensor(wins[:, 0:4:3, :], mag[:, 0:4:2, :], mag[:, 1:4:2, :], ALU.is_ge).then_inc(s_cmp, 1)
                dve.tensor_tensor(wins[:, 1:3, :], mag[:, 0:2, :], mag[:, 2:4, :], ALU.is_ge).then_inc(s_cmp, 1)
                dve.tensor_tensor(wins[:, 4, :], mag[:, 0, :], mag[:, 3, :], ALU.is_ge).then_inc(s_cmp, 1)
                dve.tensor_tensor(wins[:, 5, :], mag[:, 1, :], mag[:, 2, :], ALU.is_ge).then_inc(s_cmp, 1)
                if next_tile is not None:
                    low_xT(next_tile)
                dve.wait_ge(s_cmp, c + 2)
                dve.tensor_tensor(score[:, 0:4:3, :], wins[:, 0:4:3, :], wins[:, 1:3, :], ALU.add).then_inc(s_cmp, 1)
                dve.tensor_tensor(score[:, 1:3, :], wins[:, 2:4, :], wins[:, 0:2, :], ALU.subtract).then_inc(s_cmp, 1)
                dve.wait_ge(s_cmp, c + 6)
                dve.tensor_tensor(score[:, 0:4:3, :], score[:, 0:4:3, :],
                                  wins[:, 4:5, :].to_broadcast([P, 2, TT]), ALU.add).then_inc(s_cmp, 1)
                dve.tensor_tensor(score[:, 1, :], score[:, 1, :], wins[:, 5, :], ALU.add).then_inc(s_cmp, 1)
                dve.tensor_tensor(score[:, 2, :], score[:, 2, :], wins[:, 5, :], ALU.subtract).then_inc(s_cmp, 1)
                dve.wait_ge(s_cmp, c + CMP)
                for r, (least, op) in enumerate(((2.0, ALU.is_ge), (1.0, ALU.is_ge), (0.0, ALU.is_ge), (1.0, ALU.is_le))):
                    dve.scalar_tensor_tensor(h[:, r, :], score[:, r, :], least, h[:, r, :],
                                             op, ALU.mult).then_inc(s_kept, 1)
                for r in range(R):
                    dve.wait_ge(s_khi, R * s + r + 1)
                    dve.tensor_tensor(k_lo[:, r, :], h[:, r, :], k_hi[:, r, :], ALU.subtract).then_inc(s_klo, 1)

            def add_products(t):
                dve.wait_ge(s_res, 16 * (t + 1))
                dve.wait_ge(s_down, HB * (t + 1))
                for i in range(SUB):
                    dve.tensor_tensor(x_res[:, i, :], x_res[:, i, :], out_ps[i // 2][:, i % 2, :], ALU.add
                                      ).then_inc(s_sum, 1)

            def tile(t, first=False, more=True):
                for b in range(HB):
                    prune(t * HB + b, t + 1 if more and b == HB - 1 else None)
                    if b == 0 and not first:
                        add_products(t - 1)
                    if b == 0 and more:
                        layer_norm(t + 1)

            layer_norm(0)
            low_xT(0)
            tile(0, first=True)
            with dve.Fori(1, STEPS - 1) as t:
                tile(t)
            tile(STEPS - 1, more=False)
            add_products(STEPS - 1)

        @block.tensor
        def _(pe):
            def transposes(t):
                for i in range(SUB):
                    pe.wait_ge(s_xn, SUB * t + i + 1)
                for k in range(KD):
                    bank = (gate_ps if k < 2 else up_ps)[:, k % 2, :]
                    for i in range(SUB):
                        mm = pe.transpose(bank[:, i * P:(i + 1) * P], xn[:, i, k * P:(k + 1) * P], ident[:, :])
                    mm.then_inc(s_tr, 1)

            def up_product(bank, b, kind, r, t):
                for k in range(KD):
                    if t is not None:
                        pe.wait_ge(s_xlo, KD * t + k + 1)
                    cols = slice((k * R + r) * P, (k * R + r + 1) * P)
                    for i, (w, x) in enumerate(((w_hi, x_hi), (w_hi, x_lo), (w_lo, x_hi))):
                        mm = pe.matmul(bank, w[:, b, kind, cols], x[:, k, :],
                                       start=(k == 0 and i == 0), stop=(k == KD - 1 and i == 2))
                return mm

            def products_up(t, b, fresh):
                s = t * HB + b
                for r in range(R):
                    n = R * s + r
                    if b > 0 or r >= 2:
                        pe.wait_ge(s_silu, n - 1)
                    if r == 0 and fresh:
                        pe.wait_ge(s_lo, loaded(fresh[b], GATE))
                    up_product(gate_ps[:, r % 2, :], b, GATE, r, t if b == 0 and r == 0 else None).then_inc(s_gate, 1)
                    if b > 0 or r >= 2:
                        pe.wait_ge(s_h, n - 1)
                    if r == 0 and fresh:
                        pe.wait_ge(s_lo, loaded(fresh[b], UP))
                    up_product(up_ps[:, r % 2, :], b, UP, r, None).then_inc(s_up, 1)

            def products_down(t, b, weights, rows=range(SUB)):
                if 0 in rows:
                    pe.wait_ge(s_klo, R * (t * HB + b + 1))
                    if b == 0:
                        pe.wait_ge(s_sum, SUB * t)
                    pe.wait_ge(s_lo, weights)
                for i in rows:
                    toks = slice(i * P, (i + 1) * P)
                    for r in range(R):
                        for j, (k, w) in enumerate(((k_hi, w_hi), (k_hi, w_lo), (k_lo, w_hi))):
                            mm = pe.matmul(out_ps[i // 2][:, i % 2, :], k[:, r, toks],
                                           w[:, b, DOWN, r * D:(r + 1) * D], start=(b == 0 and r == 0 and j == 0),
                                           stop=(b == HB - 1 and r == R - 1 and j == 2))
                if SUB - 1 in rows:
                    mm.then_inc(s_down, 1)

            def tile(t, half, fresh=(), first=False, last=False):
                products_up(t, 0, fresh)
                if not first:
                    products_down(t - 1, HB - 1, loaded(HB - 1, DOWN) if half == 0 or fresh else len(pieces))
                for b in range(1, HB):
                    products_up(t, b, fresh)
                    weights = loaded(HB * half + b - 1, DOWN)
                    products_down(t, b - 1, weights, range(1))
                    if b == HB - 1 and not last:
                        pe.wait_ge(s_silu, R * HB * (t + 1))
                        pe.wait_ge(s_h, R * HB * (t + 1))
                        transposes(t + 1)
                    products_down(t, b - 1, weights, range(1, SUB))

            pe.wait_ge(s_const, 16)
            transposes(0)
            tile(0, 0, fresh=(0, 1), first=True)
            with pe.Fori(1, TILES) as t:
                tile(t, 0)
            tile(TILES, 1, fresh=(2, 3))
            with pe.Fori(TILES + 1, STEPS - 1) as t:
                tile(t, 1)
            tile(STEPS - 1, 1, last=True)
            products_down(STEPS - 1, HB - 1, len(pieces))


def delta_mixer(nc, psum, consts, x_in, x_out, w):
    ROWS, D = x_in.shape
    BATCH = 2
    KD = D // P
    SUBS = ROWS // P
    CHUNKS = SUBS // BATCH
    KH = 8
    VH = 16
    PAIRS = CHUNKS // 2
    U = 4
    TAPS = 4
    HALO = TAPS - 1
    QK = 6 * P
    LEVELS = (1, 2, 4, 8, 16, 32, 64)
    LV = len(LEVELS) - 1
    TN = 1 + 2 * LV
    GROUPS = 4
    GS = SUBS // GROUPS
    SCALE = float(P) ** -0.5
    G_MIN = -104.0
    with ExitStack() as ctx:
        def sb(n, shape, dt=F32):
            return ctx.enter_context(nc.sbuf_tensor(f"b_{n}", shape, dt))

        sem = ctx.enter_context(cleared_semaphores(nc, "b"))

        ident = sb("ident", [P, P])
        upto = sb("upto", [P, P])
        after = sb("after", [P, P])
        below = sb("below", [P, P])
        full = sb("full", [P, P])
        joins = sb("joins", [P, len(LEVELS), P])
        lower = sb("lower", [P, len(LEVELS)])
        mhalf = sb("mhalf", [P, U])
        rows = sb("rows", [P, 2, VH])
        norm_w = sb("norm_w", [P, 1])
        w_ba = sb("w_ba", [P, KD, 2 * VH])
        acc = sb("acc", [P, SUBS, D])
        xT = sb("xT", [P, KD, BATCH, CHUNKS * P])
        tab = sb("tab", [P, 5, BATCH, CHUNKS, VH])
        w_load = sb("w_load", [P, KD, QK])
        w_cur = sb("w_cur", [P, KD, QK])
        o_cur = sb("o_cur", [P, 2, D])
        taps_all = sb("taps_all", [P, KH, 4, TAPS])
        taps = sb("taps", [P, 4, TAPS])
        state = sb("state", [P, U, P])
        stats = sb("stats", [P, SUBS, 6])
        mean2, mean, gap, gap2, var, var_eps, rstd, mhalf16 = (
            sb(n, [P, SUBS]) for n in ("mean2", "mean", "gap", "gap2", "var", "var_eps", "rstd", "mhalf16"))
        raw = sb("raw", [P, 4, BATCH, HALO + P])
        bank = [t[:, lo:lo + U * P].rearrange("p (u t) -> p u t", t=P) for t in psum for lo in (0, U * P)]

        class Flight:
            def __init__(self, g):
                self.i = g
                self.wide, self.left, self.right = bank[2 + 3 * g:5 + 3 * g]

                def buf(n, shape=(P, U, P)):
                    return sb(f"{n}{g}", list(shape))

                self.x_cur = buf("x_cur", (P, KD, BATCH, P))
                self.conv, self.qkv = buf("conv", (P, 4, BATCH, P)), buf("qkv", (P, 4, BATCH, P))
                self.z_raw, self.z_act, self.sq = buf("z_raw"), buf("z_act"), buf("sq", (P, 2, BATCH, P))
                self.cur, self.g = buf("cur", (P, 5, U)), buf("g", (P, U))
                self.ss, self.rr, self.brk, self.cc, self.ngr, self.bng, self.rqs, self.ssq, self.ssq_eps, self.rn = (
                    buf(n, (P, U)) for n in ("ss", "rr", "brk", "cc", "ngr", "bng", "rqs", "ssq", "ssq_eps", "rn"))
                self.gU, self.em, self.em_s, self.em_i = buf("gU"), buf("em"), buf("em_s"), buf("em_i")
                self.k_tok, self.v_tok = buf("k_tok", (P, BATCH, P)), buf("v_tok")
                self.kb, self.kbT, self.At, self.Pt = (buf(n) for n in ("kb", "kbT", "At", "Pt"))
                self.Aj = buf("Aj", (P, 2, U, P))
                self.T, self.Tt = buf("T"), buf("Tt")
                self.X, self.qs = self.em, self.T
                self.rhs = buf("rhs")
                self.d, self.d_end, self.xf, self.xn, self.xnT = self.kb, self.kbT, self.rhs, self.em_s, self.em_i
                self.o = self.sq[:, :, :, :].rearrange("p a b t -> p (a b) t")
                self.s = {n: sem(f"{n}{g}") for n in (
                    "g", "cur", "silu", "zact", "sq", "ss", "sse", "rr", "scal", "gU", "dt", "em", "emm",
                    "ktok", "vtok", "ktoks", "vtoks", "kqs", "qss", "kb", "kbt", "kbT", "at", "atm", "joined", "T0",
                    "T", "Tps", "px", "X", "py", "rhs", "pd", "d", "pod", "dend", "ps", "o", "xf", "sqs",
                    "sse2", "rn", "xn", "txn", "xnT", "po", "acc")}

        flights = A, B = Flight(0), Flight(1)

        def flat(b):
            return b[:, :, :].rearrange("p u t -> p (u t)")

        HP = P // 2

        def half(t, level, second):
            return t[:, :, :].rearrange("p u (k s n) -> p (u k) s n", s=2, n=LEVELS[level])[:, :, second, :]

        def half_of(t, u, level, second):
            return t[:, u, :].rearrange("p (k s n) -> p k s n", s=2, n=LEVELS[level])[:, :, second, :]

        def packed(b, level, u=None):
            part = flat(b)[:, 0:U * HP] if u is None else flat(b)[:, u * HP:(u + 1) * HP]
            return part.rearrange("p (a n) -> p a n", n=LEVELS[level])

        y = w_cur[:, :, :].rearrange("p k n -> p (k n)")[:, 0:GS * D].rearrange("p (s d) -> p s d", d=D)
        sp_x, sp_abs, sp_e, sp_w, sp_l, sp_r = (
            f.qkv[:, i, :, :].rearrange("p b t -> p (b t)").rearrange("p (s v) -> p s v", v=VH)
            for f in flights for i in range(3))
        ba_feat = [f.Aj[:, i, :, :].rearrange("p u t -> p (u t)")[0:2 * VH, :] for f in flights for i in range(2)]
        ba = flat(bank[4]).rearrange("p (s n) -> p s n", n=2 * VH)

        s = {n: sem(n) for n in (
            "const", "set", "ln", "var", "rstd", "y", "trx", "xT", "bap", "bac", "ba", "soft", "sums", "tab", "chain", "gate", "dve_gate",
            "w", "ow", "wcp", "zero", "taps",
            "xcur", "pqk", "pv", "pz", "raw", "halo", "tap", "conv", "zraw", "S", "store")}
        s_x = [sem(f"x{g}") for g in range(GROUPS)]

        block = ctx.enter_context(nc.Block())

        @block.sync
        def _(sp):
            xr = x_in.rearrange("(s p) d -> p s d", p=P)
            for g in range(GROUPS):
                part = slice(g * GS, (g + 1) * GS)
                sp.dma_start(acc[:, part, :], xr[:, part, :]).then_inc(s_x[g], 16)
            for tile, src in ((ident, "ident"), (upto, "upto"), (after, "after"), (below, "below"),
                              (joins, "joins"), (lower, "lower"), (rows, "rows"), (norm_w, "norm_w"), (w_ba, "w_ba"),
                              (taps_all, "taps")):
                sp.dma_start(tile[:], w[src] if src in w else consts[src]).then_inc(s["const"], 16)
            for h in range(KH):
                if h > 0:
                    sp.wait_ge(s["wcp"], h)
                sp.dma_start(w_load[:, :, :], w["b_qkvz"].rearrange("(k p) n -> p k n", p=P)
                             [:, :, h * QK:(h + 1) * QK]).then_inc(s["w"], 16)
                if h > 0:
                    for f in flights:
                        sp.wait_ge(f.s["po"], 2 * h * PAIRS)
                sp.dma_start(o_cur[:, :, :], w["b_out"].rearrange("(h i p) n -> h p i n", p=P, i=2)[h]
                             ).then_inc(s["ow"], 16)
            outr = x_out.rearrange("(b c p) d -> b p c d", p=P, c=CHUNKS)
            for mm in range(PAIRS):
                for f in flights:
                    sp.wait_ge(f.s["acc"], 2 * ((KH - 1) * PAIRS + mm + 1))
                for b in range(BATCH):
                    sp.dma_start(outr[b][:, 2 * mm:2 * mm + 2, :],
                                 acc[:, b * CHUNKS + 2 * mm:b * CHUNKS + 2 * mm + 2, :]).then_inc(s["store"], 16)
            sp.wait_ge(s["store"], 16 * BATCH * PAIRS)

        @block.gpsimd
        def _(pool):
            pool.memset(mhalf[:, :], -0.5).then_inc(s["set"], 1)
            pool.memset(mhalf16[:, :], -0.5).then_inc(s["set"], 1)
            pool.memset(full[:, :], 1.0).then_inc(s["set"], 1)
            pool.wait_ge(s["const"], 16 * 10)
            pool.wait_ge(s["set"], 3)
            pool.wait_ge(s["var"], 1)
            pool.tensor_tensor(rstd[:, :], var[:, :], mhalf16[:, :], ALU.pow).then_inc(s["rstd"], 1)
            pool.wait_ge(s["xT"], GROUPS * KD)

            def chunk_of_x(f, c, before):
                pool.wait_ge(s["pz"], before)
                pool.sem_inc(s["gate"], 1)
                pool.tensor_copy(f.x_cur[:, :, :, :], xT[:, :, :, bass.ds(c * P, P)]).then_inc(s["xcur"], 1)

            def masked_decay(f, m, out, mask):
                pool.wait_ge(f.s["em"], m + 1)
                pool.wait_ge(f.s["txn"], m)
                pool.wait_ge(f.s["po"], 2 * m)
                pool.tensor_tensor(out[:, :, :], f.em[:, :, :],
                                   mask[:, :].rearrange("p (u t) -> p u t", u=1).to_broadcast([P, U, P]),
                                   ALU.mult).then_inc(f.s["emm"], 1)

            def rsqrt_of_keys(f, m):
                pool.wait_ge(f.s["sse"], m + 1)
                pool.wait_ge(f.s["xf"], U * m)
                pool.tensor_tensor(f.rr[:, :], f.ss[:, :], mhalf[:, :], ALU.pow).then_inc(f.s["rr"], 1)

            def join(f, m, i):
                if i == 1:
                    pool.wait_ge(f.s["atm"], 2 * m + 1)
                    pool.wait_ge(f.s["py"], LV * m)
                elif i == 2:
                    pool.wait_ge(f.s["T"], TN * m + 2)
                else:
                    pool.wait_ge(f.s["px"], LV * m + i - 2)
                pool.tensor_tensor(f.Aj[:, i % 2, :, :], f.At[:, :, :],
                                   joins[:, i:i + 1, :].to_broadcast([P, U, P]), ALU.mult).then_inc(f.s["joined"], 1)

            def rsqrt_of_output(f, m):
                pool.wait_ge(f.s["sse2"], m + 1)
                pool.tensor_tensor(f.rn[:, :], f.ssq_eps[:, :], mhalf[:, :], ALU.pow).then_inc(f.s["rn"], 1)

            def pair(h, mm, first=False, start=False, turn=False, last=False, own=False, ahead=True):
                m, c = h * PAIRS + mm, 2 * mm
                if start:
                    cleared_state(h)
                if own:
                    chunk_of_x(A, 0 if turn else c + 2, 2 * m + 1)
                masked_decay(A, m, A.em_s, below)
                rsqrt_of_keys(A, m)
                if not first:
                    rsqrt_of_output(B, m - 1)
                masked_decay(A, m, A.em_i, upto)
                join(A, m, 1)
                masked_decay(B, m, B.em_s, below)
                rsqrt_of_keys(B, m)
                masked_decay(B, m, B.em_i, upto)
                join(A, m, 2)
                join(B, m, 1)
                for i in range(3, len(LEVELS) + 1):
                    if i < len(LEVELS):
                        join(A, m, i)
                    join(B, m, i - 1)
                    if i == 4 and not last:
                        chunk_of_x(B, 1 if turn else c + 3, 2 * m + 2)
                if ahead:
                    chunk_of_x(A, 2 if turn else c + 4, 2 * m + 3)
                rsqrt_of_output(A, m)

            def cleared_state(h):
                pool.wait_ge(s["S"], U * h * CHUNKS)
                pool.sem_inc(s["gate"], 1)
                pool.memset(state[:, :, :], 0.0).then_inc(s["zero"], 1)

            pool.memset(state[:, :, :], 0.0).then_inc(s["zero"], 1)
            for f in flights:
                chunk_of_x(f, f.i, 0)
            pair(0, 0, first=True, own=True)
            with pool.Fori(0, KH - 1) as h:
                with pool.Fori(1, PAIRS - 2) as mm:
                    pair(h, mm)
                pair(h, PAIRS - 2, ahead=False)
                pair(h, PAIRS - 1, turn=True, own=True)
                pair(h + 1, 0, start=True)
            with pool.Fori(1, PAIRS - 2) as mm:
                pair(KH - 1, mm)
            pair(KH - 1, PAIRS - 2, ahead=False)
            pair(KH - 1, PAIRS - 1, last=True, ahead=False)
            rsqrt_of_output(B, KH * PAIRS - 1)

        @block.scalar
        def _(act):
            def head_weights(h):
                act.wait_ge(s["w"], 16 * (h + 1))
                act.wait_ge(s["pz"], h * CHUNKS)
                act.copy(w_cur[:, :, :], w_load[:, :, :]).then_inc(s["wcp"], 1)

            act.wait_ge(s["const"], 16 * 10)
            for g in range(GROUPS):
                for k in range(KD):
                    act.wait_ge(s["trx"], KD * g + k + 1)
                    b, t0 = divmod(g * GS * P, CHUNKS * P)
                    act.copy(xT[:, k, b, t0:t0 + GS * P], flat(bank[k])).then_inc(s["xT"], 1)
                act.wait_ge(s["bap"], g + 1)
                act.copy(ba_feat[g], flat(bank[4 + g])[0:2 * VH, :]).then_inc(s["bac"], 1)
            head_weights(0)
            act.wait_ge(s["ba"], 1)
            act.activation(tab[:, 1, :, :, :].rearrange("p b c v -> p (b c) v"), ba[:, :, 0:VH],
                           ACT.Sigmoid).then_inc(s["soft"], 1)
            act.activation(rows[:, 1, :], rows[:, 1, :], ACT.Exp).then_inc(s["soft"], 1)
            act.wait_ge(s["tab"], 1)
            act.activation(sp_e, sp_abs, ACT.Exp, scale=-1.0).then_inc(s["soft"], 1)
            act.wait_ge(s["tab"], 2)
            act.activation(sp_l, sp_w, ACT.Ln).then_inc(s["soft"], 1)
            act.wait_ge(s["sums"], 3)
            for i in range(3):
                act.activation(tab[:, 2 + i, :, :, :].rearrange("p b c v -> p (b c v)"),
                               flat(bank[5 + i])[:, 0:SUBS * VH], ACT.Exp).then_inc(s["soft"], 1)
            act.wait_ge(s["soft"], 7)

            def copy_qk_or_v(i, n):
                act.wait_ge(s[("pqk", "pv")[i]], n + 1)
                if i == 0:
                    act.wait_ge(s["halo"], n + 1)
                act.copy(raw[:, 2 * i:2 * i + 2, :, HALO:],
                         bank[i][:, :, :].rearrange("p (a b) t -> p a b t", b=BATCH)).then_inc(s["raw"], 1)

            def first_taps(f, m, n):
                act.wait_ge(s["raw"], 2 * (n + 1))
                act.wait_ge(f.s["silu"], m)
                for i in range(4):
                    act.activation(f.conv[:, i, :, :], raw[:, i, :, 0:P], ACT.Copy,
                                   scale=taps[:, i, 0:1]).then_inc(s["tap"], 1)

            def copy_z(f, m, n):
                act.wait_ge(s["pz"], n + 1)
                act.wait_ge(f.s["zact"], m)
                act.copy(f.z_raw[:, :, :], bank[0][:, :, :]).then_inc(s["zraw"], 1)

            def silus(f, m):
                q = 2 * m + f.i
                act.wait_ge(s["conv"], 12 * (q + 1))
                act.wait_ge(f.s["kqs"], m)
                act.activation(f.qkv[:, :, :, :], f.conv[:, :, :, :], ACT.Silu).then_inc(f.s["silu"], 1)
                act.wait_ge(s["zraw"], q + 1)
                act.wait_ge(f.s["xf"], U * m)
                act.activation(f.z_act[:, :, :], f.z_raw[:, :, :], ACT.Silu).then_inc(f.s["zact"], 1)

            def squares(f, m):
                act.wait_ge(f.s["silu"], m + 1)
                act.wait_ge(f.s["sqs"], 2 * m)
                act.activation(f.sq[:, :, :, :], f.qkv[:, 0:2, :, :], ACT.Square).then_inc(f.s["sq"], 1)

            def decay(f, m):
                act.wait_ge(f.s["dt"], m + 1)
                act.wait_ge(f.s["py"], LV * m)
                act.activation(f.em[:, :, :], f.wide[:, :, :], ACT.Exp).then_inc(f.s["em"], 1)

            def tokens(f, m):
                act.wait_ge(f.s["ktok"], m + 1)
                act.wait_ge(f.s["ps"], m)
                act.copy(f.k_tok[:, :, :], f.left[:, 0:2, :]).then_inc(f.s["ktoks"], 1)
                act.wait_ge(f.s["vtok"], m + 1)
                act.wait_ge(f.s["rhs"], U * m)
                act.copy(f.v_tok[:, :, :], f.right[:, :, :]).then_inc(f.s["vtoks"], 1)

            def scaled_keys(f, m):
                act.wait_ge(f.s["kbt"], m + 1)
                act.wait_ge(f.s["ps"], m)
                act.copy(f.kbT[:, :, :], f.wide[:, :, :]).then_inc(f.s["kbT"], 1)

            def first_blocks(f, m):
                act.wait_ge(f.s["Tps"], m + 1)
                act.wait_ge(f.s["o"], m)
                act.copy(f.T[:, :, :], f.right[:, :, :]).then_inc(f.s["T0"], 1)

            def level(f, m, i):
                act.wait_ge(f.s["px"], LV * m + i + 1)
                act.wait_ge(f.s["py"], LV * m + i)
                act.wait_ge(f.s["emm"], 2 * (m + 1))
                act.copy(half(f.X, i + 1, 0), packed(f.wide, i + 1)).then_inc(f.s["X"], 1)

            def from_state(f, m):
                act.wait_ge(f.s["kqs"], m + 1)
                for u in range(U):
                    act.activation(f.qs[:, u, :], f.right[:, u, :], ACT.Copy, scale=f.cur[:, 2, u:u + 1]
                                   ).then_inc(f.s["qss"], 1)

            def solved(f, m):
                act.wait_ge(f.s["pd"], m + 1)
                act.wait_ge(f.s["kbt"], m + 1)
                act.copy(f.d[:, :, :], f.wide[:, :, :]).then_inc(f.s["d"], 1)

            def output_T(f, m):
                act.wait_ge(f.s["txn"], m + 1)
                act.wait_ge(f.s["po"], 2 * m)
                act.activation(f.xnT[:, :, :], f.wide[:, :, :], ACT.Copy, scale=norm_w[:, 0:1]
                               ).then_inc(f.s["xnT"], 1)

            def project(f, m, n):
                copy_qk_or_v(0, n)
                copy_qk_or_v(1, n)
                first_taps(f, m, n)
                copy_z(f, m, n)

            def pair(h, mm, first=False, start=False, turn=False, last=False, own=False, ahead=True):
                m = h * PAIRS + mm
                silus(A, m)
                squares(A, m)
                decay(A, m)
                if turn:
                    head_weights(h + 1)
                tokens(A, m)
                scaled_keys(A, m)
                if not first:
                    output_T(B, m - 1)
                if not last:
                    copy_qk_or_v(0, 2 * m + 2)
                silus(B, m)
                squares(B, m)
                decay(B, m)
                tokens(B, m)
                first_blocks(A, m)
                if not last:
                    copy_qk_or_v(1, 2 * m + 2)
                scaled_keys(B, m)
                level(A, m, 0)
                if not last:
                    first_taps(A, m + 1, 2 * m + 2)
                first_blocks(B, m)
                if not last:
                    copy_z(A, m + 1, 2 * m + 2)
                for i in range(1, LV):
                    level(A, m, i)
                    level(B, m, i - 1)
                from_state(A, m)
                level(B, m, LV - 1)
                if not last:
                    copy_qk_or_v(0, 2 * m + 3)
                solved(A, m)
                from_state(B, m)
                solved(B, m)
                if not last:
                    copy_qk_or_v(1, 2 * m + 3)
                    copy_z(B, m + 1, 2 * m + 3)
                output_T(A, m)
                if not last:
                    first_taps(B, m + 1, 2 * m + 3)

            for f in flights:
                project(f, 0, f.i)
            pair(0, 0, first=True, own=True)
            with act.Fori(0, KH - 1) as h:
                with act.Fori(1, PAIRS - 2) as mm:
                    pair(h, mm)
                pair(h, PAIRS - 2, ahead=False)
                pair(h, PAIRS - 1, turn=True, own=True)
                pair(h + 1, 0, start=True)
            with act.Fori(1, PAIRS - 2) as mm:
                pair(KH - 1, mm)
            pair(KH - 1, PAIRS - 2, ahead=False)
            pair(KH - 1, PAIRS - 1, last=True, ahead=False)
            output_T(B, KH * PAIRS - 1)

        @block.vector
        def _(dve):
            for g in range(GROUPS):
                dve.wait_ge(s_x[g], 16)
                for i in range(g * GS, (g + 1) * GS):
                    dve.bn_stats(stats[:, i, :], acc[:, i, :]).then_inc(s["ln"], 1)
            c = SUBS
            dve.wait_ge(s["ln"], c)
            dve.tensor_tensor(mean2[:, :], stats[:, :, 1], stats[:, :, 4], ALU.add).then_inc(s["ln"], 1)
            dve.tensor_tensor(gap[:, :], stats[:, :, 1], stats[:, :, 4], ALU.subtract).then_inc(s["ln"], 1)
            dve.tensor_tensor(var[:, :], stats[:, :, 2], stats[:, :, 5], ALU.add).then_inc(s["ln"], 1)
            dve.wait_ge(s["ln"], c + 3)
            dve.tensor_scalar(mean[:, :], mean2[:, :], 0.5, None, ALU.mult).then_inc(s["ln"], 1)
            dve.scalar_tensor_tensor(gap2[:, :], gap[:, :], 0.25, gap[:, :], ALU.mult, ALU.mult).then_inc(s["ln"], 1)
            dve.tensor_scalar(var_eps[:, :], var[:, :], 1.0 / D, LN_EPS, ALU.mult, ALU.add).then_inc(s["ln"], 1)
            dve.wait_ge(s["ln"], c + 6)
            dve.tensor_tensor(var[:, :], var_eps[:, :], gap2[:, :], ALU.add).then_inc(s["var"], 1)
            dve.wait_ge(s["rstd"], 1)
            for g in range(GROUPS):
                dve.wait_ge(s["trx"], KD * g)
                for i in range(GS):
                    n = g * GS + i
                    dve.tensor_scalar(y[:, i, :], acc[:, n, :], mean[:, n:n + 1], rstd[:, n:n + 1],
                                      ALU.subtract, ALU.mult).then_inc(s["y"], 1)
            dve.wait_ge(s["const"], 16 * 10)
            dve.wait_ge(s["ba"], 1)
            dve.wait_ge(s["soft"], 1)
            dt_bias = rows[:, 0:1, :].to_broadcast([P, SUBS, VH])
            step_no = [0]

            def chain(ins):
                step_no[0] += 1
                ins.then_inc(s["chain"], 1)
                dve.wait_ge(s["chain"], step_no[0])

            chain(dve.tensor_tensor(sp_x, ba[:, :, VH:2 * VH], dt_bias, ALU.add))
            chain(dve.tensor_scalar(sp_r, sp_x, -1.0, None, ALU.mult))
            dve.tensor_tensor(sp_abs, sp_x, sp_r, ALU.max).then_inc(s["tab"], 1)
            dve.wait_ge(s["soft"], 3)
            dve.tensor_scalar(sp_w, sp_e, 1.0, None, ALU.add).then_inc(s["tab"], 1)
            dve.wait_ge(s["tab"], 2)
            chain(dve.tensor_scalar(sp_r, sp_w, 1.0, None, ALU.subtract))
            chain(dve.tensor_scalar(sp_abs, sp_r, 0.0, None, ALU.is_equal))
            chain(dve.tensor_tensor(sp_r, sp_r, sp_abs, ALU.add))
            chain(dve.reciprocal(sp_r, sp_r))
            dve.wait_ge(s["soft"], 4)
            chain(dve.tensor_tensor(sp_l, sp_l, sp_abs, ALU.add))
            chain(dve.tensor_tensor(sp_l, sp_l, sp_e, ALU.mult))
            chain(dve.tensor_tensor(sp_l, sp_l, sp_r, ALU.mult))
            chain(dve.scalar_tensor_tensor(sp_l, sp_x, 0.0, sp_l, ALU.max, ALU.add))
            chain(dve.tensor_tensor(sp_l, sp_l, rows[:, 1:2, :].to_broadcast([P, SUBS, VH]), ALU.mult))
            dve.tensor_scalar(tab[:, 0, :, :, :].rearrange("p b c v -> p (b c) v"), sp_l,
                              -1.0, G_MIN, ALU.mult, ALU.max).then_inc(s["tab"], 1)
            dve.wait_ge(s["soft"], 7)
            dve.wait_ge(s["tab"], 3)

            def halo(n):
                dve.wait_ge(s["tap"], 4 * n)
                dve.wait_ge(s["conv"], 12 * n)
                dve.tensor_copy(raw[:, :, :, 0:HALO], raw[:, :, :, P:P + HALO]).then_inc(s["halo"], 1)

            def convolve(f, n, tap):
                for i in range(4):
                    if tap == 1:
                        dve.wait_ge(s["tap"], 4 * n + i + 1)
                    else:
                        dve.wait_ge(s["conv"], 12 * n + 4 * (tap - 2) + i + 1)
                    dve.scalar_tensor_tensor(f.conv[:, i, :, :], raw[:, i, :, tap:tap + P],
                                             taps[:, i, tap:tap + 1], f.conv[:, i, :, :],
                                             ALU.mult, ALU.add).then_inc(s["conv"], 1)

            def b4(ap):
                return ap.rearrange("p (b i) -> p b i", i=1).to_broadcast([P, BATCH, 2])

            def u4(ap):
                return ap.rearrange("p (b i) -> p b i", i=2)

            def log_decays(f, m, h, c):
                dve.wait_ge(f.s["dt"], m)
                dve.wait_ge(f.s["gU"], U * m)
                dve.sem_inc(s["dve_gate"], 1)
                dve.tensor_copy(f.g[:, :].rearrange("p (b i) -> p b i", i=2),
                                tab[:, 0, :, bass.ds(c + f.i, 1), bass.ds(2 * h, 2)].rearrange("p b c i -> p (b c) i")
                                ).then_inc(f.s["g"], 1)
                dve.wait_ge(f.s["g"], m + 1)
                for u in range(U):
                    dve.tensor_scalar(f.gU[:, u, :], upto[:, :], f.g[:, u:u + 1], None, ALU.mult
                                      ).then_inc(f.s["gU"], 1)

            def factors(f, m, h, c):
                dve.wait_ge(s["S"], U * 2 * m)
                dve.wait_ge(f.s["qss"], U * m)
                dve.sem_inc(s["dve_gate"], 1)
                dve.tensor_copy(f.cur[:, :, :].rearrange("p n (b i) -> p n b i", i=2),
                                tab[:, :, :, bass.ds(c + f.i, 1), bass.ds(2 * h, 2)]
                                .rearrange("p n b c i -> p n (b c) i")).then_inc(f.s["cur"], 1)
                dve.wait_ge(f.s["cur"], m + 1)

            def key_scales(f, m):
                dve.wait_ge(f.s["ss"], m + 1)
                dve.tensor_scalar(f.ss[:, :], f.wide[:, 0, 0:U], 1e-6, None, ALU.add).then_inc(f.s["sse"], 1)

            def scaled_keys(f, m):
                dve.wait_ge(f.s["rr"], m + 1)
                dve.wait_ge(f.s["rhs"], 2 * U * m)
                k0 = 5 * m
                dve.tensor_scalar(f.rqs[:, 0:2], f.rr[:, 0:2], SCALE, None, ALU.mult).then_inc(f.s["scal"], 1)
                dve.tensor_tensor(u4(f.brk[:, :]), u4(f.cur[:, 1, :]), b4(f.rr[:, 2:4]), ALU.mult
                                  ).then_inc(f.s["scal"], 1)
                dve.tensor_tensor(u4(f.ngr[:, :]), u4(f.cur[:, 2, :]), b4(f.rr[:, 2:4]), ALU.mult
                                  ).then_inc(f.s["scal"], 1)
                dve.wait_ge(f.s["scal"], k0 + 3)
                dve.tensor_tensor(u4(f.cc[:, :]), u4(f.brk[:, :]), b4(f.rr[:, 2:4]), ALU.mult).then_inc(f.s["scal"], 1)
                dve.scalar_tensor_tensor(f.bng[:, :], f.ngr[:, :], -1.0, f.brk[:, :], ALU.mult, ALU.mult
                                         ).then_inc(f.s["scal"], 1)
                dve.wait_ge(f.s["scal"], k0 + 5)
                dve.wait_ge(f.s["ktoks"], m + 1)
                dve.wait_ge(f.s["dend"], U * m)
                dve.wait_ge(f.s["pod"], m)
                for u in range(U):
                    dve.tensor_scalar(f.kb[:, u, :], f.k_tok[:, u // 2, :], f.cc[:, u:u + 1], None, ALU.mult
                                      ).then_inc(f.s["kb"], 1)

            def scaled_values(f, m):
                dve.wait_ge(f.s["scal"], 5 * m + 5)
                dve.wait_ge(f.s["vtoks"], m + 1)
                dve.wait_ge(f.s["xn"], U * m)
                for u in range(U):
                    dve.tensor_scalar(f.rhs[:, u, :], f.v_tok[:, u, :], f.brk[:, u:u + 1], None, ALU.mult
                                      ).then_inc(f.s["rhs"], 1)

            def matrices(f, m):
                dve.wait_ge(f.s["emm"], 2 * m + 1)
                dve.wait_ge(f.s["at"], 2 * m + 1)
                dve.wait_ge(f.s["joined"], LV * m)
                dve.tensor_tensor(f.At[:, :, :], f.wide[:, :, :], f.em_s[:, :, :], ALU.mult).then_inc(f.s["atm"], 1)
                dve.wait_ge(f.s["atm"], 2 * m + 1)
                dve.wait_ge(f.s["px"], LV * m)
                dve.wait_ge(f.s["pd"], m)
                dve.tensor_tensor(f.Aj[:, 0, :, :], f.At[:, :, :], joins[:, 0:1, :].to_broadcast([P, U, P]),
                                  ALU.mult).then_inc(f.s["T"], 1)
                dve.wait_ge(f.s["T"], TN * m + 1)
                dve.tensor_tensor(f.Tt[:, :, :], f.Aj[:, 0, :, :],
                                  ident[:, :].rearrange("p (u t) -> p u t", u=1).to_broadcast([P, U, P]),
                                  ALU.add).then_inc(f.s["T"], 1)

            def within_chunk(f, m):
                dve.wait_ge(f.s["emm"], 2 * m + 2)
                dve.wait_ge(f.s["at"], 2 * m + 2)
                dve.wait_ge(f.s["pod"], m)
                qk = f.left[:, 0:2, :].rearrange("p b (i t) -> p b i t", i=1).to_broadcast([P, BATCH, 2, P])
                dve.tensor_tensor(f.Pt[:, :, :].rearrange("p (b i) t -> p b i t", i=2), qk,
                                  f.em_i[:, :, :].rearrange("p (b i) t -> p b i t", i=2), ALU.mult
                                  ).then_inc(f.s["atm"], 1)

            def level(f, m, i):
                dve.wait_ge(f.s["py"], LV * m + i + 1)
                dve.wait_ge(f.s["T"], TN * m + 2 + 2 * i)
                if i == 0:
                    dve.wait_ge(f.s["T0"], m + 1)
                if i < LV - 1:
                    dst = half(f.T, i + 1, 0)
                    dve.tensor_tensor(dst, dst, packed(f.left, i + 1), ALU.add).then_inc(f.s["T"], 1)
                dst = half(f.Tt, i + 1, 1)
                dve.scalar_tensor_tensor(dst, packed(f.right, i + 1), lower[:, i + 1:i + 2], dst,
                                         ALU.mult, ALU.add).then_inc(f.s["T"], 1)

            def right_side(f, m):
                dve.wait_ge(f.s["kqs"], m + 1)
                dve.wait_ge(f.s["rhs"], 2 * U * m + U)
                for u in range(U):
                    dve.scalar_tensor_tensor(f.rhs[:, u, :], f.left[:, u, :], f.bng[:, u:u + 1], f.rhs[:, u, :],
                                             ALU.mult, ALU.add).then_inc(f.s["rhs"], 1)

            def to_the_end(f, m):
                dve.wait_ge(f.s["d"], m + 1)
                dve.wait_ge(f.s["at"], 2 * m + 2)
                for u in range(U):
                    dve.tensor_scalar(f.d_end[:, u, :], f.d[:, u, :], f.cur[:, 3, u:u + 1], None, ALU.mult
                                      ).then_inc(f.s["dend"], 1)

            def new_state(f, m, h):
                q = 2 * m + f.i
                dve.wait_ge(f.s["ps"], m + 1)
                dve.wait_ge(s["zero"], h + 1)
                dve.wait_ge(s["S"], U * q)
                for u in range(U):
                    dve.scalar_tensor_tensor(state[:, u, :], state[:, u, :], f.cur[:, 4, u:u + 1], f.left[:, u, :],
                                             ALU.mult, ALU.add).then_inc(s["S"], 1)

            def gated(f, m):
                dve.wait_ge(f.s["pod"], m + 1)
                dve.wait_ge(f.s["qss"], U * (m + 1))
                dve.wait_ge(f.s["ss"], m + 1)
                dve.tensor_tensor(f.o, f.right[:, :, :], f.qs[:, :, :], ALU.add).then_inc(f.s["o"], 1)
                dve.wait_ge(f.s["o"], m + 1)
                dve.wait_ge(f.s["zact"], m + 1)
                dve.wait_ge(f.s["pd"], m + 1)
                for u in range(U):
                    dve.scalar_tensor_tensor(f.xf[:, u, :], f.o[:, u, :], f.rqs[:, u // 2:u // 2 + 1],
                                             f.z_act[:, u, :], ALU.mult, ALU.mult).then_inc(f.s["xf"], 1)

            def mean_square(f, m):
                dve.wait_ge(f.s["xf"], U * (m + 1))
                dve.tensor_tensor(f.o, f.xf[:, :, :], f.xf[:, :, :], ALU.mult).then_inc(f.s["sqs"], 1)
                dve.wait_ge(f.s["sqs"], 2 * m + 1)
                dve.tensor_reduce(f.ssq[:, :], f.o, AX.X, ALU.add).then_inc(f.s["sqs"], 1)
                dve.wait_ge(f.s["sqs"], 2 * m + 2)
                dve.tensor_scalar(f.ssq_eps[:, :], f.ssq[:, :], 1.0 / P, 1e-6, ALU.mult, ALU.add
                                  ).then_inc(f.s["sse2"], 1)

            def normalised(f, m):
                dve.wait_ge(f.s["rn"], m + 1)
                dve.wait_ge(f.s["atm"], 2 * (m + 1))
                for u in range(U):
                    dve.tensor_scalar(f.xn[:, u, :], f.xf[:, u, :], f.rn[:, u:u + 1], None, ALU.mult
                                      ).then_inc(f.s["xn"], 1)

            def add_up(f, m, c):
                for b in range(BATCH):
                    dve.wait_ge(f.s["po"], 2 * m + b + 1)
                    dst = acc[:, bass.ds(c + b * CHUNKS, 1), :].rearrange("p c d -> p (c d)")
                    dve.tensor_tensor(dst, dst, flat(f.left if b == 0 else f.right), ALU.add
                                      ).then_inc(f.s["acc"], 1)

            def pair(h, mm, first=False, start=False, turn=False, last=False, own=False, ahead=True):
                m, c = h * PAIRS + mm, 2 * mm
                factors(A, m, h, c)
                key_scales(A, m)
                if not first:
                    mean_square(B, m - 1)
                scaled_keys(A, m)
                if not first:
                    normalised(B, m - 1)
                if turn:
                    head_taps(h + 1)
                elif not last:
                    halo(2 * m + 2)
                log_decays(B, m, h, c)
                factors(B, m, h, c)
                scaled_values(A, m)
                matrices(A, m)
                within_chunk(A, m)
                if not first:
                    add_up(B, m - 1, CHUNKS - 1 if start else c - 1)
                key_scales(B, m)
                scaled_keys(B, m)
                scaled_values(B, m)
                matrices(B, m)
                level(A, m, 0)
                within_chunk(B, m)
                for i in range(1, LV):
                    level(A, m, i)
                    level(B, m, i - 1)
                    if i < TAPS and not last:
                        convolve(A, 2 * m + 2, i)
                right_side(A, m)
                level(B, m, LV - 1)
                if not last:
                    halo(2 * m + 3)
                to_the_end(A, m)
                new_state(A, m, h)
                right_side(B, m)
                gated(A, m)
                mean_square(A, m)
                to_the_end(B, m)
                normalised(A, m)
                new_state(B, m, h)
                if not last:
                    convolve(B, 2 * m + 3, 1)
                    log_decays(A, m + 1, h + 1 if turn else h, 0 if turn else c + 2)
                    convolve(B, 2 * m + 3, 2)
                add_up(A, m, c)
                if not last:
                    convolve(B, 2 * m + 3, 3)
                gated(B, m)

            def head_taps(h):
                dve.wait_ge(s["conv"], 12 * h * CHUNKS)
                dve.wait_ge(s["tap"], 4 * h * CHUNKS)
                dve.sem_inc(s["dve_gate"], 1)
                dve.tensor_copy(taps[:, :, :], taps_all[:, bass.ds(h, 1), :, :].rearrange("p h a b -> p (h a) b")
                                ).then_inc(s["taps"], 1)
                dve.wait_ge(s["taps"], h + 1)
                dve.sem_inc(s["dve_gate"], 1)
                dve.memset(raw[:, :, :, 0:HALO], 0.0).then_inc(s["halo"], 1)

            head_taps(0)
            for f in flights:
                if f.i > 0:
                    halo(f.i)
                dve.wait_ge(s["halo"], f.i + 1)
                for tap in range(1, TAPS):
                    convolve(f, f.i, tap)
            log_decays(A, 0, 0, 0)
            pair(0, 0, first=True, own=True)
            with dve.Fori(0, KH - 1) as h:
                with dve.Fori(1, PAIRS - 2) as mm:
                    pair(h, mm)
                pair(h, PAIRS - 2, ahead=False)
                pair(h, PAIRS - 1, turn=True, own=True)
                pair(h + 1, 0, start=True)
            with dve.Fori(1, PAIRS - 2) as mm:
                pair(KH - 1, mm)
            pair(KH - 1, PAIRS - 2, ahead=False)
            pair(KH - 1, PAIRS - 1, last=True, ahead=False)
            end = KH * PAIRS - 1
            mean_square(B, end)
            normalised(B, end)
            add_up(B, end, CHUNKS - 1)

        @block.tensor
        def _(pe):
            pe.wait_ge(s["const"], 16 * 10)
            pe.wait_ge(s["set"], 3)
            for g in range(GROUPS):
                pe.wait_ge(s["y"], GS * (g + 1))
                pe.wait_ge(s["xT"], KD * g)
                for k in range(KD):
                    for i in range(GS):
                        mm = pe.transpose(bank[k][:, i, :], y[:, i, k * P:(k + 1) * P], ident[:, :])
                    mm.then_inc(s["trx"], 1)
                pe.wait_ge(s["xT"], KD * (g + 1))
                b, t0 = divmod(g * GS * P, CHUNKS * P)
                for k in range(KD):
                    mm = pe.matmul(flat(bank[4 + g])[0:2 * VH, :], w_ba[:, k, :], xT[:, k, b, t0:t0 + GS * P],
                                   start=(k == 0), stop=(k == KD - 1))
                mm.then_inc(s["bap"], 1)
            pe.wait_ge(s["bac"], GROUPS)
            for n in range(SUBS):
                g, i = divmod(n, GS)
                mm = pe.transpose(ba[:, n, :], ba_feat[g][:, i * P:(i + 1) * P], ident[0:2 * VH, 0:2 * VH])
            mm.then_inc(s["ba"], 1)

            def project_qk(f, n, parts=range(2)):
                pe.wait_ge(s["xcur"], n + 1)
                pe.wait_ge(s["zraw"], n)
                project_part(f, 0, s["pqk"], parts)

            def project_v(f, n, parts=range(2)):
                pe.wait_ge(s["raw"], 2 * n)
                project_part(f, 1, s["pv"], parts)

            def project_part(f, i, done, parts=range(2)):
                for a in parts:
                    col = (2 * i + a) * P
                    for k in range(KD):
                        mm = pe.matmul(bank[i][:, 2 * a:2 * a + 2, :], w_cur[:, k, col:col + P],
                                       f.x_cur[:, k, :, :], start=(k == 0), stop=(k == KD - 1))
                if 1 in parts:
                    mm.then_inc(done, 1)

            def project_z(f, n, parts=range(BATCH)):
                pe.wait_ge(s["raw"], 2 * n + 1)
                for b in parts:
                    for k in range(KD):
                        mm = pe.matmul(bank[0][:, 2 * b:2 * b + 2, :], f.x_cur[:, k, b, :], w_cur[:, k, 4 * P:6 * P],
                                       start=(k == 0), stop=(k == KD - 1))
                if BATCH - 1 in parts:
                    mm.then_inc(s["pz"], 1)

            def decays(f, m):
                pe.wait_ge(f.s["gU"], U * (m + 1))
                pe.wait_ge(f.s["xnT"], m)
                pe.matmul(f.wide[:, :, :], after[:, :], f.gU[:, :, :], start=True, stop=True).then_inc(f.s["dt"], 1)

            def tokens(f, m):
                pe.wait_ge(f.s["acc"], 2 * m)
                pe.wait_ge(f.s["silu"], m + 1)
                for b in range(BATCH):
                    mm = pe.transpose(f.left[:, b, :], f.qkv[:, 1, b, :], ident[:, :])
                mm.then_inc(f.s["ktok"], 1)
                for u in range(U):
                    mm = pe.transpose(f.right[:, u, :], f.qkv[:, 2 + u % 2, u // 2, :], ident[:, :])
                mm.then_inc(f.s["vtok"], 1)

            def lengths(f, m):
                pe.wait_ge(f.s["sq"], m + 1)
                pe.wait_ge(f.s["em"], m + 1)
                for a in range(2):
                    for b in range(BATCH):
                        mm = pe.matmul(f.wide[:, 0, 2 * a + b:2 * a + b + 1], f.sq[:, a, b, :], full[:, 0:1],
                                       start=True, stop=True)
                mm.then_inc(f.s["ss"], 1)

            def keys(f, m):
                pe.wait_ge(f.s["kb"], U * (m + 1))
                for u in range(U):
                    mm = pe.transpose(f.wide[:, u, :], f.kb[:, u, :], ident[:, :])
                mm.then_inc(f.s["kbt"], 1)

            def products(f, m):
                pe.wait_ge(f.s["ktoks"], m + 1)
                pe.wait_ge(f.s["kbT"], m + 1)
                for b in range(BATCH):
                    mm = pe.matmul(f.wide[:, 2 * b:2 * b + 2, :], f.qkv[:, 1, b, :], f.kbT[:, 2 * b:2 * b + 2, :],
                                   start=True, stop=True)
                mm.then_inc(f.s["at"], 1)
                for b in range(BATCH):
                    mm = pe.matmul(f.left[:, b, :], f.qkv[:, 1, b, :], f.qkv[:, 0, b, :], start=True, stop=True)
                mm.then_inc(f.s["at"], 1)

            def first_blocks(f, m):
                pe.wait_ge(f.s["T"], TN * m + 2)
                pe.wait_ge(f.s["vtoks"], m + 1)
                for u in range(U):
                    mm = pe.transpose(f.right[:, u, :], f.Tt[:, u, :], ident[:, :])
                mm.then_inc(f.s["Tps"], 1)

            def level_x(f, m, i):
                if i == 0:
                    pe.wait_ge(f.s["T0"], m + 1)
                    pe.wait_ge(f.s["atm"], 2 * m + 2)
                pe.wait_ge(f.s["joined"], LV * m + i + 1)
                pe.wait_ge(f.s["T"], TN * m + (1 + 2 * i if i > 0 else 2))
                for u in range(U):
                    mm = pe.matmul(packed(f.wide, i + 1, u), f.Aj[:, (i + 1) % 2, u, :], half_of(f.T, u, i + 1, 0),
                                   start=True, stop=True)
                mm.then_inc(f.s["px"], 1)

            def level_y(f, m, i):
                pe.wait_ge(f.s["X"], LV * m + i + 1)
                pe.wait_ge(f.s["T"], TN * m + 2 + 2 * i)
                for u in range(U):
                    if i < LV - 1:
                        pe.matmul(packed(f.left, i + 1, u), f.Tt[:, u, :], half_of(f.X, u, i + 1, 0),
                                  start=True, stop=True)
                    mm = pe.matmul(packed(f.right, i + 1, u), f.X[:, u, :], half_of(f.Tt, u, i + 1, 1),
                                   start=True, stop=True)
                mm.then_inc(f.s["py"], 1)

            def from_state(f, m):
                pe.wait_ge(s["S"], U * (2 * m + f.i))
                pe.wait_ge(f.s["T"], TN * (m + 1))
                for a, bk in ((1, f.left), (0, f.right)):
                    for b in range(BATCH):
                        mm = pe.matmul(bk[:, 2 * b:2 * b + 2, :], f.qkv[:, a, b, :], state[:, 2 * b:2 * b + 2, :],
                                       start=True, stop=True)
                mm.then_inc(f.s["kqs"], 1)

            def solve(f, m):
                pe.wait_ge(f.s["rhs"], 2 * U * (m + 1))
                for u in range(U):
                    mm = pe.matmul(f.wide[:, u, :], f.Tt[:, u, :], f.rhs[:, u, :], start=True, stop=True)
                mm.then_inc(f.s["pd"], 1)

            def within_chunk(f, m):
                pe.wait_ge(f.s["qss"], U * (m + 1))
                pe.wait_ge(f.s["d"], m + 1)
                for u in range(U):
                    mm = pe.matmul(f.right[:, u, :], f.Pt[:, u, :], f.d[:, u, :], start=True, stop=True)
                mm.then_inc(f.s["pod"], 1)

            def to_state(f, m):
                pe.wait_ge(f.s["dend"], U * (m + 1))
                for b in range(BATCH):
                    mm = pe.matmul(f.left[:, 2 * b:2 * b + 2, :], f.k_tok[:, b, :], f.d_end[:, 2 * b:2 * b + 2, :],
                                   start=True, stop=True)
                mm.then_inc(f.s["ps"], 1)

            def output_T(f, m):
                pe.wait_ge(f.s["xn"], U * (m + 1))
                for u in range(U):
                    mm = pe.transpose(f.wide[:, u, :], f.xn[:, u, :], ident[:, :])
                mm.then_inc(f.s["txn"], 1)

            def project_out(f, m):
                pe.wait_ge(f.s["xnT"], m + 1)
                pe.wait_ge(s["S"], U * (2 * m + f.i + 1))
                for b in range(BATCH):
                    out = flat(f.left if b == 0 else f.right)
                    for i in range(2):
                        mm = pe.matmul(out, f.xnT[:, 2 * b + i, :], o_cur[:, i, :], start=(i == 0), stop=(i == 1))
                    mm.then_inc(f.s["po"], 1)

            def pair(h, mm, first=False, start=False, turn=False, last=False, own=False, ahead=True):
                m = h * PAIRS + mm
                decays(A, m)
                if turn:
                    pe.wait_ge(s["wcp"], h + 2)
                if start:
                    pe.wait_ge(s["zero"], h + 1)
                if own:
                    project_qk(A, 2 * m + 2)
                elif not last:
                    project_qk(A, 2 * m + 2, (1,))
                tokens(A, m)
                lengths(A, m)
                if not last:
                    project_v(A, 2 * m + 2)
                keys(A, m)
                if not first:
                    output_T(B, m - 1)
                products(A, m)
                if not first:
                    project_out(B, m - 1)
                decays(B, m)
                tokens(B, m)
                lengths(B, m)
                first_blocks(A, m)
                if not last:
                    project_z(A, 2 * m + 2, (0,))
                keys(B, m)
                level_x(A, m, 0)
                products(B, m)
                level_y(A, m, 0)
                if not last:
                    project_z(A, 2 * m + 2, (1,))
                first_blocks(B, m)
                for i in range(1, LV):
                    level_x(A, m, i)
                    level_x(B, m, i - 1)
                    level_y(A, m, i)
                    level_y(B, m, i - 1)
                from_state(A, m)
                level_x(B, m, LV - 1)
                if not last:
                    project_qk(B, 2 * m + 3)
                level_y(B, m, LV - 1)
                solve(A, m)
                if not last:
                    project_v(B, 2 * m + 3, (0,))
                to_state(A, m)
                within_chunk(A, m)
                from_state(B, m)
                if not last:
                    project_z(B, 2 * m + 3, (0,))
                solve(B, m)
                if not last:
                    project_v(B, 2 * m + 3, (1,))
                    project_z(B, 2 * m + 3, (1,))
                to_state(B, m)
                within_chunk(B, m)
                output_T(A, m)
                if ahead:
                    project_qk(A, 2 * m + 4, (0,))
                if first or start:
                    pe.wait_ge(s["ow"], 16 * (h + 1))
                project_out(A, m)

            pe.wait_ge(s["wcp"], 1)
            project_qk(A, 0)
            project_v(A, 0)
            pe.wait_ge(s["tab"], 3)
            for i, sums in enumerate((upto, after, full)):
                pe.matmul(flat(bank[5 + i])[:, 0:SUBS * VH], sums[:, :],
                          tab[:, 0, :, :, :].rearrange("p b c v -> p (b c v)"),
                          start=True, stop=True).then_inc(s["sums"], 1)
            pe.wait_ge(s["soft"], 7)
            pe.wait_ge(s["zero"], 1)
            project_z(A, 0)
            project_qk(B, 1)
            project_v(B, 1)
            project_z(B, 1)
            pair(0, 0, first=True, own=True)
            with pe.Fori(0, KH - 1) as h:
                with pe.Fori(1, PAIRS - 2) as mm:
                    pair(h, mm)
                pair(h, PAIRS - 2, ahead=False)
                pair(h, PAIRS - 1, turn=True, own=True)
                pair(h + 1, 0, start=True)
            with pe.Fori(1, PAIRS - 2) as mm:
                pair(KH - 1, mm)
            pair(KH - 1, PAIRS - 2, ahead=False)
            pair(KH - 1, PAIRS - 1, last=True, ahead=False)
            output_T(B, KH * PAIRS - 1)
            project_out(B, KH * PAIRS - 1)


def layer_stack(nc, ins, out):
    rows = out.shape[0] * out.shape[1]
    dim = out.shape[2]
    x1, x2, x3 = (nc.dram_tensor(f"rows_{i}", (rows, dim), F32, kind="Internal").ap() for i in (1, 2, 3))
    with ExitStack() as ctx:
        psum = [ctx.enter_context(nc.psum_tensor(f"banks_{i}", (P, 1024), F32)) for i in range(4)]
        decay_mixer(nc, psum, ins, ins["x"], x1, ins)
        ffn = (ins["ffn_gate"], ins["ffn_up"], ins["ffn_down"])
        feed_forward(nc, psum, "f1", ins, x1, x2, *ffn)
        delta_mixer(nc, psum, ins, x2, x3, ins)
        feed_forward(nc, psum, "f2", ins, x3, out.rearrange("b n d -> (b n) d"), *ffn)


def _laid_out(i):
    import numpy as np
    heads_a, key_heads = 16, 8
    width = i["L0_attn_a_in_proj_w"].shape[1]
    tiles = width // P
    column = lambda a: a.reshape(tiles, P, -1)
    cols = np.concatenate([column(i[f"L0_attn_a_{n}"]) for n in ("norm_scale", "conv_b", "dt_bias", "conv_w")], 2)
    ba = i["L0_attn_b_w_ba"].reshape(key_heads, 2, 2, width)
    taps = i["L0_attn_b_conv_w"]
    keys = key_heads * P
    per_head = [taps[:keys].reshape(key_heads, 1, P, -1), taps[keys:2 * keys].reshape(key_heads, 1, P, -1),
                taps[2 * keys:].reshape(key_heads, 2, P, -1)]
    rows = np.stack([i["L0_attn_b_dt_bias"], i["L0_attn_b_A_log"]])
    return {
        "x": i["L0_attn_a_x"],
        "cols": cols.transpose(1, 2, 0),
        "mix_rows": np.repeat(i["L0_attn_a_head_mix"], width // heads_a, axis=0).reshape(tiles, P, heads_a)
        .transpose(1, 0, 2),
        "a_in": i["L0_attn_a_in_proj_w"].T,
        "a_out": i["L0_attn_a_out_proj_w"].T,
        "ffn_gate": i["L0_ffn_w_gate"], "ffn_up": i["L0_ffn_w_up"], "ffn_down": i["L0_ffn_w_down"],
        "rows": np.broadcast_to(rows[None], (P, *rows.shape)),
        "norm_w": i["L0_attn_b_norm_weight"].reshape(P, 1),
        "w_ba": ba.transpose(1, 0, 2, 3).reshape(-1, width).T.reshape(tiles, P, -1).transpose(1, 0, 2),
        "b_qkvz": i["L0_attn_b_w_qkvz"].T,
        "b_out": i["L0_attn_b_w_out"].T,
        "taps": np.concatenate(per_head, 1).transpose(2, 0, 1, 3),
    }


def kernel(**inputs):
    import numpy as np
    import concourse.bacc as bacc
    from concourse.bass_utils import run_bass_kernel_spmd

    arrays = {**_laid_out({k: np.asarray(v) for k, v in inputs.items()}), **layer_a_tables(), **layer_b_tables()}
    arrays = {f"in_{k}": np.ascontiguousarray(v) for k, v in arrays.items()}
    nc = bacc.Bacc("TRN2", target_bir_lowering=False, num_devices=1)
    ins = {k[3:]: nc.dram_tensor(k, v.shape, mybir.dt.from_np(v.dtype), kind="ExternalInput").ap()
           for k, v in arrays.items()}
    shape = inputs["L0_attn_a_x"].shape
    out = nc.dram_tensor("out_rows", shape, F32, kind="ExternalOutput").ap()
    layer_stack(nc, ins, out)
    r = run_bass_kernel_spmd(nc, [arrays], core_ids=[0])
    return r.results[0]["out_rows"]
```
